# Optimizing a Trainium2 kernel written in Bass

```python
import numpy as np
import jax
import jax.numpy as jnp

def _softmax(x, axis=-1):
    return jax.nn.softmax(x, axis=axis)

def _gelu(x):
    return jax.nn.gelu(x, approximate=True)

def _silu(x):
    return jax.nn.silu(x)

def _sigmoid(x):
    return jax.nn.sigmoid(x)

def _layernorm(x, axis=-1, eps=1e-05):
    m = jnp.mean(x, axis=axis, keepdims=True)
    v = jnp.var(x, axis=axis, keepdims=True)
    return (x - m) / jnp.sqrt(v + eps)

def _scatter_add(tgt, idx, src, axis=0):
    return tgt.at[idx].add(src)

def _segment_sum(src, seg, n):
    return jax.ops.segment_sum(src, seg, n)
kernel_name = 'mk_decoder_preln_d2_seqx_r8_236253'

def setup_inputs(seed: int=0):
    np.random.seed(seed)
    _w = jnp.asarray

    def _rec_inputs():
        import jax
        import jax.numpy as jnp
        _rk = jax.random.key(seed)
        x = -0.000125 + 0.9999 * jax.random.normal(jax.random.fold_in(_rk, 1), (8, 256, 256), jnp.float32)
        _lenS = 256 - jax.random.randint(jax.random.fold_in(_rk, 7), (8,), 0, max(1, 256 // 4) + 1, jnp.int32)
        _lenS2 = 64 - jax.random.randint(jax.random.fold_in(_rk, 8), (8,), 0, max(1, 64 // 4) + 1, jnp.int32)
        _ctx_2048P = jax.random.normal(jax.random.fold_in(_rk, 11), (8, 16, 256), jnp.float32)
        _ctx_2048c = jax.random.dirichlet(jax.random.fold_in(_rk, 511), 0.3 * jnp.ones((16,), jnp.float32), (8, 64))
        _ctx_2048t = jnp.einsum('bsk,bkd->bsd', _ctx_2048c, _ctx_2048P)
        _ctx_2048t = _ctx_2048t * jax.lax.rsqrt(jnp.mean(jnp.square(_ctx_2048t)) + 1e-12) * 0.953939
        ctx_2048 = -0.000514642 + 1.00011 * (_ctx_2048t + 0.3 * jax.random.normal(jax.random.fold_in(_rk, 611), (8, 64, 256), jnp.float32))
        _validS = jnp.arange(256)[None, :] < _lenS[:, None]
        _validS2 = jnp.arange(64)[None, :] < _lenS2[:, None]
        _causal = jnp.tril(jnp.ones((256, 256), dtype=bool))
        mask_BxS2_bk0 = jnp.logical_not(jnp.broadcast_to(_validS2[:, :], (8, 64)))
        return (x, ctx_2048, mask_BxS2_bk0)
    x, ctx_2048, mask_BxS2_bk0 = _rec_inputs()

    def _L0_attn_setup():
        import jax, jax.numpy as jnp
        import numpy as np
        D_MODEL = 256
        N_STATE = 32
        RANK = 64
        LEVELS = int(np.log2(N_STATE))
        B, S = (4, 512)

        def _apply_butterfly(state, A_factors):
            b, s, n = state.shape
            x = state.reshape((b, s) + (2,) * LEVELS)
            for lvl in range(LEVELS):
                ax = 2 + lvl
                x = jnp.moveaxis(jnp.tensordot(x, A_factors[lvl], axes=[[ax], [0]]), -1, ax)
            return x.reshape(b, s, n)
        key = jax.random.key(seed)
        ks = jax.random.split(key, 7)
        u = jax.random.normal(ks[0], (B, S, D_MODEL), dtype=jnp.float32)
        A_factors = jax.random.normal(ks[1], (LEVELS, 2, 2), dtype=jnp.float32)
        A_factors = A_factors / jnp.linalg.norm(A_factors, axis=-1, keepdims=True)
        W_b_rank = jax.random.normal(ks[2], (D_MODEL, RANK), dtype=jnp.float32) * (1.0 / np.sqrt(D_MODEL))
        W_b_state = jax.random.normal(ks[3], (RANK, N_STATE), dtype=jnp.float32) * (1.0 / np.sqrt(RANK))
        W_c_rank = jax.random.normal(ks[4], (N_STATE, RANK), dtype=jnp.float32) * (1.0 / np.sqrt(N_STATE))
        W_c_model = jax.random.normal(ks[5], (RANK, D_MODEL), dtype=jnp.float32) * (1.0 / np.sqrt(RANK))
        D_vec = jax.random.normal(ks[6], (D_MODEL,), dtype=jnp.float32) * 0.02
        return {'u': u, 'A_factors': A_factors, 'W_b_rank': W_b_rank, 'W_b_state': W_b_state, 'W_c_rank': W_c_rank, 'W_c_model': W_c_model, 'D_vec': D_vec}
    _L0_attn_all = _L0_attn_setup()
    _L0_attn_in = {k: v for k, v in _L0_attn_all.items() if k in ('A_factors', 'W_b_rank', 'W_b_state', 'W_c_rank', 'W_c_model', 'D_vec')}
    del _L0_attn_all

    def _L0_xattn_setup():
        import jax, jax.numpy as jnp
        import numpy as np
        key = jax.random.key(seed)
        k1, k2, k3 = jax.random.split(key, 3)
        B, S, D, M = (8, 256, 256, 128)
        hidden_states = jax.random.normal(k1, (B, S, D), dtype=jnp.float32)
        memory_tokens = jax.random.normal(k2, (B, M, D), dtype=jnp.float32)
        memory_mask = jax.random.randint(k3, (B, M), 0, 2).astype(jnp.bool_)
        return {'hidden_states': hidden_states, 'memory_tokens': memory_tokens, 'memory_mask': memory_mask}
    _L0_xattn_all = _L0_xattn_setup()
    _L0_xattn_in = {k: v for k, v in _L0_xattn_all.items() if k in ()}
    del _L0_xattn_all

    def _L0_ffn_setup():
        import jax, jax.numpy as jnp
        import numpy as np
        D_MODEL = 256
        HIDDEN = 4 * D_MODEL
        B, S = (2, 512)

        def bit_linear(x, w, b):
            gamma_x = jnp.clip(jnp.max(jnp.abs(x), axis=-1, keepdims=True), 1e-05, None)
            scale_x = 127.0 / gamma_x
            x_dq = jnp.clip(jnp.round(x * scale_x), -128.0, 127.0) / scale_x
            x_ste = x + jax.lax.stop_gradient(x_dq - x)
            gamma_w = jnp.clip(jnp.mean(jnp.abs(w)), 1e-05, None)
            w_dq = jnp.clip(jnp.round(w / gamma_w), -1.0, 1.0) * gamma_w
            w_ste = w + jax.lax.stop_gradient(w_dq - w)
            return jnp.einsum('bsd,hd->bsh', x_ste, w_ste) + b
        key = jax.random.key(seed)
        ks = jax.random.split(key, 7)
        std = 0.02
        return {'x': jax.random.normal(ks[0], (B, S, D_MODEL), dtype=jnp.float32), 'gate_w': jax.random.normal(ks[1], (HIDDEN, D_MODEL), dtype=jnp.float32) * std, 'gate_b': jnp.zeros((HIDDEN,), dtype=jnp.float32), 'val_w': jax.random.normal(ks[2], (HIDDEN, D_MODEL), dtype=jnp.float32) * std, 'val_b': jnp.zeros((HIDDEN,), dtype=jnp.float32), 'out_w': jax.random.normal(ks[3], (D_MODEL, HIDDEN), dtype=jnp.float32) * std, 'out_b': jnp.zeros((D_MODEL,), dtype=jnp.float32)}
    _L0_ffn_all = _L0_ffn_setup()
    _L0_ffn_in = {k: v for k, v in _L0_ffn_all.items() if k in ('gate_w', 'gate_b', 'val_w', 'val_b', 'out_w', 'out_b')}
    del _L0_ffn_all

    def _L1_attn_setup():
        import jax, jax.numpy as jnp
        import numpy as np
        N_HEADS = 16
        CAUSAL = True
        key = jax.random.key(seed)
        ks = jax.random.split(key, 5)
        d = 256
        x = jax.random.normal(ks[0], (2, 256, d), dtype=jnp.float32)
        W_in = jax.random.normal(ks[1], (d, 3 * d), dtype=jnp.float32) * (1.0 / np.sqrt(d))
        b_in = jax.random.normal(ks[2], (3 * d,), dtype=jnp.float32) * 0.02
        W_out = jax.random.normal(ks[3], (d, d), dtype=jnp.float32) * (1.0 / np.sqrt(d))
        b_out = jax.random.normal(ks[4], (d,), dtype=jnp.float32) * 0.02
        return {'x': x, 'W_in': W_in, 'b_in': b_in, 'W_out': W_out, 'b_out': b_out}
    _L1_attn_all = _L1_attn_setup()
    _L1_attn_in = {k: v for k, v in _L1_attn_all.items() if k in ('W_in', 'b_in', 'W_out', 'b_out')}
    del _L1_attn_all

    def _L1_xattn_setup():
        import jax, jax.numpy as jnp
        import numpy as np
        HIDDEN = 256
        NUM_HEADS = 16
        NUM_KV_HEADS = 4
        HEAD_DIM = 128
        ROPE_THETA = 10000.0
        EPS = 1e-06

        def rms_norm(x, w, eps=EPS):
            var = jnp.mean(jnp.square(x), axis=-1, keepdims=True)
            return x * jax.lax.rsqrt(var + eps) * w

        def rope_cache(L, head_dim, theta, dtype):
            inv_freq = 1.0 / theta ** (jnp.arange(0, head_dim, 2, dtype=jnp.float32) / head_dim)
            t = jnp.arange(L, dtype=jnp.float32)
            freqs = jnp.outer(t, inv_freq)
            emb = jnp.concatenate([freqs, freqs], -1)
            cos = jnp.cos(emb).astype(dtype)[None, :, None, :]
            sin = jnp.sin(emb).astype(dtype)[None, :, None, :]
            return (cos, sin)

        def rotate_half(x):
            x1, x2 = jnp.split(x, 2, axis=-1)
            return jnp.concatenate([-x2, x1], axis=-1)
        key = jax.random.key(seed)
        ks = jax.random.split(key, 10)
        B, L, T = (2, 256, 64)
        q_out = NUM_HEADS * HEAD_DIM
        kv_out = NUM_KV_HEADS * HEAD_DIM
        s = lambda fan_in: 1.0 / np.sqrt(fan_in)
        return {'x': jax.random.normal(ks[0], (B, L, HIDDEN), jnp.float32), 'h_ctx_kv': jax.random.normal(ks[1], (B, T, HIDDEN), jnp.float32), 'wq': jax.random.normal(ks[2], (HIDDEN, q_out), jnp.float32) * s(HIDDEN), 'wk': jax.random.normal(ks[3], (HIDDEN, kv_out), jnp.float32) * s(HIDDEN), 'wv': jax.random.normal(ks[4], (HIDDEN, kv_out), jnp.float32) * s(HIDDEN), 'wo': jax.random.normal(ks[5], (q_out, HIDDEN), jnp.float32) * s(q_out), 'wk_ctx': jax.random.normal(ks[6], (HIDDEN, kv_out), jnp.float32) * s(HIDDEN), 'wv_ctx': jax.random.normal(ks[7], (HIDDEN, kv_out), jnp.float32) * s(HIDDEN), 'q_norm_w': jnp.ones((HEAD_DIM,), jnp.float32), 'k_norm_w': jnp.ones((HEAD_DIM,), jnp.float32)}
    _L1_xattn_all = _L1_xattn_setup()
    _L1_xattn_in = {k: v for k, v in _L1_xattn_all.items() if k in ('wq', 'wk', 'wv', 'wo', 'wk_ctx', 'wv_ctx', 'q_norm_w', 'k_norm_w')}
    del _L1_xattn_all

    def _L1_ffn_setup():
        import jax, jax.numpy as jnp
        import numpy as np
        B, S, D_IN, D_OUT, E = (4, 128, 256, 256, 32)
        MASK_DENSITY = 0.3
        THRESH = 0.5
        key = jax.random.key(seed)
        k_x, k_w, k_m, k_r = jax.random.split(key, 4)
        x = jax.random.normal(k_x, (B, S, D_IN), dtype=jnp.float32)
        bound = np.sqrt(1.0 / D_IN) * np.sqrt(3.0)
        weight = jax.random.uniform(k_w, (D_OUT, D_IN), minval=-bound, maxval=bound, dtype=jnp.float32)
        scale = jnp.ones((D_OUT,), dtype=jnp.float32)
        expert_masks = (jax.random.uniform(k_m, (E, D_OUT, D_IN)) < MASK_DENSITY).astype(jnp.float32)
        router_w = 0.01 * jax.random.normal(k_r, (E, D_IN), dtype=jnp.float32)
        return {'x': x, 'weight': weight, 'scale': scale, 'expert_masks': expert_masks, 'router_w': router_w}
    _L1_ffn_all = _L1_ffn_setup()
    _L1_ffn_in = {k: v for k, v in _L1_ffn_all.items() if k in ('weight', 'scale', 'expert_masks', 'router_w')}
    del _L1_ffn_all
    return {'x': x, 'ctx_2048': ctx_2048, 'mask_BxS2_bk0': mask_BxS2_bk0, 'L0_attn_A_factors': _L0_attn_in['A_factors'], 'L0_attn_W_b_rank': _L0_attn_in['W_b_rank'], 'L0_attn_W_b_state': _L0_attn_in['W_b_state'], 'L0_attn_W_c_rank': _L0_attn_in['W_c_rank'], 'L0_attn_W_c_model': _L0_attn_in['W_c_model'], 'L0_attn_D_vec': _L0_attn_in['D_vec'], 'L0_ffn_gate_w': _L0_ffn_in['gate_w'], 'L0_ffn_gate_b': _L0_ffn_in['gate_b'], 'L0_ffn_val_w': _L0_ffn_in['val_w'], 'L0_ffn_val_b': _L0_ffn_in['val_b'], 'L0_ffn_out_w': _L0_ffn_in['out_w'], 'L0_ffn_out_b': _L0_ffn_in['out_b'], 'L1_attn_W_in': _L1_attn_in['W_in'], 'L1_attn_b_in': _L1_attn_in['b_in'], 'L1_attn_W_out': _L1_attn_in['W_out'], 'L1_attn_b_out': _L1_attn_in['b_out'], 'L1_xattn_wq': _L1_xattn_in['wq'], 'L1_xattn_wk': _L1_xattn_in['wk'], 'L1_xattn_wv': _L1_xattn_in['wv'], 'L1_xattn_wo': _L1_xattn_in['wo'], 'L1_xattn_wk_ctx': _L1_xattn_in['wk_ctx'], 'L1_xattn_wv_ctx': _L1_xattn_in['wv_ctx'], 'L1_xattn_q_norm_w': _L1_xattn_in['q_norm_w'], 'L1_xattn_k_norm_w': _L1_xattn_in['k_norm_w'], 'L1_ffn_weight': _L1_ffn_in['weight'], 'L1_ffn_scale': _L1_ffn_in['scale'], 'L1_ffn_expert_masks': _L1_ffn_in['expert_masks'], 'L1_ffn_router_w': _L1_ffn_in['router_w']}

def reference(x, ctx_2048, mask_BxS2_bk0, L0_attn_A_factors, L0_attn_W_b_rank, L0_attn_W_b_state, L0_attn_W_c_rank, L0_attn_W_c_model, L0_attn_D_vec, L0_ffn_gate_w, L0_ffn_gate_b, L0_ffn_val_w, L0_ffn_val_b, L0_ffn_out_w, L0_ffn_out_b, L1_attn_W_in, L1_attn_b_in, L1_attn_W_out, L1_attn_b_out, L1_xattn_wq, L1_xattn_wk, L1_xattn_wv, L1_xattn_wo, L1_xattn_wk_ctx, L1_xattn_wv_ctx, L1_xattn_q_norm_w, L1_xattn_k_norm_w, L1_ffn_weight, L1_ffn_scale, L1_ffn_expert_masks, L1_ffn_router_w):
    import jax
    import jax.numpy as jnp

    def _L0_attn_ref(u, A_factors, W_b_rank, W_b_state, W_c_rank, W_c_model, D_vec):
        import jax, jax.numpy as jnp
        import numpy as np
        D_MODEL = 256
        N_STATE = 32
        RANK = 64
        LEVELS = int(np.log2(N_STATE))
        B, S = (4, 512)

        def _apply_butterfly(state, A_factors):
            b, s, n = state.shape
            x = state.reshape((b, s) + (2,) * LEVELS)
            for lvl in range(LEVELS):
                ax = 2 + lvl
                x = jnp.moveaxis(jnp.tensordot(x, A_factors[lvl], axes=[[ax], [0]]), -1, ax)
            return x.reshape(b, s, n)
        state = u @ W_b_rank @ W_b_state
        state = _apply_butterfly(state, A_factors)
        y = state @ W_c_rank @ W_c_model
        return y + D_vec * u

    def _L0_xattn_ref(hidden_states, memory_tokens, memory_mask):
        import jax, jax.numpy as jnp
        import numpy as np
        B, S, D = hidden_states.shape
        scale = 1.0 / jnp.sqrt(jnp.asarray(D, hidden_states.dtype))
        scores = jnp.einsum('bsd,bmd->bsm', hidden_states, memory_tokens) * scale
        neg_inf = jnp.asarray(-1e+30, scores.dtype)
        scores = jnp.where(memory_mask[:, None, :], scores, neg_inf)
        attn = jax.nn.softmax(scores, axis=-1)
        readout = jnp.einsum('bsm,bmd->bsd', attn, memory_tokens)
        valid_b = jnp.any(memory_mask, axis=-1)
        out = jnp.where(valid_b[:, None, None], readout, jnp.zeros_like(readout))
        return out

    def _L0_ffn_ref(x, gate_w, gate_b, val_w, val_b, out_w, out_b):
        import jax, jax.numpy as jnp
        import numpy as np
        D_MODEL = 256
        HIDDEN = 4 * D_MODEL
        B, S = (2, 512)

        def bit_linear(x, w, b):
            gamma_x = jnp.clip(jnp.max(jnp.abs(x), axis=-1, keepdims=True), 1e-05, None)
            scale_x = 127.0 / gamma_x
            x_dq = jnp.clip(jnp.round(x * scale_x), -128.0, 127.0) / scale_x
            x_ste = x + jax.lax.stop_gradient(x_dq - x)
            gamma_w = jnp.clip(jnp.mean(jnp.abs(w)), 1e-05, None)
            w_dq = jnp.clip(jnp.round(w / gamma_w), -1.0, 1.0) * gamma_w
            w_ste = w + jax.lax.stop_gradient(w_dq - w)
            return jnp.einsum('bsd,hd->bsh', x_ste, w_ste) + b
        gate = jax.nn.silu(bit_linear(x, gate_w, gate_b))
        val = bit_linear(x, val_w, val_b)
        return bit_linear(gate * val, out_w, out_b)

    def _L1_attn_ref(x, W_in, b_in, W_out, b_out):
        import jax, jax.numpy as jnp
        import numpy as np
        N_HEADS = 16
        CAUSAL = True
        B, S, D = x.shape
        H = N_HEADS
        Dh = D // H
        qkv = x @ W_in + b_in
        q, k, v = jnp.split(qkv, 3, axis=-1)

        def heads(t):
            return t.reshape(B, S, H, Dh).transpose(0, 2, 1, 3)
        q, k, v = (heads(q), heads(k), heads(v))
        scores = jnp.einsum('bhsd,bhtd->bhst', q, k)
        if CAUSAL:
            mask = jnp.triu(jnp.ones((S, S), dtype=bool), 1)
            scores = jnp.where(mask, -jnp.inf, scores)
        scores = scores / jnp.sqrt(jnp.asarray(Dh, dtype=scores.dtype))
        probs = jax.nn.softmax(scores, axis=-1)
        out = jnp.einsum('bhst,bhtd->bhsd', probs, v)
        out = out.transpose(0, 2, 1, 3).reshape(B, S, D)
        return out @ W_out + b_out

    def _L1_xattn_ref(x, h_ctx_kv, wq, wk, wv, wo, wk_ctx, wv_ctx, q_norm_w, k_norm_w):
        import jax, jax.numpy as jnp
        import numpy as np
        HIDDEN = 256
        NUM_HEADS = 16
        NUM_KV_HEADS = 4
        HEAD_DIM = 128
        ROPE_THETA = 10000.0
        EPS = 1e-06

        def rms_norm(x, w, eps=EPS):
            var = jnp.mean(jnp.square(x), axis=-1, keepdims=True)
            return x * jax.lax.rsqrt(var + eps) * w

        def rope_cache(L, head_dim, theta, dtype):
            inv_freq = 1.0 / theta ** (jnp.arange(0, head_dim, 2, dtype=jnp.float32) / head_dim)
            t = jnp.arange(L, dtype=jnp.float32)
            freqs = jnp.outer(t, inv_freq)
            emb = jnp.concatenate([freqs, freqs], -1)
            cos = jnp.cos(emb).astype(dtype)[None, :, None, :]
            sin = jnp.sin(emb).astype(dtype)[None, :, None, :]
            return (cos, sin)

        def rotate_half(x):
            x1, x2 = jnp.split(x, 2, axis=-1)
            return jnp.concatenate([-x2, x1], axis=-1)
        B, L, _ = x.shape
        T = h_ctx_kv.shape[1]
        rep = NUM_HEADS // NUM_KV_HEADS
        q = (x @ wq).reshape(B, L, NUM_HEADS, HEAD_DIM)
        k = (x @ wk).reshape(B, L, NUM_KV_HEADS, HEAD_DIM)
        v = (x @ wv).reshape(B, L, NUM_KV_HEADS, HEAD_DIM)
        q = rms_norm(q, q_norm_w)
        k = rms_norm(k, k_norm_w)
        k_ctx = (h_ctx_kv @ wk_ctx).reshape(B, T, NUM_KV_HEADS, HEAD_DIM)
        v_ctx = (h_ctx_kv @ wv_ctx).reshape(B, T, NUM_KV_HEADS, HEAD_DIM)
        k_ctx = rms_norm(k_ctx, k_norm_w)
        cos, sin = rope_cache(L, HEAD_DIM, ROPE_THETA, x.dtype)
        q = q * cos + rotate_half(q) * sin
        k = k * cos + rotate_half(k) * sin
        k_full = jnp.concatenate([k_ctx, k], axis=1)
        v_full = jnp.concatenate([v_ctx, v], axis=1)
        k_full = jnp.repeat(k_full, rep, axis=2)
        v_full = jnpp_repeat = jnp.repeat(v_full, rep, axis=2)
        i = jnp.arange(L)[:, None]
        j = jnp.arange(L)[None, :]
        causal = jnp.where(j > i, -jnp.inf, 0.0).astype(x.dtype)
        mask = jnp.concatenate([jnp.zeros((L, T), x.dtype), causal], axis=1)
        scale = 1.0 / np.sqrt(HEAD_DIM)
        scores = jnp.einsum('blhd,bmhd->bhlm', q, k_full) * scale + mask
        probs = jax.nn.softmax(scores, axis=-1)
        out = jnp.einsum('bhlm,bmhd->blhd', probs, v_full)
        out = out.reshape(B, L, NUM_HEADS * HEAD_DIM)
        return out @ wo

    def _L1_ffn_ref(x, weight, scale, expert_masks, router_w):
        import jax, jax.numpy as jnp
        import numpy as np
        B, S, D_IN, D_OUT, E = (4, 128, 256, 256, 32)
        MASK_DENSITY = 0.3
        THRESH = 0.5
        logits = jnp.einsum('bsd,ed->bse', x, router_w)
        probs = jax.nn.softmax(logits, axis=-1)
        top1_w = jnp.max(probs, axis=-1)
        top1_idx = jnp.argmax(probs, axis=-1)
        w_q = jnp.clip(jnp.round(weight / THRESH), -1.0, 1.0)
        w_scaled = w_q * scale[:, None]
        out0 = jnp.zeros((x.shape[0], x.shape[1], weight.shape[0]), dtype=x.dtype)

        def body(out, inputs):
            e_idx, mask_e = inputs
            y = jnp.einsum('bsi,oi->bso', x, w_scaled * mask_e)
            sel = (top1_idx == e_idx)[..., None]
            out = jnp.where(sel, y * top1_w[..., None], out)
            return (out, None)
        out, _ = jax.lax.scan(body, out0, (jnp.arange(E), expert_masks))
        return out
    x = x + _L0_attn_ref(_layernorm(x, axis=-1), L0_attn_A_factors, L0_attn_W_b_rank, L0_attn_W_b_state, L0_attn_W_c_rank, L0_attn_W_c_model, L0_attn_D_vec)
    x = x + _L0_xattn_ref(_layernorm(x, axis=-1), ctx_2048, mask_BxS2_bk0)
    x = x + _L0_ffn_ref(_layernorm(x, axis=-1), L0_ffn_gate_w, L0_ffn_gate_b, L0_ffn_val_w, L0_ffn_val_b, L0_ffn_out_w, L0_ffn_out_b)
    x = x + _L1_attn_ref(_layernorm(x, axis=-1), L1_attn_W_in, L1_attn_b_in, L1_attn_W_out, L1_attn_b_out)
    x = x + _L1_xattn_ref(_layernorm(x, axis=-1), ctx_2048, L1_xattn_wq, L1_xattn_wk, L1_xattn_wv, L1_xattn_wo, L1_xattn_wk_ctx, L1_xattn_wv_ctx, L1_xattn_q_norm_w, L1_xattn_k_norm_w)
    x = x + _L1_ffn_ref(_layernorm(x, axis=-1), L1_ffn_weight, L1_ffn_scale, L1_ffn_expert_masks, L1_ffn_router_w)
    return x

_drawn_inputs = setup_inputs


def setup_inputs(seed=0):
    import zlib

    import numpy as np

    out = dict(_drawn_inputs(seed))
    spreads = {'L0_ffn_gate_b': (0.0, 0.8),
     'L0_ffn_val_b': (0.0, 0.8),
     'L0_ffn_out_b': (0.0, 0.603),
     'L1_xattn_q_norm_w': (1.0, 0.6),
     'L1_xattn_k_norm_w': (1.0, 0.6),
     'L1_ffn_scale': (1.0, 0.2)}
    factors = {'L0_attn_D_vec': 4.153,
     'L0_ffn_gate_w': 7.96,
     'L0_ffn_val_w': 7.742,
     'L0_ffn_out_w': 7.029,
     'L1_attn_b_in': 17.046,
     'L1_attn_b_out': 20.764}
    for name, (base, spread) in spreads.items():
        noise = np.random.default_rng([zlib.crc32(name.encode()), seed]).standard_normal(out[name].shape)
        drawn = base * np.exp(spread * noise) if base else spread * noise
        out[name] = jnp.asarray(drawn.astype(out[name].dtype))
    for name, factor in factors.items():
        out[name] = (out[name] * factor).astype(out[name].dtype)
    return out
```

```python
import numpy as np
import concourse.bass as bass
from concourse import mybir
from contextlib import ExitStack

B, S, D = 8, 256, 256
P = 128
J, C = S // P, D // P
T = 64
R, NS = 64, 32
LV = 5
HID = 1024
HC = HID // P
NH, DH = 16, 16
XH, XG, XD = 16, 4, 128
GH = XH // XG
KEYS = P + T + P
NE = 32
LN_EPS, RMS_EPS = 1e-5, 1e-6
MAGIC = 12582912.0
NEG = -1e30
LOWEST = -3.0e38
MIX, CROSS, FFN, SELF, HYBRID, MOE = range(6)


def decoder_kernel(nc, I, out):
    F32, BF, U8, U32 = mybir.dt.float32, mybir.dt.bfloat16, mybir.dt.uint8, mybir.dt.uint32
    ALU, ACT, AX = mybir.AluOpType, mybir.ActivationFunctionType, mybir.AxisListType
    ds = bass.ds

    with ExitStack() as ctx:
        def sb(name, shape, dt=F32):
            return ctx.enter_context(nc.sbuf_tensor(name, shape, dt))

        def sem(name):
            return ctx.enter_context(nc.semaphore(name))

        X = sb("X", [P, B, J, D])
        ident = sb("ident", [P, P])
        identb = sb("identb", [P, P], BF)
        ones = sb("ones", [P, P])
        halves = sb("halves", [P, 16])
        wbrT = sb("wbrT", [R, D])
        wcrT = sb("wcrT", [R, NS])
        wcm = sb("wcm", [R, D])
        fly = sb("fly", [R, 2, NS])
        factors = sb("factors", [R, LV * 4])
        dvec = sb("dvec", [P, C])
        b_fold = sb("b_fold", [NS, D])
        c_fold = sb("c_fold", [NS, D])
        early2 = sb("early2", [P, 4096])
        ctxT = sb("ctxT", [P, C, B, T])
        masku = sb("masku", [P, B, T], U8)
        mask = sb("mask", [P, B, T])
        valid = sb("valid", [P, B])
        early = sb("early", [P, 4096])
        ffo_b = sb("ffo_b", [P, D])
        wsum = sb("wsum", [P, 3])
        gam = sb("gam", [P, 3])
        rgam = sb("rgam", [P, 3])
        gam127 = sb("gam127", [P, 3])
        w_in = sb("w_in", [P, C, 3 * D])
        w_out = sb("w_out", [P, C, D])
        bqk = sb("bqk", [P, 4])
        b_v = sb("b_v", [P, D])
        b_o = sb("b_o", [P, D])
        hmask = sb("hmask", [P, P // DH])
        causal = sb("causal", [P, J, S])
        wq = sb("wq", [P, C, XH * XD])
        wk = sb("wk", [P, C, XG * XD])
        wv = sb("wv", [P, C, XG * XD])
        wkc = sb("wkc", [P, C, XG * XD])
        wvc = sb("wvc", [P, C, XG * XD])
        wo = sb("wo", [P, XH, D])
        cosT = sb("cosT", [P, J, XD])
        sinT = sb("sinT", [P, J, XD])
        qw = sb("qw", [P, XD])
        qws = sb("qws", [P, XD])
        kw = sb("kw", [P, XD])
        kws = sb("kws", [P, XD])
        cosq = sb("cosq", [P, J, XD])
        sinq = sb("sinq", [P, J, XD])
        cosk = sb("cosk", [P, J, XD])
        sink = sb("sink", [P, J, XD])
        kmask = sb("kmask", [P, J, KEYS])
        ew = sb("ew", [P, C, D])
        rwT = sb("rwT", [P, C, NE])
        iota = sb("iota", [P, NE])
        esc = sb("esc", [P, D])
        EW = sb("EW", [P, NE, C * D], BF)
        st = sb("st", [P, J, 6])
        mv = sb("mv", [P, J, 2])
        ve = sb("ve", [P, J])
        rstd = sb("rstd", [P, J])
        XN = sb("XN", [P, J, D])
        XT = sb("XT", [P, C, S])
        magic = sb("magic", [P, 1])
        eCT = sb("eCT", [P, C, T])
        arena = sb("arena", [P, 8448])
        small = sb("small", [P, 512])

        def cut(at, shape, dt=F32, src=arena):
            n = 1
            for s in shape:
                n *= s
            words = n if dt == F32 else n // 2
            v = src[:, at:at + words]
            if dt != F32:
                v = v.bitcast(dt)
            if len(shape) > 1:
                names = "abcd"[:len(shape)]
                v = v.rearrange(f"p ({' '.join(names)}) -> p {' '.join(names)}",
                                **dict(zip(names[1:], shape[1:])))
            return v

        PS = ctx.enter_context(nc.psum_tensor("PS", [P, 8, 512], F32))

        def bank(n, k=1):
            return PS[:, n:n + k, :].rearrange("p b n -> p (b n)")

        pXT = bank(0)

        s_lx, s_lc, s_l0, s_l1, s_l2, s_l3, s_l4, s_l5 = (
            sem(n) for n in ("s_lx", "s_lc", "s_l0", "s_l1", "s_l2", "s_l3", "s_l4", "s_l5"))
        s_lg, s_lv, s_lo = sem("s_lg"), sem("s_lv"), sem("s_lo")
        s_mld = [sem(f"s_mld{i}") for i in range(4)]
        s_mfree = sem("s_mfree")
        s_ew = sem("s_ew")
        s_out = sem("s_out")
        s_held = sem("s_held")
        s_x = sem("s_x")
        s_bn, s_mv, s_ve, s_rs = sem("s_bn"), sem("s_mv"), sem("s_ve"), sem("s_rs")
        s_xn = sem("s_xn")
        s_xtp = sem("s_xtp")
        s_xt = sem("s_xt")
        s_c = sem("s_c")
        s_pc = sem("s_pc")
        s_pp = sem("s_pp")
        s_ps = sem("s_ps")

        a_mm, = (sem("a_mm"),)
        b_s, b_c, b_m, b_e, b_r, b_v2, b_p, b_t, b_tc, b_o2 = (
            sem(n) for n in ("b_s", "b_c", "b_m", "b_e", "b_r", "b_v2", "b_p", "b_t", "b_tc", "b_o2"))
        d_vv = sem("d_vv")
        c_xq = sem("c_xq")
        c_q = [sem(f"c_q{i}") for i in range(5)]
        c_g, c_v, c_gs, c_si, c_vs, c_h, c_a = (
            sem(n) for n in ("c_g", "c_v", "c_gs", "c_si", "c_vs", "c_h", "c_a"))
        c_s = [sem(f"c_s{i}") for i in range(4)]
        c_hr, c_hq, c_t, c_ht, c_o, c_y = (
            sem(n) for n in ("c_hr", "c_hq", "c_t", "c_ht", "c_o", "c_y"))
        d_pq, d_q, d_kv, d_s, d_mx, d_nm, d_e, d_t, d_pt, d_pv, d_r, d_o, d_ot, d_oc, d_y, d_yb = (
            sem(n) for n in ("d_pq", "d_q", "d_kv", "d_s", "d_mx", "d_nm", "d_e", "d_t", "d_pt",
                             "d_pv", "d_r", "d_o", "d_ot", "d_oc", "d_y", "d_yb"))
        e_ct, e_k, e_v, e_vr = (sem(n) for n in ("e_ct", "e_k", "e_v", "e_vr"))
        e_kv, e_kr, e_sq, e_ssq, e_ve, e_rk, e_kn, e_ka, e_kb, e_kf, e_kt, e_kc = (
            sem(n) for n in ("e_kv", "e_kr", "e_sq", "e_ssq", "e_ve", "e_rk", "e_kn", "e_ka",
                             "e_kb", "e_kf", "e_kt", "e_kc"))
        e_q, e_qr, e_qs, e_qb, e_qa, e_qq, e_qv, e_rq, e_qf, e_qt, e_qc, e_s, e_mx, e_nm, e_e, e_ri, \
            e_p, e_t, e_pta, e_ptd, e_pv, e_oc, e_y = (
                sem(n) for n in ("e_q", "e_qr", "e_qs", "e_qb", "e_qa", "e_qq", "e_qv", "e_rq",
                                 "e_qf", "e_qt", "e_qc", "e_s", "e_mx", "e_nm", "e_e", "e_ri", "e_p",
                                 "e_t", "e_pta", "e_ptd", "e_pv", "e_oc", "e_y"))
        f_xh, f_r1, f_xm, f_xl, f_l, f_lg, f_m, f_i, f_if, f_oh, f_nm, f_e, f_r, f_sel, f_z, f_y, f_acc, \
            f_s, f_w = (
                sem(n) for n in ("f_xh", "f_r1", "f_xm", "f_xl", "f_l", "f_lg", "f_m", "f_i", "f_if",
                                 "f_oh", "f_nm", "f_e", "f_r", "f_sel", "f_z", "f_y", "f_acc",
                                 "f_s", "f_w"))

        block = ctx.enter_context(nc.Block())

        def bc(ap, shape):
            return ap.broadcast_to(shape)

        def held(eng, s, value):
            eng.wait_ge(s, value)
            eng.sem_inc(s_held, 1)

        def over_batches(eng, phase, body):
            body(0, (phase, 1))
            with eng.Fori(1, B - 1) as b:
                body(b, (phase, b + 1))
            body(B - 1, (phase + 1, 0))

        ctxN = cut(0, (B, D), F32, early2)[0:T]; val_b = cut(2048, (HID,), F32, early2)
        mix = cut(3072, (C, D), F32, early2); mbias = cut(3584, (B, T), F32, early2)
        gateT = cut(0, (C, HID), BF, early); valT = cut(1024, (C, HID), BF, early)
        outT = cut(2048, (HC, D), BF, early); gate_b = cut(3072, (HID,), F32, early)
        wstage = cut(6400, (C, HID)); mring = cut(6400, (4, C * D))
        bSC = cut(5120, (J, T)); bP = cut(5248, (J, T)); bPT = cut(5376, (S,))
        b_nm = small[:, 0:2]; b_sum = small[:, 2:4]; b_ri = small[:, 4:6]; b_rv = small[:, 6:8]
        cXQ = cut(0, (J, D)); cXB = cut(512, (J, D), BF); cXT = cut(768, (C, S), BF)
        cHG = cut(1024, (HID,)); cHS = cHG; cHV = cut(2048, (HID,)); cH = cut(3072, (HID,))
        cHR = cut(4096, (HID,)); cHQ = cut(5120, (HID,), BF); cHT = cut(5632, (HC, P), BF); cY = cut(6144, (D,))
        c_gx = small[:, 8:10]; c_rx = small[:, 10:12]; c_sx = small[:, 12:14]
        c_new = small[:, 14:18]; c_cur = small[:, 18:22]
        c_hm = small[:, 22:23]; c_rh = small[:, 23:24]; c_sh = small[:, 24:25]; c_so = small[:, 25:26]
        dQ = cut(0, (2, S)); dK = cut(0, (NH, S), F32, early); dV = cut(512, (J, D))
        dSS = cut(1024, (2, 4, S)); dP = cut(3072, (2, 4, S)); dPT = cut(5120, (2, 8, P))
        dO = cut(7168, (J, D)); dOT = cut(7680, (C, S)); dY = dO
        d_max = small[:, 32:40].rearrange("p (a b) -> p a b", a=2)
        d_neg = small[:, 40:48].rearrange("p (a b) -> p a b", a=2)
        d_sum = small[:, 48:80]; d_ri = small[:, 80:112]
        eKR = cut(0, (3, 512), F32, early2); eKB = cut(1536, (2, 512), F32, early2)
        eKF = cut(2560, (3, 512), F32, early2); eSQ = eKF
        eSS = cut(0, (GH, KEYS)); eP = cut(1280, (GH, KEYS)); ePT = cut(2560, (3, 512))
        eKT = cut(4096, (XG, KEYS))
        eQR = cut(5376, (512,)); eQB = cut(5888, (512,)); eQS = cut(6400, (512,)); eQA = cut(6912, (512,))
        eQT = cut(7424, (512,))
        eV = w_in[:, :, :].rearrange("p c n -> p (c n)").rearrange("p (a n) -> p a n", a=3)
        eOT = cut(0, (XH, S), F32, early)
        e_ks = small[:, 112:124].rearrange("p (a b) -> p a b", a=3)
        e_kp = small[:, 124:136].rearrange("p (a b) -> p a b", a=3)
        e_rks = small[:, 136:148].rearrange("p (a b) -> p a b", a=3)
        e_q2 = small[:, 148:152]; e_q3 = small[:, 152:156]
        e_rqs = small[:, 156:164].rearrange("p (a b) -> p a b", a=2)
        e_max = small[:, 164:168]
        e_neg = small[:, 168:176].rearrange("p (a b) -> p a b", a=2)
        e_sum = small[:, 176:184].rearrange("p (a b) -> p a b", a=2)
        e_inv = small[:, 184:188]
        fXH = cut(0, (C, S), BF); fXM = cut(256, (C, S), BF); fXL = cut(512, (C, S), BF)
        fR1 = cut(768, (C, S)); fLG = cut(1280, (J, NE)); fE = cut(1344, (J, NE)); fOH = cut(1408, (J, NE))
        fSEL = cut(1472, (J, NE)); fACC = cut(1536, (2, J, D)); fSUM = cut(2560, (J, D))
        f_m8 = small[:, 192:208].rearrange("p (a b) -> p a b", a=2)
        f_i8 = small[:, 208:224].bitcast(U32).rearrange("p (a b) -> p a b", a=2)
        f_if_ = small[:, 224:226]; f_neg = small[:, 226:228]; f_sm = small[:, 228:230]; f_ri = small[:, 230:232]

        mark = {}

        @block.vector
        def _(dve):
            count = [0]

            def const(ins, name=None):
                count[0] += 1
                ins.then_inc(s_c, 1)
                dve.wait_ge(s_c, count[0])
                if name:
                    mark[name] = count[0]

            def ln_stats(phase, b):
                n = phase * B + b
                if phase == MIX:
                    dve.wait_ge(s_lx, 16)
                else:
                    dve.wait_ge(s_x, n - B + 1)
                for j in range(J):
                    last = dve.bn_stats(st[:, j, :], tokens(b, j))
                last.then_inc(s_bn, 1)
                held(dve, s_bn, n + 1)
                for j in range(J):
                    last = dve.bn_aggr(mv[:, j, :], st[:, j, :])
                last.then_inc(s_mv, 1)

            def tokens(b, j):
                return X[:, ds(b, 1), j, :].rearrange("p a d -> p (a d)")

            def batch(b):
                return X[:, ds(b, 1), :, :].rearrange("p a j d -> p (a j) d")

            def ln_apply(phase, b):
                n = phase * B + b
                dve.wait_ge(s_rs, n + 1)
                dve.wait_ge(s_xtp, n)
                for j in range(J):
                    last = dve.tensor_scalar(XN[:, j, :], tokens(b, j), mv[:, j, 0:1], rstd[:, j:j + 1],
                                             ALU.subtract, ALU.mult)
                if phase != FFN:
                    last.then_inc(s_xn, 1)
                    return
                last.then_inc(c_q[0], 1)
                dve.wait_ge(c_q[0], b + 1)
                dve.tensor_reduce(c_gx, XN[:, :, :], AX.X, ALU.max, apply_absolute_value=True).then_inc(c_q[1], 1)
                dve.wait_ge(c_q[1], b + 1)
                dve.tensor_scalar(c_gx, c_gx, 1e-5, None, ALU.max).then_inc(c_q[2], 1)
                dve.wait_ge(c_q[2], b + 1)
                dve.tensor_scalar(c_new[:, 0:2], c_gx, gam127[:, 0:1], None, ALU.mult)
                dve.tensor_scalar(c_new[:, 2:4], c_gx, gam127[:, 1:2], None, ALU.mult)
                dve.reciprocal(c_rx, c_gx).then_inc(c_q[3], 1)
                dve.wait_ge(c_q[3], b + 1)
                dve.tensor_scalar(c_sx, c_rx, 127.0, None, ALU.mult).then_inc(c_q[4], 1)
                dve.wait_ge(c_q[4], b + 1)
                for j in range(J):
                    last = dve.tensor_scalar(cXQ[:, j, :], XN[:, j, :], c_sx[:, j:j + 1], MAGIC, ALU.mult, ALU.add)
                last.then_inc(c_xq, 1)
                dve.wait_ge(c_xq, b + 1)
                dve.tensor_scalar(cXB, cXQ, MAGIC, None, ALU.subtract).then_inc(s_xn, 1)

            def ternary(dst, src, scale):
                const(dve.tensor_scalar(src, src, scale, MAGIC, ALU.mult, ALU.add))
                const(dve.tensor_scalar(src, src, MAGIC, -1.0, ALU.subtract, ALU.max))
                const(dve.tensor_scalar(dst, src, 1.0, None, ALU.min))

            dve.wait_ge(s_l0, 16 * 7)
            const(dve.tensor_copy(identb[:, :], ident[:, :]), "identb")
            for lv in range(LV):
                v = [fly[:, k, :].rearrange("r (a i c) -> r a i c", i=2, c=2 ** (LV - 1 - lv))
                     for k in (lv % 2, (lv + 1) % 2)]
                for o in range(2):
                    f = 4 * lv + o
                    const(dve.tensor_scalar(v[1][:, :, o, :], v[0][:, :, 0, :], factors[:, f:f + 1], None, ALU.mult))
                    const(dve.scalar_tensor_tensor(v[1][:, :, o, :], v[0][:, :, 1, :], factors[:, f + 2:f + 3],
                                                   v[1][:, :, o, :], ALU.mult, ALU.add), "fly")
            dve.wait_ge(s_pp, 1)
            const(dve.tensor_copy(b_fold[:, :], PS[0:NS, 1, 0:D]))
            const(dve.tensor_copy(c_fold[:, :], PS[0:NS, 2, 0:D]), "folds")
            ln_stats(MIX, 0)
            ln_apply(MIX, 0)
            dve.wait_ge(s_pp, 2)
            for c in range(C):
                const(dve.tensor_copy(mix[:, c, :], PS[:, 3 + c, 0:D]))
                const(dve.scalar_tensor_tensor(mix[:, c, c * P:(c + 1) * P], ident[:, :], dvec[:, c:c + 1],
                                               PS[:, 3 + c, c * P:(c + 1) * P], ALU.mult, ALU.add), "mix")
            dve.wait_ge(s_l1, 48)
            const(dve.tensor_copy(mask[:, :, :], masku[:, :, :]))
            const(dve.tensor_scalar(mbias[:, :, :], mask[:, :, :], 1.0, -NEG, ALU.subtract, ALU.mult))
            const(dve.tensor_reduce(valid[:, :], mask[:, :, :], AX.X, ALU.max))

            def mixer(b, nxt):
                ln_stats(*nxt)
                dve.wait_ge(a_mm, b + 1)
                dve.tensor_tensor(batch(b), batch(b), bank(1).rearrange("p (j d) -> p j d", j=J), ALU.add)\
                    .then_inc(s_x, 1)
                ln_apply(*nxt)

            over_batches(dve, MIX, mixer)

            def cross(b, nxt):
                dve.wait_ge(b_s, b + 1)
                dve.scalar_tensor_tensor(bSC, PS[:, 1, 0:J * T].rearrange("p (j t) -> p j t", j=J),
                                         1.0 / 16, bc(mbias[:, ds(b, 1), :], [P, J, T]),
                                         ALU.mult, ALU.add).then_inc(b_c, 1)
                dve.wait_ge(b_c, b + 1)
                dve.tensor_reduce(b_nm, bSC, AX.X, ALU.max, negate=True).then_inc(b_m, 1)
                ln_stats(*nxt)
                dve.wait_ge(b_e, b + 1)
                dve.reciprocal(b_ri, b_sum).then_inc(b_r, 1)
                dve.wait_ge(b_r, b + 1)
                dve.tensor_tensor(b_rv, b_ri, bc(valid[:, ds(b, 1)], [P, J]), ALU.mult).then_inc(b_v2, 1)
                dve.wait_ge(b_v2, b + 1)
                dve.tensor_tensor(bP, bP, bc(b_rv.unsqueeze(2), [P, J, T]), ALU.mult).then_inc(b_p, 1)
                ln_apply(*nxt)
                dve.wait_ge(b_o2, b + 1)
                dve.tensor_tensor(batch(b), batch(b), bank(3).rearrange("p (j d) -> p j d", j=J), ALU.add)\
                    .then_inc(s_x, 1)

            stage = wstage[:, :, :].rearrange("p c n -> p (c n)")
            for k, (dst, s) in enumerate(((gateT, s_lg), (valT, s_lv), (outT, s_lo))):
                dve.wait_ge(s, 16)
                const(dve.tensor_reduce(wsum[:, k:k + 1], stage, AX.X, ALU.add, apply_absolute_value=True), f"wsum{k}")
                dve.wait_ge(s_ps, k + 1)
                const(dve.tensor_scalar(gam[:, k:k + 1], PS[:, 7, k:k + 1], 1.0 / (D * HID), 1e-5, ALU.mult, ALU.max))
                const(dve.reciprocal(rgam[:, k:k + 1], gam[:, k:k + 1]))
                const(dve.tensor_scalar(gam127[:, k:k + 1], gam[:, k:k + 1], 1.0 / 127, None, ALU.mult))
                const(dve.tensor_scalar(stage, stage, rgam[:, k:k + 1], MAGIC, ALU.mult, ALU.add))
                const(dve.tensor_scalar(stage, stage, MAGIC, -1.0, ALU.subtract, ALU.max))
                ins = dve.tensor_scalar(dst[:, :, :].rearrange("p a b -> p (a b)"), stage, 1.0, None, ALU.min)
                count[0] += 1
                ins.then_inc(s_c, 1)
                dve.wait_ge(s_c, count[0])
                mark[f"w{k}"] = count[0]
            dve.wait_ge(s_l5, 64)
            ternary(ew[:, :, :], ew[:, :, :], 2.0)
            mark["ew"] = count[0]
            dve.wait_ge(s_l4, 16 * 13)
            const(dve.tensor_scalar(kw[:, :], kw[:, :], float(XD) ** 0.5, None, ALU.mult))
            const(dve.tensor_scalar(kws[:, :], kws[:, :], float(XD) ** 0.5, None, ALU.mult))
            for dst, tab, w in ((cosq, cosT, qw), (sinq, sinT, qws), (cosk, cosT, kw), (sink, sinT, kws)):
                const(dve.tensor_tensor(dst[:, :, :], tab[:, :, :], bc(w[:, :].unsqueeze(1), [P, J, XD]), ALU.mult),
                      "tables")

            over_batches(dve, CROSS, cross)

            dve.wait_ge(s_l2, 48)

            def ffn(b, nxt):
                dve.tensor_copy(c_cur, c_new).then_inc(c_s[0], 1)
                dve.wait_ge(c_s[0], b + 1)
                for j in range(J):
                    u = J * b + j
                    dve.wait_ge(c_g, u + 1)
                    dve.scalar_tensor_tensor(cHG, bank(1, 2), c_cur[:, j:j + 1], gate_b, ALU.mult, ALU.add)\
                        .then_inc(c_gs, 1)
                    dve.wait_ge(c_v, u + 1)
                    dve.scalar_tensor_tensor(cHV, bank(3, 2), c_cur[:, 2 + j:3 + j], val_b, ALU.mult, ALU.add)\
                        .then_inc(c_vs, 1)
                    if j == 0:
                        ln_stats(*nxt)
                    dve.wait_ge(c_vs, u + 1)
                    dve.wait_ge(c_si, u + 1)
                    dve.tensor_tensor(cH, cHS, cHV, ALU.mult).then_inc(c_h, 1)
                    dve.wait_ge(c_h, u + 1)
                    dve.tensor_reduce(c_hm, cH, AX.X, ALU.max, apply_absolute_value=True).then_inc(c_a, 1)
                    dve.wait_ge(c_a, u + 1)
                    dve.tensor_scalar(c_hm, c_hm, 1e-5, None, ALU.max).then_inc(c_s[1], 1)
                    dve.wait_ge(c_s[1], u + 1)
                    dve.tensor_scalar(c_so, c_hm, gam127[:, 2:3], None, ALU.mult)
                    dve.reciprocal(c_rh, c_hm).then_inc(c_s[2], 1)
                    dve.wait_ge(c_s[2], u + 1)
                    dve.tensor_scalar(c_sh, c_rh, 127.0, None, ALU.mult).then_inc(c_s[3], 1)
                    if j == 0:
                        ln_apply(*nxt)
                    dve.wait_ge(c_hr, u + 1)
                    dve.tensor_scalar(cHQ, cHR, MAGIC, None, ALU.subtract).then_inc(c_hq, 1)
                    dve.wait_ge(c_o, u + 1)
                    dve.scalar_tensor_tensor(cY, PS[:, 6, 0:D], c_so, ffo_b[:, :], ALU.mult, ALU.add)\
                        .then_inc(c_y, 1)
                    dve.wait_ge(c_y, u + 1)
                    last = dve.tensor_tensor(tokens(b, j), tokens(b, j), cY, ALU.add)
                last.then_inc(s_x, 1)

            over_batches(dve, FFN, ffn)

            dve.wait_ge(s_l3, 16 * 7)

            def self_keys(b):
                dve.wait_ge(d_pq, b + 1)
                for h in range(NH):
                    m = h // (P // DH)
                    k = h % (P // DH)
                    last = dve.tensor_scalar(dK[:, h, :], PS[:, 5, m * S:(m + 1) * S], bqk[:, 2 + m:3 + m],
                                             hmask[:, k:k + 1], ALU.add, ALU.mult)
                    if h % 4 == 3:
                        last.then_inc(d_kv, 1)
                dve.wait_ge(d_pv, 8 * b)
                dve.tensor_tensor(dV, bank(6).rearrange("p (j d) -> p j d", j=J),
                                  bc(b_v[:, :].unsqueeze(1), [P, J, D]), ALU.add).then_inc(d_vv, 1)

            def self_finish(b):
                dve.wait_ge(d_y, b + 1)
                dve.tensor_tensor(dY, bank(2).rearrange("p (j d) -> p j d", j=J),
                                  bc(b_o[:, :].unsqueeze(1), [P, J, D]), ALU.add).then_inc(d_yb, 1)
                dve.wait_ge(d_yb, b + 1)
                dve.tensor_tensor(batch(b), batch(b), dY, ALU.add).then_inc(s_x, 1)

            def self_attention(b, nxt):
                def masked_max(i):
                    j, u = i // 4, 8 * b + i
                    n = (j + 1) * P
                    if i >= 2:
                        dve.wait_ge(d_e, u - 1)
                    held(dve, d_s, u + 1)
                    for hh in range(4):
                        last = dve.tensor_tensor_reduce(
                            dSS[:, i % 2, hh, 0:n], PS[:, 4 + 2 * (i % 2) + hh // 2, (hh % 2) * S:(hh % 2) * S + n],
                            causal[:, j, 0:n], 1.0, LOWEST, ALU.add, ALU.max, d_max[:, i % 2, hh:hh + 1])
                    last.then_inc(d_mx, 1)
                    dve.wait_ge(d_mx, u + 1)
                    dve.tensor_scalar(d_neg[:, i % 2, :], d_max[:, i % 2, :], -0.25, None, ALU.mult).then_inc(d_nm, 1)

                def turn(i):
                    u = 8 * b + i
                    if i % 2:
                        dve.wait_ge(d_t, u + 1)
                        dve.wait_ge(d_pv, u - 1)
                        n = 4 * (1 + i // 4) * P
                        dve.tensor_copy(dPT[:, i % 2, :, :].rearrange("p a b -> p (a b)")[:, 0:n],
                                        bank(1, 2)[:, 0:n]).then_inc(d_pt, 1)

                masked_max(0)
                masked_max(1)
                if type(b) is not int or b > 0:
                    self_finish(b - 1)
                for i in range(8):
                    if i + 2 < 8:
                        masked_max(i + 2)
                    turn(i)
                    if i == 2:
                        ln_stats(*nxt)
                    if i == 4:
                        ln_apply(*nxt)
                if nxt[0] == SELF:
                    self_keys(nxt[1])
                dve.wait_ge(d_e, 8 * b + 8)
                dve.reciprocal(d_ri, d_sum).then_inc(d_r, 1)
                dve.wait_ge(d_r, b + 1)
                dve.wait_ge(d_pv, 8 * b + 8)
                dve.tensor_tensor(dO.rearrange("p j (h k) -> p (j h) k", k=DH),
                                  bank(3).rearrange("p (h k) -> p h k", k=DH),
                                  bc(d_ri.unsqueeze(2), [P, J * NH, DH]), ALU.mult).then_inc(d_o, 1)

            self_keys(0)
            over_batches(dve, SELF, self_attention)
            self_finish(B - 1)

            def turn_keys(b):
                for seg in range(3):
                    n = T if seg == 1 else P
                    dve.wait_ge(e_sq, 3 * b + seg + 1)
                    dve.tensor_reduce(e_ks[0:n, seg, :], eSQ[0:n, seg, :].rearrange("p (g d) -> p g d", g=XG),
                                      AX.X, ALU.add).then_inc(e_ssq, 1)
                for seg in range(3):
                    n = T if seg == 1 else P
                    dve.wait_ge(e_rk, 3 * b + seg + 1)
                    kr = eKR[0:n, seg, :].rearrange("p (g d) -> p g d", g=XG)
                    dve.tensor_tensor(kr, kr, bc(e_rks[0:n, seg, :].unsqueeze(2), [n, XG, XD]), ALU.mult)\
                        .then_inc(e_kn, 1)
                for seg in range(3):
                    n = T if seg == 1 else P
                    dve.wait_ge(e_kn, 3 * b + seg + 1)
                    kr = eKR[0:n, seg, :].rearrange("p (g d) -> p g d", g=XG)
                    kf = eKF[0:n, seg, :].rearrange("p (g d) -> p g d", g=XG)
                    tab = kw[0:n, :].unsqueeze(1) if seg == 1 else cosk[:, seg // 2, :].unsqueeze(1)
                    dve.tensor_tensor(kf, kr, bc(tab, [n, XG, XD]), ALU.mult).then_inc(e_ka, 1)
                for k, seg in enumerate((0, 2)):
                    dve.wait_ge(e_ka, 3 * b + seg + 1)
                    dve.wait_ge(e_kb, 2 * b + k + 1)
                    dve.tensor_tensor(eKF[:, seg, :], eKF[:, seg, :], eKB[:, k, :], ALU.add).then_inc(e_kf, 1)

            def hybrid_finish(b):
                dve.wait_ge(e_y, J * b + J)
                dve.tensor_tensor(batch(b), batch(b), bank(0).rearrange("p (j d) -> p j d", j=J), ALU.add)\
                    .then_inc(s_x, 1)

            def hybrid(b, nxt):
                def turn_query(i):
                    j, u = i // XG, 8 * b + i
                    dve.wait_ge(e_qt, u)
                    dve.wait_ge(e_qr, u + 1)
                    dve.tensor_tensor(eQA.rearrange("p (g d) -> p g d", g=GH),
                                      eQR.rearrange("p (g d) -> p g d", g=GH),
                                      bc(cosq[:, j, :].unsqueeze(1), [P, GH, XD]), ALU.mult).then_inc(e_qa, 1)
                    dve.wait_ge(e_qs, u + 1)
                    dve.tensor_reduce(e_q2, eQS.rearrange("p (g d) -> p g d", g=GH), AX.X, ALU.add)\
                        .then_inc(e_qq, 1)
                    dve.wait_ge(e_qa, u + 1)
                    dve.wait_ge(e_qb, u + 1)
                    dve.tensor_tensor(eQA, eQA, eQB, ALU.add).then_inc(e_qf, 1)

                def masked_max(i):
                    j, u = i // XG, 8 * b + i
                    n = KEYS if j else P + T
                    dve.wait_ge(e_e, u)
                    for hh in range(GH):
                        held(dve, e_s, GH * u + hh + 1)
                        dve.tensor_tensor_reduce(eSS[:, hh, 0:n], PS[:, 3 + hh % 2, 0:n], kmask[:, j, 0:n],
                                                 1.0, LOWEST, ALU.add, ALU.max, e_max[:, hh:hh + 1]).then_inc(e_mx, 1)
                    dve.wait_ge(e_mx, GH * (u + 1))
                    dve.wait_ge(e_rq, u + 1)
                    dve.scalar_tensor_tensor(e_neg[:, i % 2, :], e_max, -1.0, e_rqs[:, i % 2, :], ALU.mult, ALU.mult)\
                        .then_inc(e_nm, 1)

                def normalise(i):
                    j, u = i // XG, 8 * b + i
                    n = KEYS if j else P + T
                    dve.wait_ge(e_e, u + 1)
                    dve.reciprocal(e_inv, e_sum[:, i % 2, :]).then_inc(e_ri, 1)
                    dve.wait_ge(e_ri, u + 1)
                    for hh in range(GH):
                        last = dve.tensor_scalar(eP[:, hh, 0:n], eP[:, hh, 0:n], e_inv[:, hh:hh + 1], None, ALU.mult)
                    last.then_inc(e_p, 1)

                def turn_probs(i):
                    u = 8 * b + i
                    dve.wait_ge(e_t, u + 1)
                    dve.wait_ge(e_pv, u)
                    last = dve.tensor_copy(ePT[0:T, 1, :], PS[0:T, 6, :])
                    if i >= XG:
                        last = dve.tensor_copy(ePT[:, 2, :], PS[:, 7, :])
                    last.then_inc(e_ptd, 1)

                turn_query(0)
                turn_query(1)
                if type(b) is not int or b > 0:
                    hybrid_finish(b - 1)
                masked_max(0)
                for i in range(8):
                    if i + 2 < 8:
                        turn_query(i + 2)
                    normalise(i)
                    if i + 1 < 8:
                        masked_max(i + 1)
                    turn_probs(i)
                    if i == 3:
                        ln_stats(*nxt)
                    if i == 5:
                        ln_apply(*nxt)
                if nxt[0] == HYBRID:
                    turn_keys(nxt[1])

            turn_keys(0)
            over_batches(dve, HYBRID, hybrid)
            hybrid_finish(B - 1)

            def moe(b, nxt):
                dve.wait_ge(f_xh, b + 1)
                dve.tensor_tensor(fR1, XT[:, :, :], fXH, ALU.subtract).then_inc(f_r1, 1)
                dve.wait_ge(f_xm, b + 1)
                dve.tensor_tensor(fXL, fR1, fXM, ALU.subtract).then_inc(f_xl, 1)
                dve.wait_ge(f_l, b + 1)
                dve.tensor_copy(fLG, PS[:, 7, 0:J * NE].rearrange("p (j e) -> p j e", j=J)).then_inc(f_lg, 1)
                held(dve, f_lg, b + 1)
                for j in range(J):
                    last = dve.max(f_m8[:, j, :], fLG[:, j, :])
                last.then_inc(f_m, 1)
                dve.wait_ge(f_m, b + 1)
                dve.tensor_scalar(f_neg, f_m8[:, :, 0], -1.0, None, ALU.mult).then_inc(f_nm, 1)
                for j in range(J):
                    last = dve.max_index(f_i8[:, j, :], f_m8[:, j, :], fLG[:, j, :])
                last.then_inc(f_i, 1)
                dve.wait_ge(f_i, b + 1)
                dve.tensor_copy(f_if_, f_i8[:, :, 0]).then_inc(f_if, 1)
                dve.wait_ge(f_if, b + 1)
                for j in range(J):
                    last = dve.tensor_scalar(fOH[:, j, :], iota[:, :], f_if_[:, j:j + 1], None, ALU.is_equal)
                last.then_inc(f_oh, 1)
                dve.wait_ge(f_oh, b + 1)
                dve.wait_ge(f_e, b + 1)
                dve.reciprocal(f_ri, f_sm).then_inc(f_r, 1)
                dve.wait_ge(f_r, b + 1)
                dve.tensor_tensor(fSEL, fOH, bc(f_ri.unsqueeze(2), [P, J, NE]), ALU.mult).then_inc(f_sel, 1)
                dve.memset(fACC, 0.0).then_inc(f_z, 1)
                dve.wait_ge(f_sel, b + 1)
                dve.wait_ge(f_z, b + 1)
                if nxt[0] == MOE:
                    ln_stats(*nxt)
                acc = 0
                for j in range(J):
                    for e in range(NE):
                        n = j * (NE // 2) + e // 2
                        if e % 2 == 0:
                            dve.wait_ge(f_y, J * NE // 2 * b + n + 1)
                        if e >= 2:
                            dve.wait_ge(f_acc, J * NE * b + j * NE + e - 1)
                        dve.scalar_tensor_tensor(fACC[:, e % 2, j, :], PS[:, 1 + n % 6, (e % 2) * D:(e % 2 + 1) * D],
                                                 fSEL[:, j, e:e + 1], fACC[:, e % 2, j, :], ALU.mult, ALU.add)\
                            .then_inc(f_acc, 1)
                dve.wait_ge(f_acc, J * NE * (b + 1))
                dve.tensor_tensor(fSUM, fACC[:, 0, :, :], fACC[:, 1, :, :], ALU.add).then_inc(f_s, 1)
                dve.wait_ge(f_s, b + 1)
                dve.tensor_tensor(fSUM, fSUM, bc(esc[:, :].unsqueeze(1), [P, J, D]), ALU.mult).then_inc(f_w, 1)
                dve.wait_ge(f_w, b + 1)
                dve.tensor_tensor(batch(b), batch(b), fSUM, ALU.add).then_inc(s_x, 1)
                if nxt[0] == MOE:
                    ln_apply(*nxt)

            over_batches(dve, MOE, moe)

        @block.sync
        def _(sp):
            sp.dma_start(X[:, :, :, :], I["x"].rearrange("b (j p) d -> p b j d", p=P)).then_inc(s_lx, 16)
            for dst, name in ((wbrT, "wbrT"), (wcrT, "wcrT"), (wcm, "wcm"), (ident, "ident")):
                sp.dma_start(dst[:, :], I[name]).then_inc(s_l0, 16)
            sp.dma_start(fly[:, 0, :], I["wbs"]).then_inc(s_l0, 16)
            sp.dma_start(factors[:, :], I["factors"].partition_broadcast(R)).then_inc(s_l0, 16)
            sp.dma_start(dvec[:, :], I["dvec"]).then_inc(s_l0, 16)
            sp.dma_start(ctxT[:, :, :, :], I["ctxT"].rearrange("(c p) b t -> p c b t", p=P)).then_inc(s_l1, 16)
            sp.dma_start(ctxN[:, :, :], I["ctx"].rearrange("b t d -> t b d")).then_inc(s_l1, 16)
            sp.dma_start(masku[:, :, :], I["mask"].partition_broadcast(P)).then_inc(s_l1, 16)
            for n, (src, s) in enumerate((("gateT", s_lg), ("valT", s_lv), ("outT", s_lo))):
                if n:
                    sp.wait_ge(s_c, mark[f"w{n - 1}"])
                cols = D if src == "outT" else HID
                sp.dma_start(wstage[:, :, :].rearrange("p c n -> p (c n)").rearrange("p (c n) -> p c n", n=cols),
                             I[src].rearrange("(c p) n -> p c n", p=P)).then_inc(s, 16)
            sp.dma_start(gate_b, I["gate_b"].partition_broadcast(P)).then_inc(s_l2, 16)
            sp.dma_start(val_b, I["val_b"].partition_broadcast(P)).then_inc(s_l2, 16)
            sp.dma_start(ffo_b[:, :], I["ffo_b"].partition_broadcast(P)).then_inc(s_l2, 16)
            sp.dma_start(w_in[:, :, :], I["w_in"].rearrange("(c p) n -> p c n", p=P)).then_inc(s_l3, 16)
            sp.dma_start(w_out[:, :, :], I["w_out"].rearrange("(c p) n -> p c n", p=P)).then_inc(s_l3, 16)
            sp.dma_start(bqk[:, :], I["bqk"]).then_inc(s_l3, 16)
            sp.dma_start(b_v[:, :], I["b_v"].partition_broadcast(P)).then_inc(s_l3, 16)
            sp.dma_start(b_o[:, :], I["b_o"].partition_broadcast(P)).then_inc(s_l3, 16)
            sp.dma_start(hmask[:, :], I["hmask"]).then_inc(s_l3, 16)
            sp.dma_start(causal[:, :, :], I["causal"]).then_inc(s_l3, 16)
            for dst, name in ((wq, "wq"), (wk, "wk"), (wv, "wv"), (wkc, "wkc"), (wvc, "wvc"), (wo, "wo"),
                              (cosT, "cos"), (sinT, "sin")):
                sp.dma_start(dst[:, :, :], I[name].rearrange("(c p) n -> p c n", p=P)).then_inc(s_l4, 16)
            for dst, name in ((qw, "qw"), (qws, "qws"), (kw, "kw"), (kws, "kws")):
                sp.dma_start(dst[:, :], I[name].partition_broadcast(P)).then_inc(s_l4, 16)
            sp.dma_start(kmask[:, :, :], I["kmask"]).then_inc(s_l4, 16)
            sp.dma_start(ew[:, :, :], I["ewT"].rearrange("(c p) n -> p c n", p=P)).then_inc(s_l5, 16)
            sp.dma_start(rwT[:, :, :], I["rwT"].rearrange("(c p) n -> p c n", p=P)).then_inc(s_l5, 16)
            sp.dma_start(iota[:, :], I["iota"].partition_broadcast(P)).then_inc(s_l5, 16)
            sp.dma_start(esc[:, :], I["esc"].partition_broadcast(P)).then_inc(s_l5, 16)
            sp.wait_ge(s_c, mark["w2"])
            for e in range(4):
                sp.dma_start(mring[:, e, :], I["masksT"][e]).then_inc(s_mld[e], 16)
            with sp.Fori(1, NE // 4) as n:
                for e in range(4):
                    sp.wait_ge(s_mfree, 4 * n + (e - 3))
                    sp.dma_start(mring[:, e, :], I["masksT"][ds(4 * n + e, 1)].rearrange("a p n -> p (a n)"))\
                        .then_inc(s_mld[e], 16)
            with sp.Fori(0, B) as b:
                sp.wait_ge(s_x, MOE * B + b + 1)
                sp.dma_start(out[ds(b, 1)].rearrange("a (j p) d -> p (a j) d", p=P),
                             X[:, ds(b, 1), :, :].rearrange("p a j d -> p (a j) d")).then_inc(s_out, 16)
            sp.wait_ge(s_out, 16 * B)


        @block.gpsimd
        def _(pool):
            pool.memset(halves[:, :], -0.5).then_inc(s_pc, 1)
            pool.memset(ones[:, :], 1.0).then_inc(s_pc, 1)
            pool.memset(magic[:, :], MAGIC).then_inc(s_pc, 1)
            pool.wait_ge(s_pc, 3)

            def rstds(phase, b):
                n = phase * B + b
                held(pool, s_mv, n + 1)
                pool.tensor_scalar(ve[:, :], mv[:, :, 1], LN_EPS, None, ALU.add).then_inc(s_ve, 1)
                pool.wait_ge(s_ve, n + 1)
                pool.tensor_tensor(rstd[:, :], ve[:, :], halves[:, 0:J], ALU.pow).then_inc(s_rs, 1)

            rstds(MIX, 0)
            for phase in (MIX, CROSS):
                over_batches(pool, phase, lambda b, nxt: rstds(*nxt))

            def ffn(b, nxt):
                for e in range(4):
                    pool.wait_ge(s_mld[e], 16 * b + 16)
                    pool.tensor_tensor(EW[:, ds(4 * b + e, 1), :].rearrange("p a n -> p (a n)"),
                                       mring[:, e, :], ew[:, :, :].rearrange("p c n -> p (c n)"),
                                       ALU.mult).then_inc(s_mfree, 1)
                rstds(*nxt)

            pool.wait_ge(s_c, mark["ew"])
            over_batches(pool, FFN, ffn)
            over_batches(pool, SELF, lambda b, nxt: rstds(*nxt))

            def turn_keys(b):
                for seg in range(3):
                    n = T if seg == 1 else P
                    pool.wait_ge(e_kr, 3 * b + seg + 1)
                    pool.tensor_tensor(eSQ[0:n, seg, :], eKR[0:n, seg, :], eKR[0:n, seg, :], ALU.mult)\
                        .then_inc(e_sq, 1)
                for seg in range(3):
                    n = T if seg == 1 else P
                    held(pool, e_ssq, 3 * b + seg + 1)
                    pool.tensor_scalar(e_kp[0:n, seg, :], e_ks[0:n, seg, :], RMS_EPS * XD, None, ALU.add)\
                        .then_inc(e_ve, 1)
                    pool.wait_ge(e_ve, 3 * b + seg + 1)
                    pool.tensor_tensor(e_rks[0:n, seg, :], e_kp[0:n, seg, :], halves[0:n, 0:XG], ALU.pow)\
                        .then_inc(e_rk, 1)
                for k, seg in enumerate((0, 2)):
                    pool.wait_ge(e_kn, 3 * b + seg + 1)
                    kn = eKR[:, seg, :].rearrange("p (g u v) -> p g u v", g=XG, u=2)
                    kb = eKB[:, k, :].rearrange("p (g u v) -> p g u v", g=XG, u=2)
                    for u in range(2):
                        last = pool.tensor_tensor(kb[:, :, u, :], kn[:, :, 1 - u, :],
                                                  bc(sink[:, k, 64 * u:64 * u + 64].unsqueeze(1), [P, XG, 64]),
                                                  ALU.mult)
                    last.then_inc(e_kb, 1)

            def hybrid(b, nxt):
                def query(i):
                    j, u = i // XG, 8 * b + i
                    pool.wait_ge(e_qr, u + 1)
                    pool.wait_ge(e_qq, u)
                    pool.wait_ge(e_qf, u)
                    pool.tensor_tensor(eQS, eQR, eQR, ALU.mult).then_inc(e_qs, 1)
                    q = eQR.rearrange("p (g u v) -> p g u v", g=GH, u=2)
                    qb = eQB.rearrange("p (g u v) -> p g u v", g=GH, u=2)
                    for h in range(2):
                        last = pool.tensor_tensor(qb[:, :, h, :], q[:, :, 1 - h, :],
                                                  bc(sinq[:, j, 64 * h:64 * h + 64].unsqueeze(1), [P, GH, 64]),
                                                  ALU.mult)
                    last.then_inc(e_qb, 1)
                    held(pool, e_qq, u + 1)
                    pool.tensor_scalar(e_q3, e_q2, RMS_EPS * XD, None, ALU.add).then_inc(e_qv, 1)
                    pool.wait_ge(e_qv, u + 1)
                    if i >= 2:
                        pool.wait_ge(e_e, u - 1)
                    pool.tensor_tensor(e_rqs[:, i % 2, :], e_q3, halves[:, 0:GH], ALU.pow).then_inc(e_rq, 1)

                for i in range(8):
                    query(i)
                    if i == 6:
                        rstds(*nxt)
                if nxt[0] == HYBRID:
                    turn_keys(nxt[1])

            turn_keys(0)
            over_batches(pool, HYBRID, hybrid)
            with pool.Fori(1, B) as b:
                rstds(MOE, b)

        @block.scalar
        def _(act):
            def xt_copy(nxt, used=(), at=0):
                phase, b = nxt
                for s, value in used:
                    act.wait_ge(s, value)
                act.wait_ge(s_xtp, phase * B + b + 1)
                src, dst = (bank(at), XT[:, :, :].rearrange("p c s -> p (c s)")) if phase != FFN else \
                    (pXT[:, 0:D].bitcast(BF), cXT.rearrange("p c s -> p (c s)"))
                act.activation(dst, src, ACT.Copy).then_inc(s_xt, 1)

            act.wait_ge(s_pc, 3)
            xt_copy((MIX, 0))
            over_batches(act, MIX, lambda b, nxt: xt_copy(nxt, [(a_mm, b + 1)]))

            def cross(b, nxt):
                act.wait_ge(b_m, b + 1)
                for j in range(J):
                    last = act.activation(bP[:, j, :], bSC[:, j, :], ACT.Exp, bias=b_nm[:, j:j + 1],
                                          accum_out=b_sum[:, j:j + 1])
                last.then_inc(b_e, 1)
                act.wait_ge(b_t, b + 1)
                act.activation(bPT[0:T, :], PS[0:T, 2, 0:S], ACT.Copy).then_inc(b_tc, 1)
                xt_copy(nxt, [(b_s, b + 1)])

            over_batches(act, CROSS, cross)

            def ffn(b, nxt):
                for j in range(J):
                    u = J * b + j
                    act.wait_ge(c_gs, u + 1)
                    act.activation(cHS, cHG, ACT.Silu).then_inc(c_si, 1)
                    act.wait_ge(c_s[3], u + 1)
                    act.activation(cHR, cH, ACT.Identity, bias=magic[:, 0:1], scale=c_sh).then_inc(c_hr, 1)
                    act.wait_ge(c_t, u + 1)
                    act.activation(cHT.rearrange("p a b -> p (a b)"), bank(5).bitcast(BF), ACT.Copy).then_inc(c_ht, 1)
                    if j == 0:
                        xt_copy(nxt, [(c_v, J * b + 2)])

            over_batches(act, FFN, ffn)
            act.wait_ge(s_l3, 16 * 7)

            def self_queries(b):
                act.wait_ge(d_pq, b + 1)
                for m in range(2):
                    last = act.activation(dQ[:, m, :], PS[:, 4, m * S:(m + 1) * S], ACT.Identity, bias=bqk[:, m:m + 1])
                last.then_inc(d_q, 1)

            def self_finish(b):
                act.wait_ge(d_ot, b + 1)
                act.activation(dOT.rearrange("p c s -> p (c s)"), bank(1), ACT.Copy).then_inc(d_oc, 1)

            def self_attention(b, nxt):
                def exps(i):
                    j, u = i // 4, 8 * b + i
                    n = (j + 1) * P
                    act.wait_ge(d_nm, u + 1)
                    if i >= 2:
                        act.wait_ge(d_t, u - 1)
                    for hh in range(4):
                        h = j * NH + 4 * (i % 4) + hh
                        last = act.activation(dP[:, i % 2, hh, 0:n], dSS[:, i % 2, hh, 0:n], ACT.Exp,
                                              bias=d_neg[:, i % 2, hh:hh + 1], scale=0.25,
                                              accum_out=d_sum[:, h:h + 1])
                    last.then_inc(d_e, 1)

                exps(0)
                if type(b) is not int or b > 0:
                    self_finish(b - 1)
                for i in range(8):
                    if i + 1 < 8:
                        exps(i + 1)
                    if i % 2 == 0:
                        u = 8 * b + i
                        act.wait_ge(d_t, u + 1)
                        if i >= 2:
                            act.wait_ge(d_pv, u - 1)
                        n = 4 * (1 + i // 4) * P
                        act.activation(dPT[:, 0, :, :].rearrange("p a b -> p (a b)")[:, 0:n],
                                       bank(1, 2)[:, 0:n], ACT.Copy).then_inc(d_pt, 1)
                    if i == 5:
                        xt_copy(nxt, [(d_pq, b + 1)])
                if nxt[0] == SELF:
                    self_queries(nxt[1])

            self_queries(0)
            over_batches(act, SELF, self_attention)
            self_finish(B - 1)

            def raw_keys(b, seg):
                n = T if seg == 1 else P
                act.wait_ge(e_k, 3 * b + seg + 1)
                act.wait_ge(e_kt, 3 * b)
                act.activation(eKR[0:n, seg, :], PS[0:n, 1, :], ACT.Copy).then_inc(e_kr, 1)

            def context(b):
                act.wait_ge(e_v, 3 * b)
                act.activation(eCT[:, :, :], ctxT[:, :, ds(b, 1), :].rearrange("p c a t -> p c (a t)"), ACT.Copy)\
                    .then_inc(e_ct, 1)

            def hybrid(b, nxt):
                def raw_query(i):
                    u = 8 * b + i
                    act.wait_ge(e_q, u + 1)
                    act.wait_ge(e_qb, u)
                    act.wait_ge(e_qf, u)
                    act.activation(eQR, PS[:, 1, :], ACT.Copy).then_inc(e_qr, 1)

                def query(i):
                    u = 8 * b + i
                    act.wait_ge(e_qt, u + 1)
                    act.wait_ge(e_s, GH * u)
                    act.activation(eQT, PS[:, 2, :], ACT.Copy).then_inc(e_qc, 1)

                def exps(i):
                    j, u = i // XG, 8 * b + i
                    n = KEYS if j else P + T
                    act.wait_ge(e_nm, u + 1)
                    act.wait_ge(e_t, u)
                    for hh in range(GH):
                        last = act.activation(eP[:, hh, 0:n], eSS[:, hh, 0:n], ACT.Exp,
                                              bias=e_neg[:, i % 2, hh:hh + 1], scale=e_rqs[:, i % 2, hh:hh + 1],
                                              accum_out=e_sum[:, i % 2, hh:hh + 1])
                    last.then_inc(e_e, 1)

                def outputs(i):
                    u = 8 * b + i
                    j, g = i // XG, i % XG
                    act.wait_ge(e_pv, u + 1)
                    if i == 0:
                        act.wait_ge(e_y, J * b)
                    act.activation(eOT[:, GH * g:GH * g + GH, j * P:(j + 1) * P],
                                   PS[:, 0, :].rearrange("p (h s) -> p h s", h=GH), ACT.Copy).then_inc(e_oc, 1)

                raw_query(0)
                for seg in range(3):
                    n = T if seg == 1 else P
                    act.wait_ge(e_v, 3 * b + seg + 1)
                    act.activation(eV[0:n, seg, :], PS[0:n, 5 + seg, :], ACT.Copy).then_inc(e_vr, 1)
                for seg in range(3):
                    n = T if seg == 1 else P
                    at = (0, P, P + T)[seg]
                    act.wait_ge(e_kt, 3 * b + seg + 1)
                    act.activation(eKT[:, :, at:at + n],
                                   PS[:, 2 + seg, 0:XG * n].rearrange("p (g n) -> p g n", g=XG),
                                   ACT.Copy).then_inc(e_kc, 1)
                query(0)
                raw_query(1)
                for i in range(8):
                    u = 8 * b + i
                    if i + 1 < 8:
                        query(i + 1)
                    if i + 2 < 8:
                        raw_query(i + 2)
                    if i == 6:
                        xt_copy(nxt, [(e_q, 8 * b + 8)], 1)
                        if nxt[0] == HYBRID:
                            context(nxt[1])
                    exps(i)
                    if i >= 1:
                        outputs(i - 1)
                    if nxt[0] == HYBRID and i >= 6:
                        raw_keys(nxt[1], i - 6)
                    act.wait_ge(e_t, u + 1)
                    act.wait_ge(e_pv, u)
                    act.activation(ePT[:, 0, :], PS[:, 5, :], ACT.Copy).then_inc(e_pta, 1)
                if nxt[0] == HYBRID:
                    raw_keys(nxt[1], 2)
                outputs(7)

            context(0)
            for seg in range(3):
                raw_keys(0, seg)
            over_batches(act, HYBRID, hybrid)

            def moe(b, nxt):
                act.wait_ge(s_xt, MOE * B + b + 1)
                act.wait_ge(f_y, J * NE // 2 * b)
                act.activation(fXH, XT[:, :, :], ACT.Copy).then_inc(f_xh, 1)
                act.wait_ge(f_r1, b + 1)
                act.activation(fXM, fR1, ACT.Copy).then_inc(f_xm, 1)
                act.wait_ge(f_nm, b + 1)
                for j in range(J):
                    last = act.activation(fE[:, j, :], fLG[:, j, :], ACT.Exp, bias=f_neg[:, j:j + 1],
                                          accum_out=f_sm[:, j:j + 1])
                last.then_inc(f_e, 1)
                if nxt[0] == MOE:
                    xt_copy(nxt, [(f_l, b + 1), (f_r1, b + 1)])

            over_batches(act, MOE, moe)

        @block.tensor
        def _(pe):
            def product(dst, lhs, rhs, first=True, last=True):
                return pe.matmul(dst, lhs, rhs, start=first, stop=last)

            def xt_turn(phase, b, to=0):
                n = phase * B + b
                pe.wait_ge(s_xn, n + 1)
                pe.wait_ge(s_xt, n)
                for c in range(C):
                    for j in range(J):
                        at = c * S + j * P
                        if phase == FFN:
                            last = pe.transpose(pXT[:, 0:D].bitcast(BF)[:, at:at + P],
                                                cXB[:, j, c * P:(c + 1) * P], identb[:, :])
                        else:
                            last = pe.transpose(PS[:, to, at:at + P], XN[:, j, c * P:(c + 1) * P], ident[:, :])
                last.then_inc(s_xtp, 1)

            pe.wait_ge(s_c, mark["fly"])
            product(PS[0:NS, 1, 0:D], fly[:, LV % 2, :], wbrT[:, :])
            product(PS[0:NS, 2, 0:D], wcrT[:, :], wcm[:, :]).then_inc(s_pp, 1)
            pe.wait_ge(s_c, mark["folds"])
            for c in range(C):
                last = product(PS[:, 3 + c, 0:D], b_fold[:, c * P:(c + 1) * P], c_fold[:, :])
            last.then_inc(s_pp, 1)
            xt_turn(MIX, 0)
            pe.wait_ge(s_c, mark["mix"])

            def mixer(b, nxt):
                pe.wait_ge(s_xt, b + 1)
                pe.wait_ge(s_x, b)
                for j in range(J):
                    for c in range(C):
                        last = product(PS[:, 1, j * D:(j + 1) * D], XT[:, c, j * P:(j + 1) * P], mix[:, c, :],
                                       c == 0, c == C - 1)
                last.then_inc(a_mm, 1)
                xt_turn(*nxt)

            over_batches(pe, MIX, mixer)

            for k in range(3):
                pe.wait_ge(s_c, mark[f"wsum{k}"])
                product(PS[:, 7, k:k + 1], ones[:, :], wsum[:, k:k + 1]).then_inc(s_ps, 1)

            def cross(b, nxt):
                pe.wait_ge(s_xt, CROSS * B + b + 1)
                pe.wait_ge(s_x, CROSS * B + b)
                for j in range(J):
                    for c in range(C):
                        last = product(PS[:, 1, j * T:(j + 1) * T], XT[:, c, j * P:(j + 1) * P],
                                       ctxT[:, c, ds(b, 1), :].rearrange("p a t -> p (a t)"), c == 0, c == C - 1)
                last.then_inc(b_s, 1)
                held(pe, b_p, b + 1)
                for j in range(J):
                    last = pe.transpose(PS[0:T, 2, j * P:(j + 1) * P], bP[:, j, :], ident[:, :])
                last.then_inc(b_t, 1)
                pe.wait_ge(b_tc, b + 1)
                for j in range(J):
                    last = product(PS[:, 3, j * D:(j + 1) * D], bPT[0:T, j * P:(j + 1) * P],
                                   ctxN[:, ds(b, 1), :].rearrange("p a d -> p (a d)"))
                last.then_inc(b_o2, 1)
                xt_turn(*nxt)

            over_batches(pe, CROSS, cross)

            def gate_value(b, j):
                u = J * b + j
                pe.wait_ge(s_xt, FFN * B + b + 1)
                pe.wait_ge(c_vs, u)
                for w, at, s in ((gateT, 1, c_g), (valT, 3, c_v)):
                    for n in range(2):
                        for c in range(C):
                            last = product(PS[:, at + n, :], cXT[:, c, j * P:(j + 1) * P],
                                           w[:, c, 512 * n:512 * n + 512], c == 0, c == C - 1)
                    last.then_inc(s, 1)

            def down(b, j):
                u = J * b + j
                pe.wait_ge(c_hq, u + 1)
                for m in range(HC):
                    last = pe.transpose(bank(5).bitcast(BF)[:, m * P:(m + 1) * P], cHQ[:, m * P:(m + 1) * P], identb[:, :])
                last.then_inc(c_t, 1)
                pe.wait_ge(c_ht, u + 1)
                for m in range(HC):
                    last = product(PS[:, 6, 0:D], cHT[:, m, :], outT[:, m, :], m == 0, m == HC - 1)
                last.then_inc(c_o, 1)

            def ffn(b, nxt):
                gate_value(b, 1)
                down(b, 0)
                xt_turn(*nxt)
                if nxt[0] == FFN:
                    gate_value(nxt[1], 0)
                down(b, 1)

            pe.wait_ge(s_c, mark["w2"])
            pe.wait_ge(s_x, FFN * B)
            gate_value(0, 0)
            over_batches(pe, FFN, ffn)

            pe.wait_ge(s_l3, 16 * 7)

            def self_project(b):
                pe.wait_ge(s_xt, SELF * B + b + 1)
                pe.wait_ge(d_mx, 8 * b)
                for m in range(4):
                    for c in range(C):
                        product(PS[:, 4 + m // 2, (m % 2) * S:(m % 2 + 1) * S], w_in[:, c, m * P:(m + 1) * P],
                                XT[:, c, :], c == 0, c == C - 1)
                for j in range(J):
                    for c in range(C):
                        last = product(PS[:, 6, j * D:(j + 1) * D], XT[:, c, j * P:(j + 1) * P],
                                       w_in[:, c, 2 * D:3 * D], c == 0, c == C - 1)
                last.then_inc(d_pq, 1)

            def self_finish(b):
                pe.wait_ge(d_pt, 8 * b + 8)
                pe.wait_ge(d_o, b + 1)
                for c in range(C):
                    for j in range(J):
                        last = pe.transpose(PS[:, 1, c * S + j * P:c * S + (j + 1) * P], dO[:, j, c * P:(c + 1) * P],
                                            ident[:, :])
                last.then_inc(d_ot, 1)
                pe.wait_ge(d_oc, b + 1)
                for j in range(J):
                    for c in range(C):
                        last = product(PS[:, 2, j * D:(j + 1) * D], dOT[:, c, j * P:(j + 1) * P], w_out[:, c, :],
                                       c == 0, c == C - 1)
                last.then_inc(d_y, 1)

            def self_attention(b, nxt):
                def scores(i):
                    j, u = i // 4, 8 * b + i
                    n = (j + 1) * P
                    if i == 0:
                        pe.wait_ge(d_q, b + 1)
                        pe.wait_ge(d_vv, b + 1)
                    if i >= 2:
                        pe.wait_ge(d_mx, u - 1)
                    for hh in range(4):
                        h = 4 * (i % 4) + hh
                        last = product(PS[:, 4 + 2 * (i % 2) + hh // 2, (hh % 2) * S:(hh % 2) * S + n],
                                       dQ[:, h // 8, j * P:(j + 1) * P], dK[:, h, 0:n])
                    last.then_inc(d_s, 1)

                def turn(i):
                    j, u = i // 4, 8 * b + i
                    pe.wait_ge(d_e, u + 1)
                    pe.wait_ge(d_pt, u)
                    if i == 0:
                        pe.wait_ge(d_yb, b)
                    for hh in range(4):
                        for k in range(j + 1):
                            at = (hh * (j + 1) + k) * P
                            last = pe.transpose(bank(1, 2)[:, at:at + P], dP[:, i % 2, hh, k * P:(k + 1) * P], ident[:, :])
                    last.then_inc(d_t, 1)

                def outputs(i):
                    j, u = i // 4, 8 * b + i
                    pe.wait_ge(d_pt, u + 1)
                    if i == 0:
                        pe.wait_ge(d_o, b)
                    for hh in range(4):
                        h = 4 * (i % 4) + hh
                        for k in range(j + 1):
                            last = product(PS[:, 3, j * D + h * DH:j * D + (h + 1) * DH],
                                           dPT[:, i % 2, hh * (j + 1) + k, :], dV[:, k, h * DH:(h + 1) * DH],
                                           k == 0, k == j)
                    last.then_inc(d_pv, 1)

                scores(0)
                scores(1)
                if type(b) is not int or b > 0:
                    self_finish(b - 1)
                for i in range(8):
                    if i + 2 < 8:
                        scores(i + 2)
                    turn(i)
                    if i >= 1:
                        outputs(i - 1)
                    if i == 5:
                        xt_turn(*nxt)
                if nxt[0] == SELF:
                    self_project(nxt[1])
                outputs(7)

            pe.wait_ge(s_x, SELF * B)
            self_project(0)
            over_batches(pe, SELF, self_attention)
            self_finish(B - 1)

            pe.wait_ge(s_c, mark["tables"])

            def raw_keys(b, seg):
                n = T if seg == 1 else P
                pe.wait_ge(s_xt, HYBRID * B + b + 1)
                pe.wait_ge(e_ct, b + 1)
                pe.wait_ge(e_kr, 3 * b + seg)
                for c in range(C):
                    last = product(PS[0:n, 1, :], eCT[:, c, :] if seg == 1 else
                                   XT[:, c, (seg // 2) * P:(seg // 2 + 1) * P],
                                   (wkc if seg == 1 else wk)[:, c, :], c == 0, c == C - 1)
                last.then_inc(e_k, 1)

            def hybrid_finish(b, j):
                if j == 0:
                    pe.wait_ge(e_oc, 8 * b + 8)
                for h in range(XH):
                    last = product(PS[:, 0, j * D:(j + 1) * D], eOT[:, h, j * P:(j + 1) * P], wo[:, h, :],
                                   h == 0, h == XH - 1)
                last.then_inc(e_y, 1)

            def hybrid(b, nxt):
                def raw_query(i):
                    j, g, u = i // XG, i % XG, 8 * b + i
                    pe.wait_ge(e_qr, u)
                    for c in range(C):
                        last = product(PS[:, 1, :], XT[:, c, j * P:(j + 1) * P], wq[:, c, 512 * g:512 * g + 512],
                                       c == 0, c == C - 1)
                    last.then_inc(e_q, 1)

                def query(i):
                    u = 8 * b + i
                    pe.wait_ge(e_qf, u + 1)
                    pe.wait_ge(e_qc, u)
                    for hh in range(GH):
                        last = pe.transpose(PS[:, 2, hh * P:(hh + 1) * P], eQA[:, hh * XD:(hh + 1) * XD], ident[:, :])
                    last.then_inc(e_qt, 1)

                def scores(i):
                    j, g, u = i // XG, i % XG, 8 * b + i
                    n = KEYS if j else P + T
                    pe.wait_ge(e_qc, u + 1)
                    for hh in range(GH):
                        if GH * i + hh >= 2:
                            pe.wait_ge(e_mx, GH * u + hh - 1)
                        product(PS[:, 3 + hh % 2, 0:n], eQT[:, hh * P:(hh + 1) * P], eKT[:, g, 0:n]).then_inc(e_s, 1)

                def turn(i):
                    j, u = i // XG, 8 * b + i
                    pe.wait_ge(e_p, u + 1)
                    pe.wait_ge(e_pta, u)
                    pe.wait_ge(e_ptd, u)
                    for hh in range(GH):
                        for k, (at, n) in enumerate(((0, P), (P, T), (P + T, P))[0:2 + j]):
                            last = pe.transpose(PS[0:n, 5 + k, hh * P:(hh + 1) * P], eP[:, hh, at:at + n], ident[:, :])
                    last.then_inc(e_t, 1)

                def outputs(i):
                    j, g, u = i // XG, i % XG, 8 * b + i
                    pe.wait_ge(e_pta, u + 1)
                    pe.wait_ge(e_ptd, u + 1)
                    pe.wait_ge(e_oc, u)
                    if i == 0:
                        pe.wait_ge(s_x, HYBRID * B + b)
                    for k, n in enumerate((P, T, P)[0:2 + j]):
                        last = product(PS[:, 0, :], eV[0:n, k, g * XD:(g + 1) * XD], ePT[0:n, k, :], k == 0, k == 1 + j)
                    last.then_inc(e_pv, 1)

                pe.wait_ge(e_kr, 3 * b + 3)
                raw_query(0)
                pe.wait_ge(e_pta, 8 * b)
                pe.wait_ge(e_ptd, 8 * b)
                for seg in range(3):
                    n = T if seg == 1 else P
                    for c in range(C):
                        last = product(PS[0:n, 5 + seg, :], eCT[:, c, :] if seg == 1 else
                                       XT[:, c, (seg // 2) * P:(seg // 2 + 1) * P],
                                       (wvc if seg == 1 else wv)[:, c, :], c == 0, c == C - 1)
                    last.then_inc(e_v, 1)
                former = type(b) is not int or b > 0
                if former:
                    hybrid_finish(b - 1, 0)
                for seg in range(3):
                    n = T if seg == 1 else P
                    if seg == 1:
                        held(pe, e_ka, 3 * b + 2)
                    else:
                        pe.wait_ge(e_kf, 2 * b + 1 + seg // 2)
                    for g in range(XG):
                        last = pe.transpose(PS[:, 2 + seg, g * n:(g + 1) * n],
                                            eKF[0:n, seg, g * XD:(g + 1) * XD], ident[0:n, 0:n])
                    last.then_inc(e_kt, 1)
                pe.wait_ge(e_kc, 3 * b + 3)
                query(0)
                raw_query(1)
                if former:
                    hybrid_finish(b - 1, 1)
                scores(0)
                for i in range(8):
                    if i + 1 < 8:
                        query(i + 1)
                    if i + 2 < 8:
                        raw_query(i + 2)
                    if i == 6:
                        pe.wait_ge(e_qr, 8 * b + 8)
                        xt_turn(*nxt, 1)
                    if i == 0:
                        pe.wait_ge(e_vr, 3 * b + 3)
                    if i >= 1:
                        outputs(i - 1)
                    if nxt[0] == HYBRID and i >= 6:
                        raw_keys(nxt[1], i - 6)
                    if i + 1 < 8:
                        scores(i + 1)
                    turn(i)
                if nxt[0] == HYBRID:
                    raw_keys(nxt[1], 2)
                outputs(7)

            pe.wait_ge(s_x, HYBRID * B)
            for seg in range(3):
                raw_keys(0, seg)
            over_batches(pe, HYBRID, hybrid)
            for j in range(J):
                hybrid_finish(B - 1, j)

            def moe(b, nxt):
                pe.wait_ge(s_xt, MOE * B + b + 1)
                pe.wait_ge(s_x, MOE * B + b)
                for j in range(J):
                    for c in range(C):
                        last = product(PS[:, 7, j * NE:(j + 1) * NE], XT[:, c, j * P:(j + 1) * P], rwT[:, c, :],
                                       c == 0, c == C - 1)
                last.then_inc(f_l, 1)
                pe.wait_ge(f_xl, b + 1)
                for j in range(J):
                    for m in range(NE // 2):
                        n = j * (NE // 2) + m
                        if n >= 6:
                            pe.wait_ge(f_acc, J * NE * b + 2 * (n - 5))
                        for k, part in enumerate((fXH, fXM, fXL)):
                            for c in range(C):
                                last = product(PS[:, 1 + n % 6, :].rearrange("p (e d) -> p e d", e=2),
                                               part[:, c, j * P:(j + 1) * P],
                                               EW[:, 2 * m:2 * m + 2, c * D:(c + 1) * D],
                                               k == 0 and c == 0, k == 2 and c == C - 1)
                        last.then_inc(f_y, 1)
                if nxt[0] == MOE:
                    xt_turn(*nxt)

            pe.wait_ge(s_mfree, NE)
            over_batches(pe, MOE, moe)


def kernel(**inputs):
    import concourse.bacc as bacc
    from concourse.bass_utils import run_bass_kernel_spmd

    f = {k: np.asarray(v) for k, v in inputs.items()}
    row = lambda a: np.ascontiguousarray(a.reshape(-1))
    swap = lambda a: np.concatenate([a[XD // 2:], a[:XD // 2]])
    w_in = f["L1_attn_W_in"]
    pos = np.arange(S, dtype=np.float32)
    inv = (1.0 / 10000.0 ** (np.arange(0, XD, 2, dtype=np.float32) / np.float32(XD))).astype(np.float32)
    ang = np.outer(pos, inv).astype(np.float32)
    cos, sin = np.cos(ang), np.sin(ang)
    tri = np.where(np.arange(S)[None, :] > np.arange(S)[:, None], NEG, 0.0).astype(np.float32)
    kmask = np.concatenate([tri[:, :P], np.zeros((S, T), np.float32), tri[:, P:]], axis=1)
    tiled = lambda a: np.ascontiguousarray(a.reshape(J, P, -1).transpose(1, 0, 2))
    masksT = f["L1_ffn_expert_masks"].transpose(0, 2, 1).reshape(NE, C, P, D).transpose(0, 2, 1, 3)
    arrays = {
        "x": f["x"],
        "ctx": f["ctx_2048"],
        "ctxT": f["ctx_2048"].transpose(2, 0, 1),
        "mask": f["mask_BxS2_bk0"],
        "wbrT": f["L0_attn_W_b_rank"].T, "wbs": f["L0_attn_W_b_state"],
        "wcrT": f["L0_attn_W_c_rank"].T, "wcm": f["L0_attn_W_c_model"],
        "factors": row(f["L0_attn_A_factors"]), "dvec": f["L0_attn_D_vec"].reshape(C, P).T,
        "gateT": f["L0_ffn_gate_w"].T, "valT": f["L0_ffn_val_w"].T, "outT": f["L0_ffn_out_w"].T,
        "gate_b": f["L0_ffn_gate_b"], "val_b": f["L0_ffn_val_b"], "ffo_b": f["L0_ffn_out_b"],
        "w_in": w_in, "w_out": f["L1_attn_W_out"],
        "bqk": f["L1_attn_b_in"][:2 * D].reshape(4, P).T, "b_v": f["L1_attn_b_in"][2 * D:], "b_o": f["L1_attn_b_out"],
        "wq": f["L1_xattn_wq"], "wk": f["L1_xattn_wk"], "wv": f["L1_xattn_wv"],
        "wkc": f["L1_xattn_wk_ctx"], "wvc": f["L1_xattn_wv_ctx"], "wo": f["L1_xattn_wo"],
        "qw": f["L1_xattn_q_norm_w"], "qws": swap(f["L1_xattn_q_norm_w"]),
        "kw": f["L1_xattn_k_norm_w"], "kws": swap(f["L1_xattn_k_norm_w"]),
        "ewT": f["L1_ffn_weight"].T, "rwT": f["L1_ffn_router_w"].T, "esc": f["L1_ffn_scale"],
        "masksT": masksT.reshape(NE, P, C * D),
        "ident": np.eye(P, dtype=np.float32),
        "hmask": np.repeat(np.eye(P // DH, dtype=np.float32), DH, axis=0),
        "causal": tiled(tri), "kmask": tiled(kmask),
        "cos": np.concatenate([cos, cos], 1), "sin": np.concatenate([-sin, sin], 1),
        "iota": np.arange(NE, dtype=np.float32),
    }
    arrays = {f"in_{k}_dram": np.ascontiguousarray(v) for k, v in arrays.items()}
    nc = bacc.Bacc("TRN2", target_bir_lowering=False, num_devices=1)
    aps = {k[3:-5]: nc.dram_tensor(k, a.shape, mybir.dt.from_np(a.dtype), kind="ExternalInput").ap()
           for k, a in arrays.items()}
    out = nc.dram_tensor("out_dram", (B, S, D), mybir.dt.float32, kind="ExternalOutput").ap()
    decoder_kernel(nc, aps, out)
    return run_bass_kernel_spmd(nc, [arrays], core_ids=[0]).results[0]["out_dram"]
```

```python
import numpy as np
import concourse.bass as bass
from concourse import mybir
from contextlib import ExitStack

B, S, D = 8, 256, 256
P = 128
J, C = S // P, D // P
T = 64
R, NS = 64, 32
LV = 5
HID = 1024
HC = HID // P
NH, DH = 16, 16
XH, XG, XD = 16, 4, 128
GH = XH // XG
KEYS = P + T + P
NE = 32
TOK = B * J
HT = P // 2
QT = 4
RING = 4
ROUNDS = 4
TILES = ROUNDS * RING * QT
assert TILES >= B * S // HT + NE - 1
LN_EPS, RMS_EPS = 1e-5, 1e-6
MAGIC = 12582912.0
NEG = -1e30
LOWEST = -3.0e38
MIX, CROSS, FFN, SELF, HYBRID, MOE = range(6)


def decoder_kernel(nc, I, out, rows, results):
    F32, BF, U8, U32 = mybir.dt.float32, mybir.dt.bfloat16, mybir.dt.uint8, mybir.dt.uint32
    ALU, ACT, AX = mybir.AluOpType, mybir.ActivationFunctionType, mybir.AxisListType
    ds = bass.ds

    with ExitStack() as ctx:
        def sb(name, shape, dt=F32):
            return ctx.enter_context(nc.sbuf_tensor(name, shape, dt))

        def sem(name):
            return ctx.enter_context(nc.semaphore(name))

        X = sb("X", [P, B, J, D])
        ident = sb("ident", [P, P])
        identb = sb("identb", [P, P], BF)
        ones = sb("ones", [P, P])
        halves = sb("halves", [P, 16])
        wbrT = sb("wbrT", [R, D])
        wcrT = sb("wcrT", [R, NS])
        wcm = sb("wcm", [R, D])
        fly = sb("fly", [R, 2, NS])
        factors = sb("factors", [R, LV * 4])
        dvec = sb("dvec", [P, C])
        b_fold = sb("b_fold", [NS, D])
        c_fold = sb("c_fold", [NS, D])
        early2 = sb("early2", [P, 4096])
        ctxT = sb("ctxT", [P, C, B, T])
        masku = sb("masku", [P, B, T], U8)
        mask = sb("mask", [P, B, T])
        valid = sb("valid", [P, B])
        early = sb("early", [P, 4096])
        ffo_b = sb("ffo_b", [P, D])
        wsum = sb("wsum", [P, 3])
        gam = sb("gam", [P, 3])
        rgam = sb("rgam", [P, 3])
        gam127 = sb("gam127", [P, 3])
        w_in = sb("w_in", [P, C, 3 * D])
        w_out = sb("w_out", [P, C, D])
        bqk = sb("bqk", [P, 4])
        b_v = sb("b_v", [P, D])
        b_o = sb("b_o", [P, D])
        hmask = sb("hmask", [P, P // DH])
        causal = sb("causal", [P, J, S])
        wq = sb("wq", [P, C, XH * XD])
        wk = sb("wk", [P, C, XG * XD])
        wv = sb("wv", [P, C, XG * XD])
        wkc = sb("wkc", [P, C, XG * XD])
        wvc = sb("wvc", [P, C, XG * XD])
        wo = sb("wo", [P, XH, D])
        cosT = sb("cosT", [P, J, XD])
        sinT = sb("sinT", [P, J, XD])
        qw = sb("qw", [P, XD])
        qws = sb("qws", [P, XD])
        kw = sb("kw", [P, XD])
        kws = sb("kws", [P, XD])
        cosq = sb("cosq", [P, J, XD])
        sinq = sb("sinq", [P, J, XD])
        cosk = sb("cosk", [P, J, XD])
        sink = sb("sink", [P, J, XD])
        kmask = sb("kmask", [P, J, KEYS])
        ew = sb("ew", [P, C, D])
        rwT = sb("rwT", [P, C, NE])
        iota = sb("iota", [P, TILES])
        esc = sb("esc", [P, D])
        EW = sb("EW", [P, NE, C * D], BF)
        st = sb("st", [P, J, 6])
        mv = sb("mv", [P, J, 2])
        ve = sb("ve", [P, J])
        rstd = sb("rstd", [P, J])
        XN = sb("XN", [P, J, D])
        XT = sb("XT", [P, C, S])
        magic = sb("magic", [P, 1])
        eCT = sb("eCT", [P, C, T])
        arena = sb("arena", [P, 8448])
        small = sb("small", [P, 512])

        def cut(at, shape, dt=F32, src=arena):
            n = 1
            for s in shape:
                n *= s
            words = n if dt == F32 else n // 2
            v = src[:, at:at + words]
            if dt != F32:
                v = v.bitcast(dt)
            if len(shape) > 1:
                names = "abcd"[:len(shape)]
                v = v.rearrange(f"p ({' '.join(names)}) -> p {' '.join(names)}",
                                **dict(zip(names[1:], shape[1:])))
            return v

        PS = ctx.enter_context(nc.psum_tensor("PS", [P, 8, 512], F32))

        def bank(n, k=1):
            return PS[:, n:n + k, :].rearrange("p b n -> p (b n)")

        pXT = bank(0)

        s_lx, s_lc, s_l0, s_l1, s_l2, s_l3, s_l4, s_l5 = (
            sem(n) for n in ("s_lx", "s_lc", "s_l0", "s_l1", "s_l2", "s_l3", "s_l4", "s_l5"))
        s_lg, s_lv, s_lo = sem("s_lg"), sem("s_lv"), sem("s_lo")
        s_mld = [sem(f"s_mld{i}") for i in range(4)]
        s_mfree = sem("s_mfree")
        s_ew = sem("s_ew")
        s_out = sem("s_out")
        s_held = sem("s_held")
        s_x = sem("s_x")
        s_bn, s_mv, s_ve, s_rs = sem("s_bn"), sem("s_mv"), sem("s_ve"), sem("s_rs")
        s_xn = sem("s_xn")
        s_xtp = sem("s_xtp")
        s_xt = sem("s_xt")
        s_c = sem("s_c")
        s_pc = sem("s_pc")
        s_pp = sem("s_pp")
        s_ps = sem("s_ps")

        a_mm, = (sem("a_mm"),)
        b_s, b_c, b_m, b_e, b_r, b_v2, b_p, b_t, b_tc, b_o2 = (
            sem(n) for n in ("b_s", "b_c", "b_m", "b_e", "b_r", "b_v2", "b_p", "b_t", "b_tc", "b_o2"))
        d_vv = sem("d_vv")
        c_xq = sem("c_xq")
        c_q = [sem(f"c_q{i}") for i in range(5)]
        c_g, c_v, c_gs, c_si, c_vs, c_h, c_a = (
            sem(n) for n in ("c_g", "c_v", "c_gs", "c_si", "c_vs", "c_h", "c_a"))
        c_s = [sem(f"c_s{i}") for i in range(4)]
        c_hr, c_hq, c_t, c_ht, c_o, c_y = (
            sem(n) for n in ("c_hr", "c_hq", "c_t", "c_ht", "c_o", "c_y"))
        d_pq, d_q, d_kv, d_s, d_mx, d_nm, d_e, d_t, d_pt, d_pv, d_r, d_o, d_ot, d_oc, d_y, d_yb = (
            sem(n) for n in ("d_pq", "d_q", "d_kv", "d_s", "d_mx", "d_nm", "d_e", "d_t", "d_pt",
                             "d_pv", "d_r", "d_o", "d_ot", "d_oc", "d_y", "d_yb"))
        e_ct, e_k, e_v, e_vr = (sem(n) for n in ("e_ct", "e_k", "e_v", "e_vr"))
        e_kv, e_kr, e_sq, e_ssq, e_ve, e_rk, e_kn, e_ka, e_kb, e_kf, e_kt, e_kc = (
            sem(n) for n in ("e_kv", "e_kr", "e_sq", "e_ssq", "e_ve", "e_rk", "e_kn", "e_ka",
                             "e_kb", "e_kf", "e_kt", "e_kc"))
        e_q, e_qr, e_qs, e_qb, e_qa, e_qq, e_qv, e_rq, e_qf, e_qt, e_qc, e_s, e_mx, e_nm, e_e, e_ri, \
            e_p, e_t, e_pta, e_ptd, e_pv, e_oc, e_y = (
                sem(n) for n in ("e_q", "e_qr", "e_qs", "e_qb", "e_qa", "e_qq", "e_qv", "e_rq",
                                 "e_qf", "e_qt", "e_qc", "e_s", "e_mx", "e_nm", "e_e", "e_ri", "e_p",
                                 "e_t", "e_pta", "e_ptd", "e_pv", "e_oc", "e_y"))
        f_l, f_lg, f_m, f_i, f_if, f_oh, f_nm, f_e, f_row = (
            sem(n) for n in ("f_l", "f_lg", "f_m", "f_i", "f_if", "f_oh", "f_nm", "f_e", "f_row"))
        f_count, f_rank, f_base, f_tex = (sem(n) for n in ("f_count", "f_rank", "f_base", "f_tex"))
        f_tp, f_xh, f_r1, f_xm, f_xl, f_y, f_yo = (
            sem(n) for n in ("f_tp", "f_xh", "f_r1", "f_xm", "f_xl", "f_y", "f_yo"))
        s_zero = sem("s_zero")
        s_cleared = sem("s_cleared")
        s_sorted = sem("s_sorted")
        s_rows = [sem(f"s_rows{i}") for i in range(RING)]
        s_stored = [sem(f"s_stored{i}") for i in range(RING)]
        s_back = [sem(f"s_back{i}") for i in range(4)]

        block = ctx.enter_context(nc.Block())

        def bc(ap, shape):
            return ap.broadcast_to(shape)

        def held(eng, s, value):
            eng.wait_ge(s, value)
            eng.sem_inc(s_held, 1)

        def over_batches(eng, phase, body):
            body(0, (phase, 1))
            with eng.Fori(1, B - 1) as b:
                body(b, (phase, b + 1))
            body(B - 1, (phase + 1, 0))

        def over_rounds(eng, body):
            body(0)
            body(1)
            with eng.Fori(2, ROUNDS) as n:
                body(n)

        def after(eng, s, value):
            if type(value) is not int or value > 0:
                eng.wait_ge(s, value)

        ctxN = cut(0, (B, D), F32, early2)[0:T]; val_b = cut(2048, (HID,), F32, early2)
        mix = cut(3072, (C, D), F32, early2); mbias = cut(3584, (B, T), F32, early2)
        gateT = cut(0, (C, HID), BF, early); valT = cut(1024, (C, HID), BF, early)
        outT = cut(2048, (HC, D), BF, early); gate_b = cut(3072, (HID,), F32, early)
        wstage = cut(6400, (C, HID)); mring = cut(6400, (4, C * D))
        bSC = cut(5120, (J, T)); bP = cut(5248, (J, T)); bPT = cut(5376, (S,))
        b_nm = small[:, 0:2]; b_sum = small[:, 2:4]; b_ri = small[:, 4:6]; b_rv = small[:, 6:8]
        cXQ = cut(0, (J, D)); cXB = cut(512, (J, D), BF); cXT = cut(768, (C, S), BF)
        cHG = cut(1024, (HID,)); cHS = cHG; cHV = cut(2048, (HID,)); cH = cut(3072, (HID,))
        cHR = cut(4096, (HID,)); cHQ = cut(5120, (HID,), BF); cHT = cut(5632, (HC, P), BF); cY = cut(6144, (D,))
        c_gx = small[:, 8:10]; c_rx = small[:, 10:12]; c_sx = small[:, 12:14]
        c_new = small[:, 14:18]; c_cur = small[:, 18:22]
        c_hm = small[:, 22:23]; c_rh = small[:, 23:24]; c_sh = small[:, 24:25]; c_so = small[:, 25:26]
        dQ = cut(0, (2, S)); dK = cut(0, (NH, S), F32, early); dV = cut(512, (J, D))
        dSS = cut(1024, (2, 4, S)); dP = cut(3072, (2, 4, S)); dPT = cut(5120, (2, 8, P))
        dO = cut(7168, (J, D)); dOT = cut(7680, (C, S)); dY = dO
        d_max = small[:, 32:40].rearrange("p (a b) -> p a b", a=2)
        d_neg = small[:, 40:48].rearrange("p (a b) -> p a b", a=2)
        d_sum = small[:, 48:80]; d_ri = small[:, 80:112]
        eKR = cut(0, (3, 512), F32, early2); eKB = cut(1536, (2, 512), F32, early2)
        eKF = cut(2560, (3, 512), F32, early2); eSQ = eKF
        eP = cut(0, (2, GH, KEYS)); ePT = cut(2560, (3, 512))
        eKT = cut(4096, (XG, KEYS))
        eQR = cut(5376, (512,)); eQB = cut(5888, (512,)); eQS = cut(6400, (512,)); eQA = cut(6912, (512,))
        eQT = cut(7424, (512,))
        eV = w_in[:, :, :].rearrange("p c n -> p (c n)").rearrange("p (a n) -> p a n", a=3)
        eOT = cut(0, (XH, S), F32, early)
        e_ks = small[:, 112:124].rearrange("p (a b) -> p a b", a=3)
        e_kp = small[:, 124:136].rearrange("p (a b) -> p a b", a=3)
        e_rks = small[:, 136:148].rearrange("p (a b) -> p a b", a=3)
        e_q2 = small[:, 148:152]; e_q3 = small[:, 152:156]
        e_rqs = small[:, 156:164].rearrange("p (a b) -> p a b", a=2)
        e_max = small[:, 164:168]
        e_neg = small[:, 168:176].rearrange("p (a b) -> p a b", a=2)
        e_sum = small[:, 176:184].rearrange("p (a b) -> p a b", a=2)
        e_inv = small[:, 184:188]
        sIN = cut(0, (RING, 2, D))
        sXH = cut(2048, (RING, 2, C * P), BF); sXM = cut(3072, (RING, 2, C * P), BF)
        sXL = cut(4096, (RING, 2, C * P), BF); sR = cut(5120, (RING, 2 * C * P))
        fOH = cut(7168, (TOK, NE), BF); fSLOT = cut(0, (TOK, NE))
        before = cut(7424, (P,), BF); onesb = cut(7488, (P,), BF)
        lower = cut(7552, (NE,)); upto = cut(7584, (NE,)); tilesB = cut(7616, (P,)); past = cut(7744, (TILES,))
        fLG = cut(7808, (J, NE)); fE = cut(7872, (J, NE)); fBASE = cut(7936, (NE,))
        zeros = cut(8192, (D,))
        sY = cut(0, (RING, QT, D), F32, early)[0:HT]
        fROW = cut(0, (TOK, D), F32, early2)
        fBACK = cut(0, (TOK, D))
        f_m8 = small[:, 192:208].rearrange("p (a b) -> p a b", a=2)
        f_i8 = small[:, 208:224].bitcast(U32).rearrange("p (a b) -> p a b", a=2)
        f_if_ = small[:, 224:226]; f_neg = small[:, 226:228]
        f_sm = small[:, 232:248]; f_w = small[:, 248:264]
        f_slot = small[:, 264:280]; f_slotu = small[:, 280:296].bitcast(U32)
        f_tiles = small[0:NE, 296:297]; f_incl = small[0:NE, 297:298]
        f_ex = small[0:1, 304:304 + TILES]; f_exu = small[0:1, 368:368 + TILES].bitcast(U32)

        mark = {}

        @block.vector
        def _(dve):
            count = [0]

            def const(ins, name=None):
                count[0] += 1
                ins.then_inc(s_c, 1)
                dve.wait_ge(s_c, count[0])
                if name:
                    mark[name] = count[0]

            def ln_stats(phase, b):
                n = phase * B + b
                if phase == MIX:
                    dve.wait_ge(s_lx, 16)
                else:
                    dve.wait_ge(s_x, n - B + 1)
                for j in range(J):
                    last = dve.bn_stats(st[:, j, :], tokens(b, j))
                last.then_inc(s_bn, 1)
                held(dve, s_bn, n + 1)
                for j in range(J):
                    last = dve.bn_aggr(mv[:, j, :], st[:, j, :])
                last.then_inc(s_mv, 1)

            def tokens(b, j):
                return X[:, ds(b, 1), j, :].rearrange("p a d -> p (a d)")

            def batch(b):
                return X[:, ds(b, 1), :, :].rearrange("p a j d -> p (a j) d")

            def ln_apply(phase, b):
                n = phase * B + b
                dve.wait_ge(s_rs, n + 1)
                dve.wait_ge(s_xtp, n)
                for j in range(J):
                    last = dve.tensor_scalar(XN[:, j, :], tokens(b, j), mv[:, j, 0:1], rstd[:, j:j + 1],
                                             ALU.subtract, ALU.mult)
                if phase != FFN:
                    last.then_inc(s_xn, 1)
                    return
                last.then_inc(c_q[0], 1)
                dve.wait_ge(c_q[0], b + 1)
                dve.tensor_reduce(c_gx, XN[:, :, :], AX.X, ALU.max, apply_absolute_value=True).then_inc(c_q[1], 1)
                dve.wait_ge(c_q[1], b + 1)
                dve.tensor_scalar(c_gx, c_gx, 1e-5, None, ALU.max).then_inc(c_q[2], 1)
                dve.wait_ge(c_q[2], b + 1)
                dve.tensor_scalar(c_new[:, 0:2], c_gx, gam127[:, 0:1], None, ALU.mult)
                dve.tensor_scalar(c_new[:, 2:4], c_gx, gam127[:, 1:2], None, ALU.mult)
                dve.reciprocal(c_rx, c_gx).then_inc(c_q[3], 1)
                dve.wait_ge(c_q[3], b + 1)
                dve.tensor_scalar(c_sx, c_rx, 127.0, None, ALU.mult).then_inc(c_q[4], 1)
                dve.wait_ge(c_q[4], b + 1)
                for j in range(J):
                    last = dve.tensor_scalar(cXQ[:, j, :], XN[:, j, :], c_sx[:, j:j + 1], MAGIC, ALU.mult, ALU.add)
                last.then_inc(c_xq, 1)
                dve.wait_ge(c_xq, b + 1)
                dve.tensor_scalar(cXB, cXQ, MAGIC, None, ALU.subtract).then_inc(s_xn, 1)

            def ternary(dst, src, scale):
                const(dve.tensor_scalar(src, src, scale, MAGIC, ALU.mult, ALU.add))
                const(dve.tensor_scalar(src, src, MAGIC, -1.0, ALU.subtract, ALU.max))
                const(dve.tensor_scalar(dst, src, 1.0, None, ALU.min))

            dve.wait_ge(s_l0, 16 * 7)
            const(dve.tensor_copy(identb[:, :], ident[:, :]), "identb")
            for lv in range(LV):
                v = [fly[:, k, :].rearrange("r (a i c) -> r a i c", i=2, c=2 ** (LV - 1 - lv))
                     for k in (lv % 2, (lv + 1) % 2)]
                for o in range(2):
                    f = 4 * lv + o
                    const(dve.tensor_scalar(v[1][:, :, o, :], v[0][:, :, 0, :], factors[:, f:f + 1], None, ALU.mult))
                    const(dve.scalar_tensor_tensor(v[1][:, :, o, :], v[0][:, :, 1, :], factors[:, f + 2:f + 3],
                                                   v[1][:, :, o, :], ALU.mult, ALU.add), "fly")
            dve.wait_ge(s_pp, 1)
            const(dve.tensor_copy(b_fold[:, :], PS[0:NS, 1, 0:D]))
            const(dve.tensor_copy(c_fold[:, :], PS[0:NS, 2, 0:D]), "folds")
            ln_stats(MIX, 0)
            ln_apply(MIX, 0)
            dve.wait_ge(s_pp, 2)
            for c in range(C):
                const(dve.tensor_copy(mix[:, c, :], PS[:, 3 + c, 0:D]))
                const(dve.scalar_tensor_tensor(mix[:, c, c * P:(c + 1) * P], ident[:, :], dvec[:, c:c + 1],
                                               PS[:, 3 + c, c * P:(c + 1) * P], ALU.mult, ALU.add), "mix")
            dve.wait_ge(s_l1, 48)
            const(dve.tensor_copy(mask[:, :, :], masku[:, :, :]))
            const(dve.tensor_scalar(mbias[:, :, :], mask[:, :, :], 1.0, -NEG, ALU.subtract, ALU.mult))
            const(dve.tensor_reduce(valid[:, :], mask[:, :, :], AX.X, ALU.max))

            def mixer(b, nxt):
                ln_stats(*nxt)
                dve.wait_ge(a_mm, b + 1)
                dve.tensor_tensor(batch(b), batch(b), bank(1).rearrange("p (j d) -> p j d", j=J), ALU.add)\
                    .then_inc(s_x, 1)
                ln_apply(*nxt)

            over_batches(dve, MIX, mixer)

            def cross(b, nxt):
                dve.wait_ge(b_s, b + 1)
                dve.scalar_tensor_tensor(bSC, PS[:, 1, 0:J * T].rearrange("p (j t) -> p j t", j=J),
                                         1.0 / 16, bc(mbias[:, ds(b, 1), :], [P, J, T]),
                                         ALU.mult, ALU.add).then_inc(b_c, 1)
                dve.wait_ge(b_c, b + 1)
                dve.tensor_reduce(b_nm, bSC, AX.X, ALU.max, negate=True).then_inc(b_m, 1)
                ln_stats(*nxt)
                dve.wait_ge(b_e, b + 1)
                dve.reciprocal(b_ri, b_sum).then_inc(b_r, 1)
                dve.wait_ge(b_r, b + 1)
                dve.tensor_tensor(b_rv, b_ri, bc(valid[:, ds(b, 1)], [P, J]), ALU.mult).then_inc(b_v2, 1)
                dve.wait_ge(b_v2, b + 1)
                dve.tensor_tensor(bP, bP, bc(b_rv.unsqueeze(2), [P, J, T]), ALU.mult).then_inc(b_p, 1)
                ln_apply(*nxt)
                dve.wait_ge(b_o2, b + 1)
                dve.tensor_tensor(batch(b), batch(b), bank(3).rearrange("p (j d) -> p j d", j=J), ALU.add)\
                    .then_inc(s_x, 1)

            stage = wstage[:, :, :].rearrange("p c n -> p (c n)")
            for k, (dst, s) in enumerate(((gateT, s_lg), (valT, s_lv), (outT, s_lo))):
                dve.wait_ge(s, 16)
                const(dve.tensor_reduce(wsum[:, k:k + 1], stage, AX.X, ALU.add, apply_absolute_value=True), f"wsum{k}")
                dve.wait_ge(s_ps, k + 1)
                const(dve.tensor_scalar(gam[:, k:k + 1], PS[:, 7, k:k + 1], 1.0 / (D * HID), 1e-5, ALU.mult, ALU.max))
                const(dve.reciprocal(rgam[:, k:k + 1], gam[:, k:k + 1]))
                const(dve.tensor_scalar(gam127[:, k:k + 1], gam[:, k:k + 1], 1.0 / 127, None, ALU.mult))
                const(dve.tensor_scalar(stage, stage, rgam[:, k:k + 1], MAGIC, ALU.mult, ALU.add))
                const(dve.tensor_scalar(stage, stage, MAGIC, -1.0, ALU.subtract, ALU.max))
                ins = dve.tensor_scalar(dst[:, :, :].rearrange("p a b -> p (a b)"), stage, 1.0, None, ALU.min)
                count[0] += 1
                ins.then_inc(s_c, 1)
                dve.wait_ge(s_c, count[0])
                mark[f"w{k}"] = count[0]
            dve.wait_ge(s_l5, 64)
            ternary(ew[:, :, :], ew[:, :, :], 2.0)
            mark["ew"] = count[0]
            dve.wait_ge(s_l4, 16 * 13)
            const(dve.tensor_scalar(kw[:, :], kw[:, :], float(XD) ** 0.5, None, ALU.mult))
            const(dve.tensor_scalar(kws[:, :], kws[:, :], float(XD) ** 0.5, None, ALU.mult))
            for dst, tab, w in ((cosq, cosT, qw), (sinq, sinT, qws), (cosk, cosT, kw), (sink, sinT, kws)):
                const(dve.tensor_tensor(dst[:, :, :], tab[:, :, :], bc(w[:, :].unsqueeze(1), [P, J, XD]), ALU.mult),
                      "tables")

            over_batches(dve, CROSS, cross)

            dve.wait_ge(s_l2, 48)

            def ffn(b, nxt):
                dve.tensor_copy(c_cur, c_new).then_inc(c_s[0], 1)
                dve.wait_ge(c_s[0], b + 1)
                for j in range(J):
                    u = J * b + j
                    dve.wait_ge(c_g, u + 1)
                    dve.scalar_tensor_tensor(cHG, bank(1, 2), c_cur[:, j:j + 1], gate_b, ALU.mult, ALU.add)\
                        .then_inc(c_gs, 1)
                    dve.wait_ge(c_v, u + 1)
                    dve.scalar_tensor_tensor(cHV, bank(3, 2), c_cur[:, 2 + j:3 + j], val_b, ALU.mult, ALU.add)\
                        .then_inc(c_vs, 1)
                    if j == 0:
                        ln_stats(*nxt)
                    dve.wait_ge(c_vs, u + 1)
                    dve.wait_ge(c_si, u + 1)
                    dve.tensor_tensor(cH, cHS, cHV, ALU.mult).then_inc(c_h, 1)
                    dve.wait_ge(c_h, u + 1)
                    dve.tensor_reduce(c_hm, cH, AX.X, ALU.max, apply_absolute_value=True).then_inc(c_a, 1)
                    dve.wait_ge(c_a, u + 1)
                    dve.tensor_scalar(c_hm, c_hm, 1e-5, None, ALU.max).then_inc(c_s[1], 1)
                    dve.wait_ge(c_s[1], u + 1)
                    dve.tensor_scalar(c_so, c_hm, gam127[:, 2:3], None, ALU.mult)
                    dve.reciprocal(c_rh, c_hm).then_inc(c_s[2], 1)
                    dve.wait_ge(c_s[2], u + 1)
                    dve.tensor_scalar(c_sh, c_rh, 127.0, None, ALU.mult).then_inc(c_s[3], 1)
                    if j == 0:
                        ln_apply(*nxt)
                    dve.wait_ge(c_hr, u + 1)
                    dve.tensor_scalar(cHQ, cHR, MAGIC, None, ALU.subtract).then_inc(c_hq, 1)
                    dve.wait_ge(c_o, u + 1)
                    dve.scalar_tensor_tensor(cY, PS[:, 6, 0:D], c_so, ffo_b[:, :], ALU.mult, ALU.add)\
                        .then_inc(c_y, 1)
                    dve.wait_ge(c_y, u + 1)
                    last = dve.tensor_tensor(tokens(b, j), tokens(b, j), cY, ALU.add)
                last.then_inc(s_x, 1)

            over_batches(dve, FFN, ffn)

            dve.wait_ge(s_l3, 16 * 7)

            def self_keys(b):
                dve.wait_ge(d_pq, b + 1)
                for h in range(NH):
                    m = h // (P // DH)
                    k = h % (P // DH)
                    last = dve.tensor_scalar(dK[:, h, :], PS[:, 5, m * S:(m + 1) * S], bqk[:, 2 + m:3 + m],
                                             hmask[:, k:k + 1], ALU.add, ALU.mult)
                    if h % 4 == 3:
                        last.then_inc(d_kv, 1)
                dve.wait_ge(d_pv, 8 * b)
                dve.tensor_tensor(dV, bank(6).rearrange("p (j d) -> p j d", j=J),
                                  bc(b_v[:, :].unsqueeze(1), [P, J, D]), ALU.add).then_inc(d_vv, 1)

            def self_finish(b):
                dve.wait_ge(d_y, b + 1)
                dve.tensor_tensor(dY, bank(2).rearrange("p (j d) -> p j d", j=J),
                                  bc(b_o[:, :].unsqueeze(1), [P, J, D]), ALU.add).then_inc(d_yb, 1)
                dve.wait_ge(d_yb, b + 1)
                dve.tensor_tensor(batch(b), batch(b), dY, ALU.add).then_inc(s_x, 1)

            def self_attention(b, nxt):
                def masked_max(i):
                    j, u = i // 4, 8 * b + i
                    n = (j + 1) * P
                    if i >= 2:
                        dve.wait_ge(d_e, u - 1)
                    held(dve, d_s, u + 1)
                    for hh in range(4):
                        last = dve.tensor_tensor_reduce(
                            dSS[:, i % 2, hh, 0:n], PS[:, 4 + 2 * (i % 2) + hh // 2, (hh % 2) * S:(hh % 2) * S + n],
                            causal[:, j, 0:n], 1.0, LOWEST, ALU.add, ALU.max, d_max[:, i % 2, hh:hh + 1])
                    last.then_inc(d_mx, 1)
                    dve.wait_ge(d_mx, u + 1)
                    dve.tensor_scalar(d_neg[:, i % 2, :], d_max[:, i % 2, :], -0.25, None, ALU.mult).then_inc(d_nm, 1)

                def turn(i):
                    u = 8 * b + i
                    if i % 2:
                        dve.wait_ge(d_t, u + 1)
                        dve.wait_ge(d_pv, u - 1)
                        n = 4 * (1 + i // 4) * P
                        dve.tensor_copy(dPT[:, i % 2, :, :].rearrange("p a b -> p (a b)")[:, 0:n],
                                        bank(1, 2)[:, 0:n]).then_inc(d_pt, 1)

                masked_max(0)
                masked_max(1)
                if type(b) is not int or b > 0:
                    self_finish(b - 1)
                for i in range(8):
                    if i + 2 < 8:
                        masked_max(i + 2)
                    turn(i)
                    if i == 2:
                        ln_stats(*nxt)
                    if i == 4:
                        ln_apply(*nxt)
                if nxt[0] == SELF:
                    self_keys(nxt[1])
                dve.wait_ge(d_e, 8 * b + 8)
                dve.reciprocal(d_ri, d_sum).then_inc(d_r, 1)
                dve.wait_ge(d_r, b + 1)
                dve.wait_ge(d_pv, 8 * b + 8)
                dve.tensor_tensor(dO.rearrange("p j (h k) -> p (j h) k", k=DH),
                                  bank(3).rearrange("p (h k) -> p h k", k=DH),
                                  bc(d_ri.unsqueeze(2), [P, J * NH, DH]), ALU.mult).then_inc(d_o, 1)

            self_keys(0)
            over_batches(dve, SELF, self_attention)
            self_finish(B - 1)

            def turn_keys(b):
                for seg in range(3):
                    n = T if seg == 1 else P
                    dve.wait_ge(e_sq, 3 * b + seg + 1)
                    dve.tensor_reduce(e_ks[0:n, seg, :], eSQ[0:n, seg, :].rearrange("p (g d) -> p g d", g=XG),
                                      AX.X, ALU.add).then_inc(e_ssq, 1)
                for seg in range(3):
                    n = T if seg == 1 else P
                    dve.wait_ge(e_rk, 3 * b + seg + 1)
                    kr = eKR[0:n, seg, :].rearrange("p (g d) -> p g d", g=XG)
                    dve.tensor_tensor(kr, kr, bc(e_rks[0:n, seg, :].unsqueeze(2), [n, XG, XD]), ALU.mult)\
                        .then_inc(e_kn, 1)
                for seg in range(3):
                    n = T if seg == 1 else P
                    dve.wait_ge(e_kn, 3 * b + seg + 1)
                    kr = eKR[0:n, seg, :].rearrange("p (g d) -> p g d", g=XG)
                    kf = eKF[0:n, seg, :].rearrange("p (g d) -> p g d", g=XG)
                    tab = kw[0:n, :].unsqueeze(1) if seg == 1 else cosk[:, seg // 2, :].unsqueeze(1)
                    dve.tensor_tensor(kf, kr, bc(tab, [n, XG, XD]), ALU.mult).then_inc(e_ka, 1)
                for k, seg in enumerate((0, 2)):
                    dve.wait_ge(e_ka, 3 * b + seg + 1)
                    dve.wait_ge(e_kb, 2 * b + k + 1)
                    dve.tensor_tensor(eKF[:, seg, :], eKF[:, seg, :], eKB[:, k, :], ALU.add).then_inc(e_kf, 1)

            def hybrid_finish(b):
                dve.wait_ge(e_y, J * b + J)
                dve.tensor_tensor(batch(b), batch(b), bank(0).rearrange("p (j d) -> p j d", j=J), ALU.add)\
                    .then_inc(s_x, 1)

            def hybrid(b, nxt):
                def scale_query(i):
                    j, u = i // XG, 8 * b + i
                    dve.wait_ge(e_qt, u)
                    dve.wait_ge(e_qr, u + 1)
                    dve.tensor_tensor(eQA.rearrange("p (g d) -> p g d", g=GH),
                                      eQR.rearrange("p (g d) -> p g d", g=GH),
                                      bc(cosq[:, j, :].unsqueeze(1), [P, GH, XD]), ALU.mult).then_inc(e_qa, 1)

                def sum_squares(i):
                    u = 8 * b + i
                    dve.wait_ge(e_qs, u + 1)
                    dve.tensor_reduce(e_q2, eQS.rearrange("p (g d) -> p g d", g=GH), AX.X, ALU.add)\
                        .then_inc(e_qq, 1)

                def turn_query(i):
                    u = 8 * b + i
                    dve.wait_ge(e_qa, u + 1)
                    dve.wait_ge(e_qb, u + 1)
                    dve.tensor_tensor(eQA, eQA, eQB, ALU.add).then_inc(e_qf, 1)

                def masked_max(i):
                    j, u = i // XG, 8 * b + i
                    n = KEYS if j else P + T
                    after(dve, e_t, u - 1)
                    for hh in range(GH):
                        held(dve, e_s, GH * u + hh + 1)
                        dve.tensor_tensor_reduce(eP[:, i % 2, hh, 0:n], PS[:, 3 + hh % 2, 0:n], kmask[:, j, 0:n],
                                                 1.0, LOWEST, ALU.add, ALU.max, e_max[:, hh:hh + 1]).then_inc(e_mx, 1)
                    dve.wait_ge(e_mx, GH * (u + 1))
                    dve.wait_ge(e_rq, u + 1)
                    dve.scalar_tensor_tensor(e_neg[:, i % 2, :], e_max, -1.0, e_rqs[:, i % 2, :], ALU.mult, ALU.mult)\
                        .then_inc(e_nm, 1)

                def normalise(i):
                    j, u = i // XG, 8 * b + i
                    n = KEYS if j else P + T
                    dve.wait_ge(e_e, u + 1)
                    dve.reciprocal(e_inv, e_sum[:, i % 2, :]).then_inc(e_ri, 1)
                    dve.wait_ge(e_ri, u + 1)
                    for hh in range(GH):
                        last = dve.tensor_scalar(eP[:, i % 2, hh, 0:n], eP[:, i % 2, hh, 0:n], e_inv[:, hh:hh + 1], None, ALU.mult)
                    last.then_inc(e_p, 1)

                def turn_probs(i):
                    u = 8 * b + i
                    dve.wait_ge(e_t, u + 1)
                    dve.wait_ge(e_pv, u)
                    last = dve.tensor_copy(ePT[0:T, 1, :], PS[0:T, 6, :])
                    if i >= XG:
                        last = dve.tensor_copy(ePT[:, 2, :], PS[:, 7, :])
                    last.then_inc(e_ptd, 1)

                for i in range(2):
                    scale_query(i)
                    turn_query(i)
                    sum_squares(i)
                if type(b) is not int or b > 0:
                    hybrid_finish(b - 1)
                masked_max(0)
                for i in range(8):
                    if i >= 1:
                        turn_probs(i - 1)
                    normalise(i)
                    if i + 2 < 8:
                        scale_query(i + 2)
                    if i + 1 < 8:
                        masked_max(i + 1)
                    if i + 2 < 8:
                        turn_query(i + 2)
                        sum_squares(i + 2)
                    if i == 3:
                        ln_stats(*nxt)
                    if i == 5:
                        ln_apply(*nxt)
                turn_probs(7)
                if nxt[0] == HYBRID:
                    turn_keys(nxt[1])

            turn_keys(0)
            over_batches(dve, HYBRID, hybrid)
            hybrid_finish(B - 1)

            dve.wait_ge(s_x, MOE * B)
            dve.wait_ge(s_cleared, 16)
            const(dve.tensor_scalar(before, causal[:, 0, 0:P], 0.0, None, ALU.is_lt))
            const(dve.tensor_copy(onesb, ones[:, :]))
            const(dve.tensor_scalar(lower[0:NE, :], causal[0:NE, 0, 0:NE], 0.0, None, ALU.is_lt))
            const(dve.tensor_tensor(upto[0:NE, :], lower[0:NE, :], ident[0:NE, 0:NE], ALU.add), "routing")

            def route(b, nxt):
                if nxt[0] == MOE:
                    ln_stats(*nxt)
                dve.wait_ge(f_e, b)
                dve.wait_ge(f_l, b + 1)
                dve.tensor_copy(fLG, PS[:, 7, 0:J * NE].rearrange("p (j e) -> p j e", j=J)).then_inc(f_lg, 1)
                held(dve, f_lg, b + 1)
                for j in range(J):
                    last = dve.max(f_m8[:, j, :], fLG[:, j, :])
                last.then_inc(f_m, 1)
                dve.wait_ge(f_m, b + 1)
                dve.tensor_scalar(f_neg, f_m8[:, :, 0], -1.0, None, ALU.mult).then_inc(f_nm, 1)
                for j in range(J):
                    last = dve.max_index(f_i8[:, j, :], f_m8[:, j, :], fLG[:, j, :])
                last.then_inc(f_i, 1)
                if nxt[0] == MOE:
                    dve.wait_ge(f_row, b + 1)
                    ln_apply(*nxt)
                dve.wait_ge(f_i, b + 1)
                dve.tensor_copy(f_if_, f_i8[:, :, 0]).then_inc(f_if, 1)
                dve.wait_ge(f_if, b + 1)
                for j in range(J):
                    last = dve.tensor_scalar(fOH[:, ds(J * b + j, 1), :].rearrange("p a e -> p (a e)"),
                                             iota[:, 0:NE], f_if_[:, j:j + 1], None, ALU.is_equal)
                last.then_inc(f_oh, 1)

            over_batches(dve, MOE, route)

            dve.wait_ge(f_count, 1)
            const(dve.tensor_scalar(f_tiles, PS[0:NE, 2, 0:1], 1.0 / HT, 0.5 - 0.5 / HT, ALU.mult, ALU.add))
            const(dve.tensor_scalar(f_tiles, f_tiles, MAGIC, None, ALU.add))
            const(dve.tensor_scalar(f_tiles, f_tiles, MAGIC, None, ALU.subtract))
            const(dve.tensor_scalar(tilesB[0:NE, :], ones[0:NE, :], f_tiles, None, ALU.mult), "tiles")
            dve.wait_ge(f_base, 1)
            const(dve.tensor_copy(f_incl, PS[0:NE, 4, 0:1]))
            const(dve.tensor_scalar(past[0:NE, :], iota[0:NE, :], f_incl, None, ALU.is_ge), "past")
            const(dve.tensor_scalar(fBASE, PS[:, 3, 0:NE], float(HT), None, ALU.mult))
            dve.wait_ge(f_rank, 1)
            const(dve.tensor_tensor(fSLOT, PS[:, 1, :].rearrange("p (i e) -> p i e", e=NE),
                                    bc(fBASE.unsqueeze(1), [P, TOK, NE]), ALU.add))
            const(dve.tensor_tensor(fSLOT, fSLOT, fOH, ALU.mult))
            const(dve.tensor_reduce(f_slot, fSLOT, AX.X, ALU.add))
            const(dve.tensor_copy(f_slotu, f_slot), "slots")
            dve.wait_ge(f_tex, 1)
            const(dve.tensor_scalar(f_ex, PS[0:1, 5, 0:TILES], float(NE - 1), None, ALU.min))
            const(dve.tensor_copy(f_exu, f_ex), "experts")
            dve.wait_ge(f_e, B)
            const(dve.reciprocal(f_w, f_sm))

            def remainder(k, u):
                dve.wait_ge(f_xh, u + 1)
                after(dve, f_xl, u - RING + 1)
                dve.tensor_tensor(sR[:, k, :], bank(k), sXH[:, k].rearrange("p t n -> p (t n)"), ALU.subtract) \
                    .then_inc(f_r1, 1)

            def scale(k, n, u):
                after(dve, s_stored[k], 16 * n)
                dve.wait_ge(f_y, u + 1)
                dve.tensor_tensor(sY[:, k], bank(4 + 2 * (k % 2), 2)[0:HT, :].rearrange("p (t d) -> p t d", t=QT),
                                  bc(esc[0:HT, :].unsqueeze(1), [HT, QT, D]), ALU.mult).then_inc(f_yo, 1)

            def experts(n):
                for k in range(RING):
                    u = RING * n + k
                    remainder(k, u)
                    if k >= 3:
                        scale(k - 3, n, u - 3)
                    elif type(n) is not int or n > 0:
                        scale(k + 1, n - 1, u - 3)

            over_rounds(dve, experts)
            for k in range(1, RING):
                scale(k, ROUNDS - 1, RING * (ROUNDS - 1) + k)
            for b in range(B):
                for j in range(J):
                    i = J * b + j
                    if i % (TOK // 4) == 0:
                        dve.wait_ge(s_back[i // (TOK // 4)], 4 * TOK)
                    last = dve.scalar_tensor_tensor(X[:, b, j, :], fBACK[:, i, :], f_w[:, i:i + 1], X[:, b, j, :],
                                                    ALU.mult, ALU.add)
                last.then_inc(s_x, 1)

        @block.sync
        def _(sp):
            sp.dma_start(X[:, :, :, :], I["x"].rearrange("b (j p) d -> p b j d", p=P)).then_inc(s_lx, 16)
            for dst, name in ((wbrT, "wbrT"), (wcrT, "wcrT"), (wcm, "wcm"), (ident, "ident")):
                sp.dma_start(dst[:, :], I[name]).then_inc(s_l0, 16)
            sp.dma_start(fly[:, 0, :], I["wbs"]).then_inc(s_l0, 16)
            sp.dma_start(factors[:, :], I["factors"].partition_broadcast(R)).then_inc(s_l0, 16)
            sp.dma_start(dvec[:, :], I["dvec"]).then_inc(s_l0, 16)
            sp.dma_start(ctxT[:, :, :, :], I["ctxT"].rearrange("(c p) b t -> p c b t", p=P)).then_inc(s_l1, 16)
            sp.dma_start(ctxN[:, :, :], I["ctx"].rearrange("b t d -> t b d")).then_inc(s_l1, 16)
            sp.dma_start(masku[:, :, :], I["mask"].partition_broadcast(P)).then_inc(s_l1, 16)
            for n, (src, s) in enumerate((("gateT", s_lg), ("valT", s_lv), ("outT", s_lo))):
                if n:
                    sp.wait_ge(s_c, mark[f"w{n - 1}"])
                cols = D if src == "outT" else HID
                sp.dma_start(wstage[:, :, :].rearrange("p c n -> p (c n)").rearrange("p (c n) -> p c n", n=cols),
                             I[src].rearrange("(c p) n -> p c n", p=P)).then_inc(s, 16)
            sp.dma_start(gate_b, I["gate_b"].partition_broadcast(P)).then_inc(s_l2, 16)
            sp.dma_start(val_b, I["val_b"].partition_broadcast(P)).then_inc(s_l2, 16)
            sp.dma_start(ffo_b[:, :], I["ffo_b"].partition_broadcast(P)).then_inc(s_l2, 16)
            sp.dma_start(w_in[:, :, :], I["w_in"].rearrange("(c p) n -> p c n", p=P)).then_inc(s_l3, 16)
            sp.dma_start(w_out[:, :, :], I["w_out"].rearrange("(c p) n -> p c n", p=P)).then_inc(s_l3, 16)
            sp.dma_start(bqk[:, :], I["bqk"]).then_inc(s_l3, 16)
            sp.dma_start(b_v[:, :], I["b_v"].partition_broadcast(P)).then_inc(s_l3, 16)
            sp.dma_start(b_o[:, :], I["b_o"].partition_broadcast(P)).then_inc(s_l3, 16)
            sp.dma_start(hmask[:, :], I["hmask"]).then_inc(s_l3, 16)
            sp.dma_start(causal[:, :, :], I["causal"]).then_inc(s_l3, 16)
            for dst, name in ((wq, "wq"), (wk, "wk"), (wv, "wv"), (wkc, "wkc"), (wvc, "wvc"), (wo, "wo"),
                              (cosT, "cos"), (sinT, "sin")):
                sp.dma_start(dst[:, :, :], I[name].rearrange("(c p) n -> p c n", p=P)).then_inc(s_l4, 16)
            for dst, name in ((qw, "qw"), (qws, "qws"), (kw, "kw"), (kws, "kws")):
                sp.dma_start(dst[:, :], I[name].partition_broadcast(P)).then_inc(s_l4, 16)
            sp.dma_start(kmask[:, :, :], I["kmask"]).then_inc(s_l4, 16)
            sp.dma_start(ew[:, :, :], I["ewT"].rearrange("(c p) n -> p c n", p=P)).then_inc(s_l5, 16)
            sp.dma_start(rwT[:, :, :], I["rwT"].rearrange("(c p) n -> p c n", p=P)).then_inc(s_l5, 16)
            sp.dma_start(iota[:, :], I["iota"].partition_broadcast(P)).then_inc(s_l5, 16)
            sp.dma_start(esc[:, :], I["esc"].partition_broadcast(P)).then_inc(s_l5, 16)
            sp.wait_ge(s_c, mark["w2"])
            for e in range(4):
                sp.dma_start(mring[:, e, :], I["masksT"][e]).then_inc(s_mld[e], 16)
            with sp.Fori(1, NE // 4) as n:
                for e in range(4):
                    sp.wait_ge(s_mfree, 4 * n + (e - 3))
                    sp.dma_start(mring[:, e, :], I["masksT"][ds(4 * n + e, 1)].rearrange("a p n -> p (a n)"))\
                        .then_inc(s_mld[e], 16)
            sp.wait_ge(s_zero, 1)
            sp.dma_start(rows.rearrange("(t p) d -> p t d", p=P), bc(zeros.unsqueeze(1), [P, TILES * HT // P, D]))\
                .then_inc(s_cleared, 16)
            group_rows = rows.rearrange("(g t p) d -> g p t d", t=2, p=P)

            def groups(n):
                for k in range(RING):
                    g = RING * n + k
                    after(sp, f_tp, g - RING + 1)
                    sp.dma_start(sIN[:, k], group_rows[ds(g, 1)].rearrange("a p t d -> p (a t) d")) \
                        .then_inc(s_rows[k], 16)

            sp.wait_ge(s_sorted, 16 * TOK)
            over_rounds(sp, groups)
            with sp.Fori(0, B) as b:
                sp.wait_ge(s_x, MOE * B + b + 1)
                sp.dma_start(out[ds(b, 1)].rearrange("a (j p) d -> p (a j) d", p=P),
                             X[:, ds(b, 1), :, :].rearrange("p a j d -> p (a j) d")).then_inc(s_out, 16)
            sp.wait_ge(s_out, 16 * B)


        @block.gpsimd
        def _(pool):
            pool.memset(halves[:, :], -0.5).then_inc(s_pc, 1)
            pool.memset(ones[:, :], 1.0).then_inc(s_pc, 1)
            pool.memset(magic[:, :], MAGIC).then_inc(s_pc, 1)
            pool.wait_ge(s_pc, 3)

            def rstds(phase, b):
                n = phase * B + b
                held(pool, s_mv, n + 1)
                pool.tensor_scalar(ve[:, :], mv[:, :, 1], LN_EPS, None, ALU.add).then_inc(s_ve, 1)
                pool.wait_ge(s_ve, n + 1)
                pool.tensor_tensor(rstd[:, :], ve[:, :], halves[:, 0:J], ALU.pow).then_inc(s_rs, 1)

            rstds(MIX, 0)
            for phase in (MIX, CROSS):
                over_batches(pool, phase, lambda b, nxt: rstds(*nxt))

            def ffn(b, nxt):
                for e in range(4):
                    pool.wait_ge(s_mld[e], 16 * b + 16)
                    pool.tensor_tensor(EW[:, ds(4 * b + e, 1), :].rearrange("p a n -> p (a n)"),
                                       mring[:, e, :], ew[:, :, :].rearrange("p c n -> p (c n)"),
                                       ALU.mult).then_inc(s_mfree, 1)
                rstds(*nxt)

            pool.wait_ge(s_c, mark["ew"])
            over_batches(pool, FFN, ffn)
            pool.wait_ge(s_mfree, NE)
            pool.memset(zeros, 0.0).then_inc(s_zero, 1)
            over_batches(pool, SELF, lambda b, nxt: rstds(*nxt))

            def turn_keys(b):
                for seg in range(3):
                    n = T if seg == 1 else P
                    pool.wait_ge(e_kr, 3 * b + seg + 1)
                    pool.tensor_tensor(eSQ[0:n, seg, :], eKR[0:n, seg, :], eKR[0:n, seg, :], ALU.mult)\
                        .then_inc(e_sq, 1)
                for seg in range(3):
                    n = T if seg == 1 else P
                    held(pool, e_ssq, 3 * b + seg + 1)
                    pool.tensor_scalar(e_kp[0:n, seg, :], e_ks[0:n, seg, :], RMS_EPS * XD, None, ALU.add)\
                        .then_inc(e_ve, 1)
                    pool.wait_ge(e_ve, 3 * b + seg + 1)
                    pool.tensor_tensor(e_rks[0:n, seg, :], e_kp[0:n, seg, :], halves[0:n, 0:XG], ALU.pow)\
                        .then_inc(e_rk, 1)
                for k, seg in enumerate((0, 2)):
                    pool.wait_ge(e_kn, 3 * b + seg + 1)
                    kn = eKR[:, seg, :].rearrange("p (g u v) -> p g u v", g=XG, u=2)
                    kb = eKB[:, k, :].rearrange("p (g u v) -> p g u v", g=XG, u=2)
                    for u in range(2):
                        last = pool.tensor_tensor(kb[:, :, u, :], kn[:, :, 1 - u, :],
                                                  bc(sink[:, k, 64 * u:64 * u + 64].unsqueeze(1), [P, XG, 64]),
                                                  ALU.mult)
                    last.then_inc(e_kb, 1)

            def hybrid(b, nxt):
                def query(i):
                    j, u = i // XG, 8 * b + i
                    pool.wait_ge(e_qr, u + 1)
                    pool.wait_ge(e_qq, u)
                    pool.wait_ge(e_qf, u)
                    pool.tensor_tensor(eQS, eQR, eQR, ALU.mult).then_inc(e_qs, 1)
                    q = eQR.rearrange("p (g u v) -> p g u v", g=GH, u=2)
                    qb = eQB.rearrange("p (g u v) -> p g u v", g=GH, u=2)
                    for h in range(2):
                        last = pool.tensor_tensor(qb[:, :, h, :], q[:, :, 1 - h, :],
                                                  bc(sinq[:, j, 64 * h:64 * h + 64].unsqueeze(1), [P, GH, 64]),
                                                  ALU.mult)
                    last.then_inc(e_qb, 1)
                    held(pool, e_qq, u + 1)
                    pool.tensor_scalar(e_q3, e_q2, RMS_EPS * XD, None, ALU.add).then_inc(e_qv, 1)
                    pool.wait_ge(e_qv, u + 1)
                    if i >= 2:
                        pool.wait_ge(e_e, u - 1)
                    pool.tensor_tensor(e_rqs[:, i % 2, :], e_q3, halves[:, 0:GH], ALU.pow).then_inc(e_rq, 1)

                for i in range(8):
                    query(i)
                    if i == 6:
                        rstds(*nxt)
                if nxt[0] == HYBRID:
                    turn_keys(nxt[1])

            turn_keys(0)
            over_batches(pool, HYBRID, hybrid)

            def route(b, nxt):
                if nxt[0] == MOE:
                    rstds(*nxt)
                held(pool, s_xn, MOE * B + b + 1)
                pool.tensor_copy(fROW[:, ds(J * b, J), :], XN[:, :, :]).then_inc(f_row, 1)

            over_batches(pool, MOE, route)
            pool.wait_ge(s_c, mark["slots"])
            pool.wait_ge(f_row, B)
            for i in range(TOK):
                pool.indirect_dma_start(rows[:, :], bass.IndirectOffsetOnAxis(ap=f_slotu[:, i:i + 1], axis=0),
                                        fROW[:, i, :], None).then_inc(s_sorted, 16)

            def low_parts(n):
                for k in range(RING):
                    u = RING * n + k
                    after(pool, f_y, u - RING + 1)
                    pool.wait_ge(f_xm, u + 1)
                    pool.tensor_tensor(sXL[:, k].rearrange("p t n -> p (t n)"), sR[:, k, :],
                                       sXM[:, k].rearrange("p t n -> p (t n)"), ALU.subtract).then_inc(f_xl, 1)

            over_rounds(pool, low_parts)
            for k in range(RING):
                pool.wait_ge(s_stored[k], 16 * ROUNDS)
            for i in range(TOK):
                pool.indirect_dma_start(fBACK[:, i, :], None, results[:, :],
                                        bass.IndirectOffsetOnAxis(ap=f_slotu[:, i:i + 1], axis=0))\
                    .then_inc(s_back[i // (TOK // 4)], 16)

        @block.scalar
        def _(act):
            def xt_copy(nxt, used=(), at=0):
                phase, b = nxt
                for s, value in used:
                    act.wait_ge(s, value)
                act.wait_ge(s_xtp, phase * B + b + 1)
                src, dst = (bank(at), XT[:, :, :].rearrange("p c s -> p (c s)")) if phase != FFN else \
                    (pXT[:, 0:D].bitcast(BF), cXT.rearrange("p c s -> p (c s)"))
                act.activation(dst, src, ACT.Copy).then_inc(s_xt, 1)

            act.wait_ge(s_pc, 3)
            xt_copy((MIX, 0))
            over_batches(act, MIX, lambda b, nxt: xt_copy(nxt, [(a_mm, b + 1)]))

            def cross(b, nxt):
                act.wait_ge(b_m, b + 1)
                for j in range(J):
                    last = act.activation(bP[:, j, :], bSC[:, j, :], ACT.Exp, bias=b_nm[:, j:j + 1],
                                          accum_out=b_sum[:, j:j + 1])
                last.then_inc(b_e, 1)
                act.wait_ge(b_t, b + 1)
                act.activation(bPT[0:T, :], PS[0:T, 2, 0:S], ACT.Copy).then_inc(b_tc, 1)
                xt_copy(nxt, [(b_s, b + 1)])

            over_batches(act, CROSS, cross)

            def ffn(b, nxt):
                for j in range(J):
                    u = J * b + j
                    act.wait_ge(c_gs, u + 1)
                    act.activation(cHS, cHG, ACT.Silu).then_inc(c_si, 1)
                    act.wait_ge(c_s[3], u + 1)
                    act.activation(cHR, cH, ACT.Identity, bias=magic[:, 0:1], scale=c_sh).then_inc(c_hr, 1)
                    act.wait_ge(c_t, u + 1)
                    act.activation(cHT.rearrange("p a b -> p (a b)"), bank(5).bitcast(BF), ACT.Copy).then_inc(c_ht, 1)
                    if j == 0:
                        xt_copy(nxt, [(c_v, J * b + 2)])

            over_batches(act, FFN, ffn)
            act.wait_ge(s_l3, 16 * 7)

            def self_queries(b):
                act.wait_ge(d_pq, b + 1)
                for m in range(2):
                    last = act.activation(dQ[:, m, :], PS[:, 4, m * S:(m + 1) * S], ACT.Identity, bias=bqk[:, m:m + 1])
                last.then_inc(d_q, 1)

            def self_finish(b):
                act.wait_ge(d_ot, b + 1)
                act.activation(dOT.rearrange("p c s -> p (c s)"), bank(1), ACT.Copy).then_inc(d_oc, 1)

            def self_attention(b, nxt):
                def exps(i):
                    j, u = i // 4, 8 * b + i
                    n = (j + 1) * P
                    act.wait_ge(d_nm, u + 1)
                    if i >= 2:
                        act.wait_ge(d_t, u - 1)
                    for hh in range(4):
                        h = j * NH + 4 * (i % 4) + hh
                        last = act.activation(dP[:, i % 2, hh, 0:n], dSS[:, i % 2, hh, 0:n], ACT.Exp,
                                              bias=d_neg[:, i % 2, hh:hh + 1], scale=0.25,
                                              accum_out=d_sum[:, h:h + 1])
                    last.then_inc(d_e, 1)

                exps(0)
                if type(b) is not int or b > 0:
                    self_finish(b - 1)
                for i in range(8):
                    if i + 1 < 8:
                        exps(i + 1)
                    if i % 2 == 0:
                        u = 8 * b + i
                        act.wait_ge(d_t, u + 1)
                        if i >= 2:
                            act.wait_ge(d_pv, u - 1)
                        n = 4 * (1 + i // 4) * P
                        act.activation(dPT[:, 0, :, :].rearrange("p a b -> p (a b)")[:, 0:n],
                                       bank(1, 2)[:, 0:n], ACT.Copy).then_inc(d_pt, 1)
                    if i == 5:
                        xt_copy(nxt, [(d_pq, b + 1)])
                if nxt[0] == SELF:
                    self_queries(nxt[1])

            self_queries(0)
            over_batches(act, SELF, self_attention)
            self_finish(B - 1)

            def raw_keys(b, seg):
                n = T if seg == 1 else P
                act.wait_ge(e_k, 3 * b + seg + 1)
                act.wait_ge(e_kt, 3 * b)
                act.activation(eKR[0:n, seg, :], PS[0:n, 1, :], ACT.Copy).then_inc(e_kr, 1)

            def context(b):
                act.wait_ge(e_v, 3 * b)
                act.activation(eCT[:, :, :], ctxT[:, :, ds(b, 1), :].rearrange("p c a t -> p c (a t)"), ACT.Copy)\
                    .then_inc(e_ct, 1)

            def hybrid(b, nxt):
                def raw_query(i):
                    u = 8 * b + i
                    act.wait_ge(e_q, u + 1)
                    act.wait_ge(e_qb, u)
                    act.wait_ge(e_qf, u)
                    act.activation(eQR, PS[:, 1, :], ACT.Copy).then_inc(e_qr, 1)

                def query(i):
                    u = 8 * b + i
                    act.wait_ge(e_qt, u + 1)
                    act.wait_ge(e_s, GH * u)
                    act.activation(eQT, PS[:, 2, :], ACT.Copy).then_inc(e_qc, 1)

                def exps(i):
                    j, u = i // XG, 8 * b + i
                    n = KEYS if j else P + T
                    act.wait_ge(e_nm, u + 1)
                    for hh in range(GH):
                        last = act.activation(eP[:, i % 2, hh, 0:n], eP[:, i % 2, hh, 0:n], ACT.Exp,
                                              bias=e_neg[:, i % 2, hh:hh + 1], scale=e_rqs[:, i % 2, hh:hh + 1],
                                              accum_out=e_sum[:, i % 2, hh:hh + 1])
                    last.then_inc(e_e, 1)

                def outputs(i):
                    u = 8 * b + i
                    j, g = i // XG, i % XG
                    act.wait_ge(e_pv, u + 1)
                    if i == 0:
                        act.wait_ge(e_y, J * b)
                    act.activation(eOT[:, GH * g:GH * g + GH, j * P:(j + 1) * P],
                                   PS[:, 0, :].rearrange("p (h s) -> p h s", h=GH), ACT.Copy).then_inc(e_oc, 1)

                raw_query(0)
                for seg in range(3):
                    n = T if seg == 1 else P
                    act.wait_ge(e_v, 3 * b + seg + 1)
                    act.activation(eV[0:n, seg, :], PS[0:n, 5 + seg, :], ACT.Copy).then_inc(e_vr, 1)
                for seg in range(3):
                    n = T if seg == 1 else P
                    at = (0, P, P + T)[seg]
                    act.wait_ge(e_kt, 3 * b + seg + 1)
                    act.activation(eKT[:, :, at:at + n],
                                   PS[:, 2 + seg, 0:XG * n].rearrange("p (g n) -> p g n", g=XG),
                                   ACT.Copy).then_inc(e_kc, 1)
                query(0)
                raw_query(1)

                def turn(i):
                    u = 8 * b + i
                    act.wait_ge(e_t, u + 1)
                    act.wait_ge(e_pv, u)
                    act.activation(ePT[:, 0, :], PS[:, 5, :], ACT.Copy).then_inc(e_pta, 1)

                for i in range(8):
                    if i >= 1:
                        turn(i - 1)
                    if i + 1 < 8:
                        query(i + 1)
                    exps(i)
                    if i + 2 < 8:
                        raw_query(i + 2)
                    if i == 6:
                        xt_copy(nxt, [(e_q, 8 * b + 8)], 1)
                        if nxt[0] == HYBRID:
                            context(nxt[1])
                    if i >= 1:
                        outputs(i - 1)
                    if nxt[0] == HYBRID and i >= 6:
                        raw_keys(nxt[1], i - 6)
                turn(7)
                if nxt[0] == HYBRID:
                    raw_keys(nxt[1], 2)
                outputs(7)

            context(0)
            for seg in range(3):
                raw_keys(0, seg)
            over_batches(act, HYBRID, hybrid)

            def route(b, nxt):
                act.wait_ge(f_nm, b + 1)
                for j in range(J):
                    last = act.activation(fE[:, j, :], fLG[:, j, :], ACT.Exp, bias=f_neg[:, j:j + 1],
                                          accum_out=f_sm[:, ds(J * b + j, 1)])
                last.then_inc(f_e, 1)
                if nxt[0] == MOE:
                    xt_copy(nxt, [(f_l, b + 1)])

            over_batches(act, MOE, route)

            group_results = results.rearrange("(g t p) d -> g p t d", t=QT, p=HT)

            def store(k, u):
                act.wait_ge(f_yo, u + 1)
                act.dma_start(group_results[ds(u, 1)].rearrange("a p t d -> p (a t) d"), sY[:, k]) \
                    .then_inc(s_stored[k], 16)

            def parts(n):
                for k in range(RING):
                    u = RING * n + k
                    act.wait_ge(f_tp, u + 1)
                    after(act, f_y, u - RING + 1)
                    act.activation(sXH[:, k].rearrange("p t n -> p (t n)"), bank(k), ACT.Copy).then_inc(f_xh, 1)
                    act.wait_ge(f_r1, u + 1)
                    act.activation(sXM[:, k].rearrange("p t n -> p (t n)"), sR[:, k, :], ACT.Copy).then_inc(f_xm, 1)
                    if k >= 3:
                        store(k - 3, u - 3)
                    elif type(n) is not int or n > 0:
                        store(k + 1, u - 3)

            over_rounds(act, parts)
            for k in range(1, RING):
                store(k, RING * (ROUNDS - 1) + k)

        @block.tensor
        def _(pe):
            def product(dst, lhs, rhs, first=True, last=True):
                return pe.matmul(dst, lhs, rhs, start=first, stop=last)

            def xt_turn(phase, b, to=0):
                n = phase * B + b
                pe.wait_ge(s_xn, n + 1)
                pe.wait_ge(s_xt, n)
                for c in range(C):
                    for j in range(J):
                        at = c * S + j * P
                        if phase == FFN:
                            last = pe.transpose(pXT[:, 0:D].bitcast(BF)[:, at:at + P],
                                                cXB[:, j, c * P:(c + 1) * P], identb[:, :])
                        else:
                            last = pe.transpose(PS[:, to, at:at + P], XN[:, j, c * P:(c + 1) * P], ident[:, :])
                last.then_inc(s_xtp, 1)

            pe.wait_ge(s_c, mark["fly"])
            product(PS[0:NS, 1, 0:D], fly[:, LV % 2, :], wbrT[:, :])
            product(PS[0:NS, 2, 0:D], wcrT[:, :], wcm[:, :]).then_inc(s_pp, 1)
            pe.wait_ge(s_c, mark["folds"])
            for c in range(C):
                last = product(PS[:, 3 + c, 0:D], b_fold[:, c * P:(c + 1) * P], c_fold[:, :])
            last.then_inc(s_pp, 1)
            xt_turn(MIX, 0)
            pe.wait_ge(s_c, mark["mix"])

            def mixer(b, nxt):
                pe.wait_ge(s_xt, b + 1)
                pe.wait_ge(s_x, b)
                for j in range(J):
                    for c in range(C):
                        last = product(PS[:, 1, j * D:(j + 1) * D], XT[:, c, j * P:(j + 1) * P], mix[:, c, :],
                                       c == 0, c == C - 1)
                last.then_inc(a_mm, 1)
                xt_turn(*nxt)

            over_batches(pe, MIX, mixer)

            for k in range(3):
                pe.wait_ge(s_c, mark[f"wsum{k}"])
                product(PS[:, 7, k:k + 1], ones[:, :], wsum[:, k:k + 1]).then_inc(s_ps, 1)

            def cross(b, nxt):
                pe.wait_ge(s_xt, CROSS * B + b + 1)
                pe.wait_ge(s_x, CROSS * B + b)
                for j in range(J):
                    for c in range(C):
                        last = product(PS[:, 1, j * T:(j + 1) * T], XT[:, c, j * P:(j + 1) * P],
                                       ctxT[:, c, ds(b, 1), :].rearrange("p a t -> p (a t)"), c == 0, c == C - 1)
                last.then_inc(b_s, 1)
                held(pe, b_p, b + 1)
                for j in range(J):
                    last = pe.transpose(PS[0:T, 2, j * P:(j + 1) * P], bP[:, j, :], ident[:, :])
                last.then_inc(b_t, 1)
                pe.wait_ge(b_tc, b + 1)
                for j in range(J):
                    last = product(PS[:, 3, j * D:(j + 1) * D], bPT[0:T, j * P:(j + 1) * P],
                                   ctxN[:, ds(b, 1), :].rearrange("p a d -> p (a d)"))
                last.then_inc(b_o2, 1)
                xt_turn(*nxt)

            over_batches(pe, CROSS, cross)

            def gate_value(b, j):
                u = J * b + j
                pe.wait_ge(s_xt, FFN * B + b + 1)
                pe.wait_ge(c_vs, u)
                for w, at, s in ((gateT, 1, c_g), (valT, 3, c_v)):
                    for n in range(2):
                        for c in range(C):
                            last = product(PS[:, at + n, :], cXT[:, c, j * P:(j + 1) * P],
                                           w[:, c, 512 * n:512 * n + 512], c == 0, c == C - 1)
                    last.then_inc(s, 1)

            def down(b, j):
                u = J * b + j
                pe.wait_ge(c_hq, u + 1)
                for m in range(HC):
                    last = pe.transpose(bank(5).bitcast(BF)[:, m * P:(m + 1) * P], cHQ[:, m * P:(m + 1) * P], identb[:, :])
                last.then_inc(c_t, 1)
                pe.wait_ge(c_ht, u + 1)
                for m in range(HC):
                    last = product(PS[:, 6, 0:D], cHT[:, m, :], outT[:, m, :], m == 0, m == HC - 1)
                last.then_inc(c_o, 1)

            def ffn(b, nxt):
                gate_value(b, 1)
                down(b, 0)
                xt_turn(*nxt)
                if nxt[0] == FFN:
                    gate_value(nxt[1], 0)
                down(b, 1)

            pe.wait_ge(s_c, mark["w2"])
            pe.wait_ge(s_x, FFN * B)
            gate_value(0, 0)
            over_batches(pe, FFN, ffn)

            pe.wait_ge(s_l3, 16 * 7)

            def self_project(b):
                pe.wait_ge(s_xt, SELF * B + b + 1)
                pe.wait_ge(d_mx, 8 * b)
                for m in range(4):
                    for c in range(C):
                        product(PS[:, 4 + m // 2, (m % 2) * S:(m % 2 + 1) * S], w_in[:, c, m * P:(m + 1) * P],
                                XT[:, c, :], c == 0, c == C - 1)
                for j in range(J):
                    for c in range(C):
                        last = product(PS[:, 6, j * D:(j + 1) * D], XT[:, c, j * P:(j + 1) * P],
                                       w_in[:, c, 2 * D:3 * D], c == 0, c == C - 1)
                last.then_inc(d_pq, 1)

            def self_finish(b):
                pe.wait_ge(d_pt, 8 * b + 8)
                pe.wait_ge(d_o, b + 1)
                for c in range(C):
                    for j in range(J):
                        last = pe.transpose(PS[:, 1, c * S + j * P:c * S + (j + 1) * P], dO[:, j, c * P:(c + 1) * P],
                                            ident[:, :])
                last.then_inc(d_ot, 1)
                pe.wait_ge(d_oc, b + 1)
                for j in range(J):
                    for c in range(C):
                        last = product(PS[:, 2, j * D:(j + 1) * D], dOT[:, c, j * P:(j + 1) * P], w_out[:, c, :],
                                       c == 0, c == C - 1)
                last.then_inc(d_y, 1)

            def self_attention(b, nxt):
                def scores(i):
                    j, u = i // 4, 8 * b + i
                    n = (j + 1) * P
                    if i == 0:
                        pe.wait_ge(d_q, b + 1)
                        pe.wait_ge(d_vv, b + 1)
                    if i >= 2:
                        pe.wait_ge(d_mx, u - 1)
                    for hh in range(4):
                        h = 4 * (i % 4) + hh
                        last = product(PS[:, 4 + 2 * (i % 2) + hh // 2, (hh % 2) * S:(hh % 2) * S + n],
                                       dQ[:, h // 8, j * P:(j + 1) * P], dK[:, h, 0:n])
                    last.then_inc(d_s, 1)

                def turn(i):
                    j, u = i // 4, 8 * b + i
                    pe.wait_ge(d_e, u + 1)
                    pe.wait_ge(d_pt, u)
                    if i == 0:
                        pe.wait_ge(d_yb, b)
                    for hh in range(4):
                        for k in range(j + 1):
                            at = (hh * (j + 1) + k) * P
                            last = pe.transpose(bank(1, 2)[:, at:at + P], dP[:, i % 2, hh, k * P:(k + 1) * P], ident[:, :])
                    last.then_inc(d_t, 1)

                def outputs(i):
                    j, u = i // 4, 8 * b + i
                    pe.wait_ge(d_pt, u + 1)
                    if i == 0:
                        pe.wait_ge(d_o, b)
                    for hh in range(4):
                        h = 4 * (i % 4) + hh
                        for k in range(j + 1):
                            last = product(PS[:, 3, j * D + h * DH:j * D + (h + 1) * DH],
                                           dPT[:, i % 2, hh * (j + 1) + k, :], dV[:, k, h * DH:(h + 1) * DH],
                                           k == 0, k == j)
                    last.then_inc(d_pv, 1)

                scores(0)
                scores(1)
                if type(b) is not int or b > 0:
                    self_finish(b - 1)
                for i in range(8):
                    if i + 2 < 8:
                        scores(i + 2)
                    turn(i)
                    if i >= 1:
                        outputs(i - 1)
                    if i == 5:
                        xt_turn(*nxt)
                if nxt[0] == SELF:
                    self_project(nxt[1])
                outputs(7)

            pe.wait_ge(s_x, SELF * B)
            self_project(0)
            over_batches(pe, SELF, self_attention)
            self_finish(B - 1)

            pe.wait_ge(s_c, mark["tables"])

            def raw_keys(b, seg):
                n = T if seg == 1 else P
                pe.wait_ge(s_xt, HYBRID * B + b + 1)
                pe.wait_ge(e_ct, b + 1)
                pe.wait_ge(e_kr, 3 * b + seg)
                for c in range(C):
                    last = product(PS[0:n, 1, :], eCT[:, c, :] if seg == 1 else
                                   XT[:, c, (seg // 2) * P:(seg // 2 + 1) * P],
                                   (wkc if seg == 1 else wk)[:, c, :], c == 0, c == C - 1)
                last.then_inc(e_k, 1)

            def hybrid_finish(b, j):
                if j == 0:
                    pe.wait_ge(e_oc, 8 * b + 8)
                for h in range(XH):
                    last = product(PS[:, 0, j * D:(j + 1) * D], eOT[:, h, j * P:(j + 1) * P], wo[:, h, :],
                                   h == 0, h == XH - 1)
                last.then_inc(e_y, 1)

            def hybrid(b, nxt):
                def raw_query(i):
                    j, g, u = i // XG, i % XG, 8 * b + i
                    pe.wait_ge(e_qr, u)
                    for c in range(C):
                        last = product(PS[:, 1, :], XT[:, c, j * P:(j + 1) * P], wq[:, c, 512 * g:512 * g + 512],
                                       c == 0, c == C - 1)
                    last.then_inc(e_q, 1)

                def query(i):
                    u = 8 * b + i
                    pe.wait_ge(e_qf, u + 1)
                    pe.wait_ge(e_qc, u)
                    for hh in range(GH):
                        last = pe.transpose(PS[:, 2, hh * P:(hh + 1) * P], eQA[:, hh * XD:(hh + 1) * XD], ident[:, :])
                    last.then_inc(e_qt, 1)

                def scores(i):
                    j, g, u = i // XG, i % XG, 8 * b + i
                    n = KEYS if j else P + T
                    pe.wait_ge(e_qc, u + 1)
                    for hh in range(GH):
                        if GH * i + hh >= 2:
                            pe.wait_ge(e_mx, GH * u + hh - 1)
                        product(PS[:, 3 + hh % 2, 0:n], eQT[:, hh * P:(hh + 1) * P], eKT[:, g, 0:n]).then_inc(e_s, 1)

                def turn(i):
                    j, u = i // XG, 8 * b + i
                    pe.wait_ge(e_p, u + 1)
                    pe.wait_ge(e_pta, u)
                    pe.wait_ge(e_ptd, u)
                    for hh in range(GH):
                        for k, (at, n) in enumerate(((0, P), (P, T), (P + T, P))[0:2 + j]):
                            last = pe.transpose(PS[0:n, 5 + k, hh * P:(hh + 1) * P], eP[:, i % 2, hh, at:at + n], ident[:, :])
                    last.then_inc(e_t, 1)

                def outputs(i):
                    j, g, u = i // XG, i % XG, 8 * b + i
                    pe.wait_ge(e_pta, u + 1)
                    pe.wait_ge(e_ptd, u + 1)
                    pe.wait_ge(e_oc, u)
                    if i == 0:
                        pe.wait_ge(s_x, HYBRID * B + b)
                    for k, n in enumerate((P, T, P)[0:2 + j]):
                        last = product(PS[:, 0, :], eV[0:n, k, g * XD:(g + 1) * XD], ePT[0:n, k, :], k == 0, k == 1 + j)
                    last.then_inc(e_pv, 1)

                pe.wait_ge(e_kr, 3 * b + 3)
                raw_query(0)
                pe.wait_ge(e_pta, 8 * b)
                pe.wait_ge(e_ptd, 8 * b)
                for seg in range(3):
                    n = T if seg == 1 else P
                    for c in range(C):
                        last = product(PS[0:n, 5 + seg, :], eCT[:, c, :] if seg == 1 else
                                       XT[:, c, (seg // 2) * P:(seg // 2 + 1) * P],
                                       (wvc if seg == 1 else wv)[:, c, :], c == 0, c == C - 1)
                    last.then_inc(e_v, 1)
                former = type(b) is not int or b > 0
                if former:
                    hybrid_finish(b - 1, 0)
                for seg in range(3):
                    n = T if seg == 1 else P
                    if seg == 1:
                        held(pe, e_ka, 3 * b + 2)
                    else:
                        pe.wait_ge(e_kf, 2 * b + 1 + seg // 2)
                    for g in range(XG):
                        last = pe.transpose(PS[:, 2 + seg, g * n:(g + 1) * n],
                                            eKF[0:n, seg, g * XD:(g + 1) * XD], ident[0:n, 0:n])
                    last.then_inc(e_kt, 1)
                pe.wait_ge(e_kc, 3 * b + 3)
                query(0)
                raw_query(1)
                if former:
                    hybrid_finish(b - 1, 1)
                scores(0)
                for i in range(8):
                    if i + 1 < 8:
                        query(i + 1)
                    if i + 2 < 8:
                        raw_query(i + 2)
                    if i == 6:
                        pe.wait_ge(e_qr, 8 * b + 8)
                        xt_turn(*nxt, 1)
                    if i == 0:
                        pe.wait_ge(e_vr, 3 * b + 3)
                    if i >= 1:
                        outputs(i - 1)
                    if nxt[0] == HYBRID and i >= 6:
                        raw_keys(nxt[1], i - 6)
                    if i + 1 < 8:
                        scores(i + 1)
                    turn(i)
                if nxt[0] == HYBRID:
                    raw_keys(nxt[1], 2)
                outputs(7)

            pe.wait_ge(s_x, HYBRID * B)
            for seg in range(3):
                raw_keys(0, seg)
            over_batches(pe, HYBRID, hybrid)
            for j in range(J):
                hybrid_finish(B - 1, j)

            def route(b, nxt):
                pe.wait_ge(s_xt, MOE * B + b + 1)
                pe.wait_ge(f_lg, b)
                for j in range(J):
                    for c in range(C):
                        last = product(PS[:, 7, j * NE:(j + 1) * NE], XT[:, c, j * P:(j + 1) * P], rwT[:, c, :],
                                       c == 0, c == C - 1)
                last.then_inc(f_l, 1)
                if nxt[0] == MOE:
                    xt_turn(*nxt)

            over_batches(pe, MOE, route)
            pe.wait_ge(s_c, mark["routing"])
            pe.wait_ge(f_oh, B)
            for i in range(TOK):
                last = product(PS[0:NE, 2, 0:1], fOH[:, i, :], onesb[:, 0:1], i == 0, i == TOK - 1)
            last.then_inc(f_count, 1)
            product(PS[:, 1, :], before, fOH.rearrange("p i e -> p (i e)"), True, False)
            for i in range(TOK - 1):
                last = product(PS[:, 1, (i + 1) * NE:].rearrange("p (i e) -> p i e", e=NE), onesb,
                               bc(fOH[:, i:i + 1, :], [P, TOK - 1 - i, NE]), False, i == TOK - 2)
            last.then_inc(f_rank, 1)
            pe.wait_ge(s_c, mark["tiles"])
            product(PS[:, 3, 0:NE], tilesB[0:NE, :], lower[0:NE, :])
            product(PS[0:NE, 4, 0:1], upto[0:NE, :], f_tiles).then_inc(f_base, 1)
            pe.wait_ge(s_c, mark["past"])
            product(PS[:, 5, 0:TILES], ones[0:NE, :], past[0:NE, :]).then_inc(f_tex, 1)
            pe.wait_ge(s_c, mark["experts"])

            registers = [pe.alloc_register(f"expert{t}") for t in range(QT)]

            def apply(k, u):
                pe.load(registers, f_exu[0:1, ds(QT * u, QT)])
                expert = [bass.RuntimeValue.of_register_unchecked(r, min_val=0, max_val=NE - 1) for r in registers]
                after(pe, f_yo, u - 1)
                held(pe, f_xl, u + 1)
                for t in range(QT):
                    for m, part in enumerate((sXH, sXM, sXL)):
                        for c in range(C):
                            last = product(PS[0:HT, 4 + 2 * (k % 2) + t // 2, t % 2 * D:(t % 2 + 1) * D],
                                           part[:, k, t // 2, c * P + t % 2 * HT:c * P + t % 2 * HT + HT],
                                           EW[:, ds(expert[t], 1), c * D:(c + 1) * D].rearrange("p a d -> p (a d)"),
                                           m == 0 and c == 0, m == 2 and c == C - 1)
                last.then_inc(f_y, 1)

            def experts(n):
                for k in range(RING):
                    u = RING * n + k
                    pe.wait_ge(s_rows[k], 16 * n + 16)
                    after(pe, f_xl, u - RING + 1)
                    for t in range(2):
                        for c in range(C):
                            last = pe.transpose(PS[:, k, (t * C + c) * P:(t * C + c + 1) * P],
                                                sIN[:, k, t, c * P:(c + 1) * P], ident[:, :])
                    last.then_inc(f_tp, 1)
                    if k >= 2:
                        apply(k - 2, u - 2)
                    elif type(n) is not int or n > 0:
                        apply(k + 2, u - 2)

            over_rounds(pe, experts)
            for k in range(2, RING):
                apply(k, RING * (ROUNDS - 1) + k)


def kernel(**inputs):
    import concourse.bacc as bacc
    from concourse.bass_utils import run_bass_kernel_spmd

    f = {k: np.asarray(v) for k, v in inputs.items()}
    row = lambda a: np.ascontiguousarray(a.reshape(-1))
    swap = lambda a: np.concatenate([a[XD // 2:], a[:XD // 2]])
    w_in = f["L1_attn_W_in"]
    pos = np.arange(S, dtype=np.float32)
    inv = (1.0 / 10000.0 ** (np.arange(0, XD, 2, dtype=np.float32) / np.float32(XD))).astype(np.float32)
    ang = np.outer(pos, inv).astype(np.float32)
    cos, sin = np.cos(ang), np.sin(ang)
    tri = np.where(np.arange(S)[None, :] > np.arange(S)[:, None], NEG, 0.0).astype(np.float32)
    kmask = np.concatenate([tri[:, :P], np.zeros((S, T), np.float32), tri[:, P:]], axis=1)
    tiled = lambda a: np.ascontiguousarray(a.reshape(J, P, -1).transpose(1, 0, 2))
    masksT = f["L1_ffn_expert_masks"].transpose(0, 2, 1).reshape(NE, C, P, D).transpose(0, 2, 1, 3)
    arrays = {
        "x": f["x"],
        "ctx": f["ctx_2048"],
        "ctxT": f["ctx_2048"].transpose(2, 0, 1),
        "mask": f["mask_BxS2_bk0"],
        "wbrT": f["L0_attn_W_b_rank"].T, "wbs": f["L0_attn_W_b_state"],
        "wcrT": f["L0_attn_W_c_rank"].T, "wcm": f["L0_attn_W_c_model"],
        "factors": row(f["L0_attn_A_factors"]), "dvec": f["L0_attn_D_vec"].reshape(C, P).T,
        "gateT": f["L0_ffn_gate_w"].T, "valT": f["L0_ffn_val_w"].T, "outT": f["L0_ffn_out_w"].T,
        "gate_b": f["L0_ffn_gate_b"], "val_b": f["L0_ffn_val_b"], "ffo_b": f["L0_ffn_out_b"],
        "w_in": w_in, "w_out": f["L1_attn_W_out"],
        "bqk": f["L1_attn_b_in"][:2 * D].reshape(4, P).T, "b_v": f["L1_attn_b_in"][2 * D:], "b_o": f["L1_attn_b_out"],
        "wq": f["L1_xattn_wq"], "wk": f["L1_xattn_wk"], "wv": f["L1_xattn_wv"],
        "wkc": f["L1_xattn_wk_ctx"], "wvc": f["L1_xattn_wv_ctx"], "wo": f["L1_xattn_wo"],
        "qw": f["L1_xattn_q_norm_w"], "qws": swap(f["L1_xattn_q_norm_w"]),
        "kw": f["L1_xattn_k_norm_w"], "kws": swap(f["L1_xattn_k_norm_w"]),
        "ewT": f["L1_ffn_weight"].T, "rwT": f["L1_ffn_router_w"].T, "esc": f["L1_ffn_scale"],
        "masksT": masksT.reshape(NE, P, C * D),
        "ident": np.eye(P, dtype=np.float32),
        "hmask": np.repeat(np.eye(P // DH, dtype=np.float32), DH, axis=0),
        "causal": tiled(tri), "kmask": tiled(kmask),
        "cos": np.concatenate([cos, cos], 1), "sin": np.concatenate([-sin, sin], 1),
        "iota": np.arange(TILES, dtype=np.float32),
    }
    arrays = {f"in_{k}_dram": np.ascontiguousarray(v) for k, v in arrays.items()}
    nc = bacc.Bacc("TRN2", target_bir_lowering=False, num_devices=1)
    aps = {k[3:-5]: nc.dram_tensor(k, a.shape, mybir.dt.from_np(a.dtype), kind="ExternalInput").ap()
           for k, a in arrays.items()}
    out = nc.dram_tensor("out_dram", (B, S, D), mybir.dt.float32, kind="ExternalOutput").ap()
    rows = nc.dram_tensor("rows_dram", (TILES * HT, D), mybir.dt.float32, kind="Internal").ap()
    results = nc.dram_tensor("results_dram", (TILES * HT, D), mybir.dt.float32, kind="Internal").ap()
    decoder_kernel(nc, aps, out, rows, results)
    return run_bass_kernel_spmd(nc, [arrays], core_ids=[0]).results[0]["out_dram"]
```

```python
import numpy as np
import concourse.bass as bass
from concourse import mybir
from contextlib import ExitStack

B, S, D = 8, 256, 256
P = 128
J, C = S // P, D // P
T = 64
R, NS = 64, 32
LV = 5
HID = 1024
HC = HID // P
NH, DH = 16, 16
XH, XG, XD = 16, 4, 128
GH = XH // XG
KEYS = P + T + P
NE = 32
TOK = B * J
HT = P // 2
QT = 4
RING = 4
ROUNDS = 4
TILES = ROUNDS * RING * QT
assert TILES >= B * S // HT + NE - 1
LN_EPS, RMS_EPS = 1e-5, 1e-6
MAGIC = 12582912.0
NEG = -1e30
LOWEST = -3.0e38
MIX, CROSS, FFN, SELF, HYBRID, MOE = range(6)


def decoder_kernel(nc, I, out, rows, results):
    F32, BF, U8, U32 = mybir.dt.float32, mybir.dt.bfloat16, mybir.dt.uint8, mybir.dt.uint32
    ALU, ACT, AX = mybir.AluOpType, mybir.ActivationFunctionType, mybir.AxisListType
    ds = bass.ds

    with ExitStack() as ctx:
        def sb(name, shape, dt=F32):
            return ctx.enter_context(nc.sbuf_tensor(name, shape, dt))

        def sem(name):
            return ctx.enter_context(nc.semaphore(name))

        X = sb("X", [P, B, J, D])
        ident = sb("ident", [P, P])
        identb = sb("identb", [P, P], BF)
        ones = sb("ones", [P, P])
        halves = sb("halves", [P, 16])
        wbrT = sb("wbrT", [R, D])
        wcrT = sb("wcrT", [R, NS])
        wcm = sb("wcm", [R, D])
        fly = sb("fly", [R, 2, NS])
        factors = sb("factors", [R, LV * 4])
        dvec = sb("dvec", [P, C])
        b_fold = sb("b_fold", [NS, D])
        c_fold = sb("c_fold", [NS, D])
        early2 = sb("early2", [P, 4096])
        ctxT = sb("ctxT", [P, C, B, T])
        masku = sb("masku", [P, B, T], U8)
        mask = sb("mask", [P, B, T])
        valid = sb("valid", [P, B])
        early = sb("early", [P, 4096])
        ffo_b = sb("ffo_b", [P, D])
        wsum = sb("wsum", [P, 3])
        wpart = sb("wpart", [P, 3, B])
        gam = sb("gam", [P, 3])
        rgam = sb("rgam", [P, 3])
        gam127 = sb("gam127", [P, 3])
        w_in = sb("w_in", [P, C, 3 * D])
        w_out = sb("w_out", [P, C, D])
        bqk = sb("bqk", [P, 4])
        bk_head = sb("bk_head", [P, NH // 2])
        b_v = sb("b_v", [P, D])
        b_o = sb("b_o", [P, D])
        hmask = sb("hmask", [P, P // DH])
        causal = sb("causal", [P, J, S])
        wq = sb("wq", [P, C, XH * XD])
        wk = sb("wk", [P, C, XG * XD])
        wv = sb("wv", [P, C, XG * XD])
        wkc = sb("wkc", [P, C, XG * XD])
        wvc = sb("wvc", [P, C, XG * XD])
        wo = sb("wo", [P, XH, D])
        cosT = sb("cosT", [P, J, XD])
        sinT = sb("sinT", [P, J, XD])
        qw = sb("qw", [P, XD])
        qws = sb("qws", [P, XD])
        kw = sb("kw", [P, XD])
        kws = sb("kws", [P, XD])
        cosq = sb("cosq", [P, J, XD])
        sinq = sb("sinq", [P, J, XD])
        cosk = sb("cosk", [P, J, XD])
        sink = sb("sink", [P, J, XD])
        kmask = sb("kmask", [P, J, KEYS])
        ew = sb("ew", [P, C, D])
        rwT = sb("rwT", [P, C, NE])
        iota = sb("iota", [P, TILES])
        esc = sb("esc", [P, D])
        EW = sb("EW", [P, NE, C * D], BF)
        st = sb("st", [P, J, 6])
        mv = sb("mv", [P, J, 2])
        ve = sb("ve", [P, J])
        rstd = sb("rstd", [P, J])
        XN = sb("XN", [P, J, D])
        XT = sb("XT", [P, C, S])
        magic = sb("magic", [P, 1])
        unmagic = sb("unmagic", [P, 1])
        eCT = sb("eCT", [P, C, T])
        arena = sb("arena", [P, 8448])
        small = sb("small", [P, 512])

        def cut(at, shape, dt=F32, src=arena):
            n = 1
            for s in shape:
                n *= s
            words = n if dt == F32 else n // 2
            v = src[:, at:at + words]
            if dt != F32:
                v = v.bitcast(dt)
            if len(shape) > 1:
                names = "abcd"[:len(shape)]
                v = v.rearrange(f"p ({' '.join(names)}) -> p {' '.join(names)}",
                                **dict(zip(names[1:], shape[1:])))
            return v

        PS = ctx.enter_context(nc.psum_tensor("PS", [P, 8, 512], F32))

        def bank(n, k=1):
            return PS[:, n:n + k, :].rearrange("p b n -> p (b n)")

        pXT = bank(0)

        s_lx, s_l0, s_l1, s_l2, s_l3, s_l4, s_l5 = (
            sem(n) for n in ("s_lx", "s_l0", "s_l1", "s_l2", "s_l3", "s_l4", "s_l5"))
        s_lw = sem("s_lw")
        s_mld = [sem(f"s_mld{i}") for i in range(4)]
        s_mfree = sem("s_mfree")
        s_out = sem("s_out")
        s_held = sem("s_held")
        s_x = sem("s_x")
        s_bn, s_mv, s_ve, s_rs = sem("s_bn"), sem("s_mv"), sem("s_ve"), sem("s_rs")
        s_xn = sem("s_xn")
        s_xtp = sem("s_xtp")
        s_xt = sem("s_xt")
        s_c = sem("s_c")
        s_pc = sem("s_pc")
        s_abs = sem("s_abs")
        s_clip = sem("s_clip")
        s_tern = sem("s_tern")
        s_pp = sem("s_pp")
        s_ps = sem("s_ps")

        a_mm, = (sem("a_mm"),)
        b_s, b_c, b_m, b_e, b_r, b_v2, b_p, b_t, b_tc, b_o2 = (
            sem(n) for n in ("b_s", "b_c", "b_m", "b_e", "b_r", "b_v2", "b_p", "b_t", "b_tc", "b_o2"))
        d_vv = sem("d_vv")
        c_xq = sem("c_xq")
        c_q = [sem(f"c_q{i}") for i in range(5)]
        c_g, c_v, c_gs, c_si, c_vs, c_h, c_a = (
            sem(n) for n in ("c_g", "c_v", "c_gs", "c_si", "c_vs", "c_h", "c_a"))
        c_s = [sem(f"c_s{i}") for i in range(4)]
        c_hr, c_hq, c_t, c_ht, c_o, c_y = (
            sem(n) for n in ("c_hr", "c_hq", "c_t", "c_ht", "c_o", "c_y"))
        d_pq, d_q, d_k2, d_s, d_mx, d_nm, d_e, d_t, d_pt, d_pv, d_r, d_o, d_ot, d_oc, d_y, d_yb = (
            sem(n) for n in ("d_pq", "d_q", "d_k2", "d_s", "d_mx", "d_nm", "d_e", "d_t", "d_pt",
                             "d_pv", "d_r", "d_o", "d_ot", "d_oc", "d_y", "d_yb"))
        e_ct, e_k, e_v, e_vr = (sem(n) for n in ("e_ct", "e_k", "e_v", "e_vr"))
        e_kr, e_sq, e_ssq, e_ve, e_rk, e_kn, e_ka, e_kb, e_kf, e_kt, e_kc = (
            sem(n) for n in ("e_kr", "e_sq", "e_ssq", "e_ve", "e_rk", "e_kn", "e_ka",
                             "e_kb", "e_kf", "e_kt", "e_kc"))
        e_q, e_qr, e_qs, e_qb, e_qa, e_qq, e_qv, e_rq, e_qf, e_qt, e_qc, e_s, e_mx, e_nm, e_e, e_ri, \
            e_p, e_t, e_pta, e_ptd, e_pv, e_oc, e_y = (
                sem(n) for n in ("e_q", "e_qr", "e_qs", "e_qb", "e_qa", "e_qq", "e_qv", "e_rq",
                                 "e_qf", "e_qt", "e_qc", "e_s", "e_mx", "e_nm", "e_e", "e_ri", "e_p",
                                 "e_t", "e_pta", "e_ptd", "e_pv", "e_oc", "e_y"))
        f_l, f_lg, f_m, f_i, f_if, f_oh, f_nm, f_e, f_row = (
            sem(n) for n in ("f_l", "f_lg", "f_m", "f_i", "f_if", "f_oh", "f_nm", "f_e", "f_row"))
        f_count, f_rank, f_base, f_tex = (sem(n) for n in ("f_count", "f_rank", "f_base", "f_tex"))
        f_tp, f_xh, f_r1, f_xm, f_xl, f_y, f_yo = (
            sem(n) for n in ("f_tp", "f_xh", "f_r1", "f_xm", "f_xl", "f_y", "f_yo"))
        d_k1 = sem("d_k1")
        s_zero = sem("s_zero")
        s_cleared = sem("s_cleared")
        s_sorted = sem("s_sorted")
        s_rows = [sem(f"s_rows{i}") for i in range(RING)]
        s_stored = [sem(f"s_stored{i}") for i in range(RING)]
        s_back = [sem(f"s_back{i}") for i in range(4)]

        block = ctx.enter_context(nc.Block())

        def bc(ap, shape):
            return ap.broadcast_to(shape)

        def held(eng, s, value):
            eng.wait_ge(s, value)
            eng.sem_inc(s_held, 1)

        def over_batches(eng, phase, body):
            body(0, (phase, 1))
            with eng.Fori(1, B - 1) as b:
                body(b, (phase, b + 1))
            body(B - 1, (phase + 1, 0))

        def over_rounds(eng, body):
            body(0)
            body(1)
            with eng.Fori(2, ROUNDS) as n:
                body(n)

        def after(eng, s, value):
            if type(value) is not int or value > 0:
                eng.wait_ge(s, value)

        ctxN = cut(0, (B, D), F32, early2)[0:T]; val_b = cut(2048, (HID,), F32, early2)
        mix = cut(3072, (C, D), F32, early2); mbias = cut(3584, (B, T), F32, early2)
        gateT = cut(0, (C, HID), BF, early); valT = cut(1024, (C, HID), BF, early)
        outT = cut(2048, (HC, D), BF, early); gate_b = cut(3072, (HID,), F32, early)
        ternaries = cut(0, (3 * C * HID,), BF, early)
        wstage = EW[:, :, :].rearrange("p e n -> p (e n)").bitcast(F32)[:, 0:3 * C * HID]
        mring = cut(6400, (4, C * D))
        bSC = cut(5120, (J, T)); bP = cut(5248, (J, T)); bPT = cut(5376, (S,))
        junk = cut(0, (C * HID // B,))
        b_nm = small[:, 0:2]; b_sum = small[:, 2:4]; b_ri = small[:, 4:6]; b_rv = small[:, 6:8]
        cXQ = cut(0, (J, D)); cXB = cut(512, (J, D), BF); cXT = cut(768, (C, S), BF)
        cHG = cut(1024, (HID,)); cHS = cHG; cHV = cut(2048, (HID,)); cH = cut(3072, (HID,))
        cHR = cut(4096, (HID,)); cHQ = cut(5120, (HID,), BF); cHT = cut(5632, (HC, P), BF); cY = cut(0, (J, D), F32, early2)
        c_gx = small[:, 8:10]; c_rx = small[:, 10:12]; c_sx = small[:, 12:14]
        c_new = small[:, 14:18]; c_cur = small[:, 18:22]
        c_hm = small[:, 22:23]; c_rh = small[:, 23:24]; c_sh = small[:, 24:25]
        c_so = small[:, 26:28]
        dQ = cut(0, (2, S)); dK = cut(0, (NH, S), F32, early); dV = cut(512, (J, D))
        dSS = cut(1024, (2, 4, S)); dP = cut(3072, (2, 4, S)); dPT = cut(5120, (2, 8, P))
        dO = cut(7168, (J, D)); dOT = cut(7680, (C, S)); dY = dO
        d_max = small[:, 32:40].rearrange("p (a b) -> p a b", a=2)
        d_neg = small[:, 40:48].rearrange("p (a b) -> p a b", a=2)
        d_sum = small[:, 48:80]; d_ri = small[:, 80:112]
        eKR = cut(0, (3, 512), F32, early2); eKB = cut(1536, (2, 512), F32, early2)
        eKF = cut(2560, (3, 512), F32, early2); eSQ = eKF
        eP = cut(0, (2, GH, KEYS)); ePT = cut(2560, (3, 512))
        eKT = cut(4096, (XG, KEYS))
        eQR = cut(5376, (512,)); eQB = cut(5888, (512,)); eQS = cut(6400, (512,)); eQA = cut(6912, (512,))
        eQT = cut(7424, (512,))
        eV = w_in[:, :, :].rearrange("p c n -> p (c n)").rearrange("p (a n) -> p a n", a=3)
        eOT = cut(0, (XH, S), F32, early)
        e_ks = small[:, 112:124].rearrange("p (a b) -> p a b", a=3)
        e_kp = small[:, 124:136].rearrange("p (a b) -> p a b", a=3)
        e_rks = small[:, 136:148].rearrange("p (a b) -> p a b", a=3)
        e_q2 = small[:, 148:152]; e_q3 = small[:, 152:156]
        e_rqs = small[:, 432:444].rearrange("p (a b) -> p a b", a=3)
        e_max = small[:, 164:168]
        e_neg = small[:, 168:176].rearrange("p (a b) -> p a b", a=2)
        e_sum = small[:, 176:184].rearrange("p (a b) -> p a b", a=2)
        e_inv = small[:, 184:188]
        sIN = cut(0, (RING, 2, D))
        sXH = cut(2048, (RING, 2, C * P), BF); sXM = cut(3072, (RING, 2, C * P), BF)
        sXL = cut(4096, (RING, 2, C * P), BF); sR = cut(5120, (RING, 2 * C * P))
        fOH = cut(7168, (TOK, NE), BF); fSLOT = cut(0, (TOK, NE))
        before = cut(7424, (P,), BF); onesb = cut(7488, (P,), BF)
        lower = cut(7552, (NE,)); upto = cut(7584, (NE,)); tilesB = cut(7616, (P,)); past = cut(7744, (TILES,))
        fLG = cut(7808, (J, NE)); fE = cut(7872, (J, NE)); fBASE = cut(7936, (NE,))
        zeros = cut(8192, (D,))
        sY = cut(0, (RING, QT, D), F32, early)[0:HT]
        fROW = cut(0, (TOK, D), F32, early2)
        fBACK = cut(0, (TOK, D))
        f_m8 = small[:, 192:208].rearrange("p (a b) -> p a b", a=2)
        f_i8 = small[:, 208:224].bitcast(U32).rearrange("p (a b) -> p a b", a=2)
        f_if_ = small[:, 224:226]; f_neg = small[:, 226:228]
        f_sm = small[:, 232:248]; f_w = small[:, 248:264]
        f_slot = small[:, 264:280]; f_slotu = small[:, 280:296].bitcast(U32)
        f_tiles = small[0:NE, 296:297]; f_incl = small[0:NE, 297:298]
        f_ex = small[0:1, 304:304 + TILES]; f_exu = small[0:1, 368:368 + TILES].bitcast(U32)

        mark = {}

        @block.vector
        def _(dve):
            count = [0]

            def const(ins, name=None):
                count[0] += 1
                ins.then_inc(s_c, 1)
                dve.wait_ge(s_c, count[0])
                if name:
                    mark[name] = count[0]

            def ln_stats(phase, b):
                n = phase * B + b
                if phase == MIX:
                    dve.wait_ge(s_lx, 16)
                else:
                    dve.wait_ge(s_x, n - B + 1)
                for j in range(J):
                    last = dve.bn_stats(st[:, j, :], tokens(b, j))
                last.then_inc(s_bn, 1)
                held(dve, s_bn, n + 1)
                for j in range(J):
                    last = dve.bn_aggr(mv[:, j, :], st[:, j, :])
                last.then_inc(s_mv, 1)

            def tokens(b, j):
                return X[:, ds(b, 1), j, :].rearrange("p a d -> p (a d)")

            def batch(b):
                return X[:, ds(b, 1), :, :].rearrange("p a j d -> p (a j) d")

            def ln_apply(phase, b):
                n = phase * B + b
                dve.wait_ge(s_rs, n + 1)
                dve.wait_ge(s_xtp, n)
                for j in range(J):
                    last = dve.tensor_scalar(XN[:, j, :], tokens(b, j), mv[:, j, 0:1], rstd[:, j:j + 1],
                                             ALU.subtract, ALU.mult)
                if phase != FFN:
                    last.then_inc(s_xn, 1)
                    return
                last.then_inc(c_q[0], 1)
                dve.wait_ge(c_q[0], b + 1)
                dve.tensor_reduce(c_gx, XN[:, :, :], AX.X, ALU.max, apply_absolute_value=True).then_inc(c_q[1], 1)
                dve.wait_ge(c_q[1], b + 1)
                dve.tensor_scalar(c_gx, c_gx, 1e-5, None, ALU.max).then_inc(c_q[2], 1)
                dve.wait_ge(c_q[2], b + 1)
                dve.tensor_scalar(c_new[:, 0:2], c_gx, gam127[:, 0:1], None, ALU.mult)
                dve.tensor_scalar(c_new[:, 2:4], c_gx, gam127[:, 1:2], None, ALU.mult)
                dve.reciprocal(c_rx, c_gx).then_inc(c_q[3], 1)
                dve.wait_ge(c_q[3], b + 1)
                dve.tensor_scalar(c_sx, c_rx, 127.0, None, ALU.mult).then_inc(c_q[4], 1)
                dve.wait_ge(c_q[4], b + 1)
                for j in range(J):
                    last = dve.tensor_scalar(cXQ[:, j, :], XN[:, j, :], c_sx[:, j:j + 1], MAGIC, ALU.mult, ALU.add)
                last.then_inc(c_xq, 1)
                dve.wait_ge(c_xq, b + 1)
                dve.tensor_scalar(cXB, cXQ, MAGIC, None, ALU.subtract).then_inc(s_xn, 1)

            def ternary(dst, src, scale):
                const(dve.tensor_scalar(src, src, scale, MAGIC, ALU.mult, ALU.add))
                const(dve.tensor_scalar(src, src, MAGIC, -1.0, ALU.subtract, ALU.max))
                const(dve.tensor_scalar(dst, src, 1.0, None, ALU.min))

            dve.wait_ge(s_l0, 16 * 7)
            const(dve.tensor_copy(identb[:, :], ident[:, :]), "identb")
            for lv in range(LV):
                v = [fly[:, k, :].rearrange("r (a i c) -> r a i c", i=2, c=2 ** (LV - 1 - lv))
                     for k in (lv % 2, (lv + 1) % 2)]
                for o in range(2):
                    f = 4 * lv + o
                    const(dve.tensor_scalar(v[1][:, :, o, :], v[0][:, :, 0, :], factors[:, f:f + 1], None, ALU.mult))
                    const(dve.scalar_tensor_tensor(v[1][:, :, o, :], v[0][:, :, 1, :], factors[:, f + 2:f + 3],
                                                   v[1][:, :, o, :], ALU.mult, ALU.add), "fly")
            dve.wait_ge(s_pp, 1)
            const(dve.tensor_copy(b_fold[:, :], PS[0:NS, 1, 0:D]))
            const(dve.tensor_copy(c_fold[:, :], PS[0:NS, 2, 0:D]), "folds")
            ln_stats(MIX, 0)
            ln_apply(MIX, 0)
            dve.wait_ge(s_pp, 2)
            for c in range(C):
                const(dve.tensor_copy(mix[:, c, :], PS[:, 3 + c, 0:D]))
                const(dve.scalar_tensor_tensor(mix[:, c, c * P:(c + 1) * P], ident[:, :], dvec[:, c:c + 1],
                                               PS[:, 3 + c, c * P:(c + 1) * P], ALU.mult, ALU.add), "mix")
            dve.wait_ge(s_l1, 48)
            const(dve.tensor_copy(mask[:, :, :], masku[:, :, :]))
            const(dve.tensor_scalar(mbias[:, :, :], mask[:, :, :], 1.0, -NEG, ALU.subtract, ALU.mult))
            const(dve.tensor_reduce(valid[:, :], mask[:, :, :], AX.X, ALU.max))

            def mixer(b, nxt):
                ln_stats(*nxt)
                ln_apply(*nxt)
                dve.wait_ge(a_mm, b + 1)
                dve.tensor_tensor(batch(b), batch(b), bank(1).rearrange("p (j d) -> p j d", j=J), ALU.add)\
                    .then_inc(s_x, 1)

            over_batches(dve, MIX, mixer)

            dve.wait_ge(s_abs, 3 * B)
            const(dve.tensor_reduce(wsum[:, :], wpart[:, :, :], AX.X, ALU.add), "wsum")
            dve.wait_ge(s_ps, 1)
            const(dve.tensor_scalar(gam[:, :], PS[:, 7, 0:3], 1.0 / (D * HID), 1e-5, ALU.mult, ALU.max))
            const(dve.reciprocal(rgam[:, :], gam[:, :]))
            const(dve.tensor_scalar(gam127[:, :], gam[:, :], 1.0 / 127, None, ALU.mult))

            def clip(b, k):
                w = wstage[:, ds(C * HID * k + C * HID // B * b, C * HID // B)]
                n = 3 * b + k
                dve.tensor_scalar(w, w, rgam[:, k:k + 1], 1.0, ALU.mult, ALU.min).then_inc(s_clip, 1)
                dve.wait_ge(s_clip, 2 * n + 1)
                dve.tensor_scalar(w, w, -1.0, MAGIC, ALU.max, ALU.add).then_inc(s_clip, 1)

            def read_out(b):
                dve.wait_ge(b_o2, b + 1)
                dve.tensor_tensor(batch(b), batch(b), bank(3).rearrange("p (j d) -> p j d", j=J), ALU.add)\
                    .then_inc(s_x, 1)

            def cross(b):
                last = type(b) is int and b == B - 1
                ln_apply(*((FFN, 0) if last else (CROSS, b + 1)))
                dve.wait_ge(b_s, b + 1)
                dve.scalar_tensor_tensor(bSC, PS[:, 1, 0:J * T].rearrange("p (j t) -> p j t", j=J),
                                         1.0 / 16, bc(mbias[:, ds(b, 1), :], [P, J, T]),
                                         ALU.mult, ALU.add).then_inc(b_c, 1)
                dve.wait_ge(b_c, b + 1)
                dve.tensor_reduce(b_nm, bSC, AX.X, ALU.max, negate=True).then_inc(b_m, 1)
                if type(b) is not int or b > 0:
                    read_out(b - 1)
                if not last:
                    ln_stats(*((FFN, 0) if type(b) is int and b == B - 2 else (CROSS, b + 2)))
                clip(b, 0)
                dve.wait_ge(b_e, b + 1)
                dve.reciprocal(b_ri, b_sum).then_inc(b_r, 1)
                dve.wait_ge(b_r, b + 1)
                dve.tensor_tensor(b_rv, b_ri, bc(valid[:, ds(b, 1)], [P, J]), ALU.mult).then_inc(b_v2, 1)
                dve.wait_ge(b_v2, b + 1)
                dve.tensor_tensor(bP, bP, bc(b_rv.unsqueeze(2), [P, J, T]), ALU.mult).then_inc(b_p, 1)
                for k in (1, 2):
                    clip(b, k)

            ln_stats(CROSS, 1)
            cross(0)
            with dve.Fori(1, B - 2) as b:
                cross(b)
            cross(B - 2)
            cross(B - 1)
            read_out(B - 1)

            dve.wait_ge(s_l5, 64)
            ternary(ew[:, :, :], ew[:, :, :], 2.0)
            mark["ew"] = count[0]

            dve.wait_ge(s_l2, 48)

            def widen(b, j):
                u = J * b + j
                dve.wait_ge(c_g, u + 1)
                dve.wait_ge(c_h, u)
                dve.scalar_tensor_tensor(cHG, bank(1, 2), c_cur[:, j:j + 1], gate_b, ALU.mult, ALU.add)\
                    .then_inc(c_gs, 1)
                dve.wait_ge(c_v, u + 1)
                dve.scalar_tensor_tensor(cHV, bank(3, 2), c_cur[:, 2 + j:3 + j], val_b, ALU.mult, ALU.add)\
                    .then_inc(c_vs, 1)

            def step_size(b, j):
                u = J * b + j
                dve.wait_ge(c_h, u + 1)
                dve.tensor_reduce(c_hm, cH, AX.X, ALU.max, apply_absolute_value=True).then_inc(c_a, 1)
                dve.wait_ge(c_a, u + 1)
                dve.tensor_scalar(c_hm, c_hm, 1e-5, None, ALU.max).then_inc(c_s[1], 1)
                dve.wait_ge(c_s[1], u + 1)
                dve.tensor_scalar(c_so[:, j:j + 1], c_hm, gam127[:, 2:3], None, ALU.mult)
                dve.reciprocal(c_rh, c_hm).then_inc(c_s[2], 1)
                dve.wait_ge(c_s[2], u + 1)
                dve.tensor_scalar(c_sh, c_rh, 127.0, None, ALU.mult).then_inc(c_s[3], 1)

            def narrow(b, j):
                u = J * b + j
                dve.wait_ge(c_o, u + 1)
                dve.scalar_tensor_tensor(cY[:, j, :], PS[:, 6, 0:D], c_so[:, j:j + 1], ffo_b[:, :], ALU.mult, ALU.add)\
                    .then_inc(c_y, 1)
                dve.wait_ge(c_y, u + 1)
                last = dve.tensor_tensor(tokens(b, j), tokens(b, j), cY[:, j, :], ALU.add)
                if j == J - 1:
                    last.then_inc(s_x, 1)

            def ffn(b, nxt):
                dve.tensor_copy(c_cur, c_new).then_inc(c_s[0], 1)
                for j in range(J):
                    former = (b, j - 1) if j else (b - 1, J - 1)
                    behind = j > 0 or type(b) is not int or b > 0
                    if j == 0:
                        ln_stats(*nxt)
                        dve.wait_ge(c_s[0], b + 1)
                    widen(b, j)
                    if j == 0:
                        ln_apply(*nxt)
                    else:
                        dve.wait_ge(c_si, J * b + j + 1)
                        dve.wait_ge(c_vs, J * b + j + 1)
                        dve.wait_ge(c_hr, J * b + j)
                        dve.tensor_tensor(cH, cHS, cHV, ALU.mult).then_inc(c_h, 1)
                    step_size(b, j)
                    if behind:
                        narrow(*former)

            over_batches(dve, FFN, ffn)
            narrow(B - 1, J - 1)

            dve.wait_ge(s_l3, 16 * 7)
            dve.wait_ge(s_mfree, NE)

            def self_keys(b, heads):
                dve.wait_ge(d_pq, b + 1)
                for h in heads:
                    last = dve.tensor_scalar(dK[:, h, :], PS[:, 5, 0:S], bqk[:, 2:3], hmask[:, h:h + 1],
                                             ALU.add, ALU.mult)
                if h == NH // 2 - 1:
                    last.then_inc(d_k1, 1)

            def self_values(b):
                dve.wait_ge(d_pv, 8 * b)
                dve.tensor_tensor(dV, bank(6).rearrange("p (j d) -> p j d", j=J),
                                  bc(b_v[:, :].unsqueeze(1), [P, J, D]), ALU.add).then_inc(d_vv, 1)

            def self_finish(b):
                dve.wait_ge(d_y, b + 1)
                dve.tensor_tensor(dY, bank(2).rearrange("p (j d) -> p j d", j=J),
                                  bc(b_o[:, :].unsqueeze(1), [P, J, D]), ALU.add).then_inc(d_yb, 1)
                dve.wait_ge(d_yb, b + 1)
                dve.tensor_tensor(batch(b), batch(b), dY, ALU.add).then_inc(s_x, 1)

            def square_keys(b):
                for seg in range(3):
                    n = T if seg == 1 else P
                    dve.wait_ge(e_sq, 3 * b + seg + 1)
                    dve.tensor_reduce(e_ks[0:n, seg, :], eSQ[0:n, seg, :].rearrange("p (g d) -> p g d", g=XG),
                                      AX.X, ALU.add).then_inc(e_ssq, 1)

            def turn_keys(b):
                for seg in range(3):
                    n = T if seg == 1 else P
                    dve.wait_ge(e_rk, 3 * b + seg + 1)
                    kr = eKR[0:n, seg, :].rearrange("p (g d) -> p g d", g=XG)
                    dve.tensor_tensor(kr, kr, bc(e_rks[0:n, seg, :].unsqueeze(2), [n, XG, XD]), ALU.mult)\
                        .then_inc(e_kn, 1)
                for seg in range(3):
                    n = T if seg == 1 else P
                    dve.wait_ge(e_kn, 3 * b + seg + 1)
                    kr = eKR[0:n, seg, :].rearrange("p (g d) -> p g d", g=XG)
                    kf = eKF[0:n, seg, :].rearrange("p (g d) -> p g d", g=XG)
                    tab = kw[0:n, :].unsqueeze(1) if seg == 1 else cosk[:, seg // 2, :].unsqueeze(1)
                    dve.tensor_tensor(kf, kr, bc(tab, [n, XG, XD]), ALU.mult).then_inc(e_ka, 1)
                for k, seg in enumerate((0, 2)):
                    dve.wait_ge(e_ka, 3 * b + seg + 1)
                    dve.wait_ge(e_kb, 2 * b + k + 1)
                    dve.tensor_tensor(eKF[:, seg, :], eKF[:, seg, :], eKB[:, k, :], ALU.add).then_inc(e_kf, 1)

            def self_attention(b, nxt):
                def masked_max(i):
                    j, u = i // 4, 8 * b + i
                    n = (j + 1) * P
                    if i >= 2:
                        dve.wait_ge(d_e, u - 1)
                    held(dve, d_s, u + 1)
                    for hh in range(4):
                        last = dve.tensor_tensor_reduce(
                            dSS[:, i % 2, hh, 0:n], PS[:, 4 + 2 * (i % 2) + hh // 2, (hh % 2) * S:(hh % 2) * S + n],
                            causal[:, j, 0:n], 1.0, LOWEST, ALU.add, ALU.max, d_max[:, i % 2, hh:hh + 1])
                    last.then_inc(d_mx, 1)
                    dve.wait_ge(d_mx, u + 1)
                    dve.tensor_scalar(d_neg[:, i % 2, :], d_max[:, i % 2, :], -0.25, None, ALU.mult).then_inc(d_nm, 1)

                def turn(i):
                    u = 8 * b + i
                    if i % 2:
                        dve.wait_ge(d_t, u + 1)
                        dve.wait_ge(d_pv, u - 1)
                        n = 4 * (1 + i // 4) * P
                        dve.tensor_copy(dPT[:, i % 2, :, :].rearrange("p a b -> p (a b)")[:, 0:n],
                                        bank(1, 2)[:, 0:n]).then_inc(d_pt, 1)

                masked_max(0)
                masked_max(1)
                if type(b) is not int or b > 0:
                    self_finish(b - 1)
                for i in range(8):
                    if i + 2 < 8:
                        masked_max(i + 2)
                    if i == 7 and nxt[0] == SELF:
                        self_keys(nxt[1], range(6))
                    turn(i)
                    if i == 1:
                        ln_stats(*nxt)
                    if i == 3:
                        ln_apply(*nxt)
                if nxt[0] == SELF:
                    self_keys(nxt[1], range(6, NH // 2))
                    self_values(nxt[1])
                dve.wait_ge(d_e, 8 * b + 8)
                dve.reciprocal(d_ri, d_sum).then_inc(d_r, 1)
                dve.wait_ge(d_r, b + 1)
                if nxt[0] == HYBRID:
                    square_keys(0)
                dve.wait_ge(d_pv, 8 * b + 8)
                dve.tensor_tensor(dO.rearrange("p j (h k) -> p (j h) k", k=DH),
                                  bank(3).rearrange("p (h k) -> p h k", k=DH),
                                  bc(d_ri.unsqueeze(2), [P, J * NH, DH]), ALU.mult).then_inc(d_o, 1)

            const(dve.tensor_scalar(bk_head[:, :], hmask[:, :], bqk[:, 3:4], None, ALU.mult), "bk_head")
            self_keys(0, range(NH // 2))
            self_values(0)
            dve.wait_ge(s_l4, 16 * 13)
            const(dve.tensor_scalar(kw[:, :], kw[:, :], float(XD) ** 0.5, None, ALU.mult))
            const(dve.tensor_scalar(kws[:, :], kws[:, :], float(XD) ** 0.5, None, ALU.mult))
            for dst, tab, w in ((cosq, cosT, qw), (sinq, sinT, qws), (cosk, cosT, kw), (sink, sinT, kws)):
                const(dve.tensor_tensor(dst[:, :, :], tab[:, :, :], bc(w[:, :].unsqueeze(1), [P, J, XD]), ALU.mult),
                      "tables")

            over_batches(dve, SELF, self_attention)
            turn_keys(0)
            self_finish(B - 1)

            def hybrid_finish(b):
                dve.wait_ge(e_y, J * b + J)
                dve.tensor_tensor(batch(b), batch(b), bank(0).rearrange("p (j d) -> p j d", j=J), ALU.add)\
                    .then_inc(s_x, 1)

            def hybrid(b, nxt):
                def scale_query(i):
                    j, u = i // XG, 8 * b + i
                    dve.wait_ge(e_qt, u)
                    dve.wait_ge(e_qr, u + 1)
                    dve.tensor_tensor(eQA.rearrange("p (g d) -> p g d", g=GH),
                                      eQR.rearrange("p (g d) -> p g d", g=GH),
                                      bc(cosq[:, j, :].unsqueeze(1), [P, GH, XD]), ALU.mult).then_inc(e_qa, 1)

                def sum_squares(i):
                    u = 8 * b + i
                    dve.wait_ge(e_qs, u + 1)
                    dve.tensor_reduce(e_q2, eQS.rearrange("p (g d) -> p g d", g=GH), AX.X, ALU.add)\
                        .then_inc(e_qq, 1)

                def turn_query(i):
                    u = 8 * b + i
                    dve.wait_ge(e_qa, u + 1)
                    dve.wait_ge(e_qb, u + 1)
                    dve.tensor_tensor(eQA, eQA, eQB, ALU.add).then_inc(e_qf, 1)

                def masked_max(i, heads):
                    j, u = i // XG, 8 * b + i
                    n = KEYS if j else P + T
                    dve.wait_ge(e_nm, u)
                    after(dve, e_t, u - 1)
                    for hh in heads:
                        held(dve, e_s, GH * u + hh + 1)
                        dve.tensor_tensor_reduce(eP[:, i % 2, hh, 0:n], PS[:, 3 + hh % 2, 0:n], kmask[:, j, 0:n],
                                                 1.0, LOWEST, ALU.add, ALU.max, e_max[:, hh:hh + 1]).then_inc(e_mx, 1)
                    if GH - 1 not in heads:
                        return
                    dve.wait_ge(e_mx, GH * (u + 1))
                    dve.wait_ge(e_rq, u + 1)
                    dve.scalar_tensor_tensor(e_neg[:, i % 2, :], e_max, -1.0, e_rqs[:, i % 3, :], ALU.mult, ALU.mult)\
                        .then_inc(e_nm, 1)

                def normalise(i):
                    j, u = i // XG, 8 * b + i
                    n = KEYS if j else P + T
                    dve.wait_ge(e_e, u + 1)
                    dve.reciprocal(e_inv, e_sum[:, i % 2, :]).then_inc(e_ri, 1)
                    dve.wait_ge(e_ri, u + 1)
                    for hh in range(GH):
                        last = dve.tensor_scalar(eP[:, i % 2, hh, 0:n], eP[:, i % 2, hh, 0:n], e_inv[:, hh:hh + 1], None, ALU.mult)
                    last.then_inc(e_p, 1)

                def turn_probs(i):
                    u = 8 * b + i
                    dve.wait_ge(e_t, u + 1)
                    dve.wait_ge(e_pv, u)
                    dve.tensor_copy(ePT[0:T, 1, :], PS[0:T, 6, :]).then_inc(e_ptd, 1)
                    if i >= XG:
                        dve.tensor_copy(ePT[:, 2, :], PS[:, 7, :]).then_inc(e_ptd, 1)

                for i in range(2):
                    scale_query(i)
                    turn_query(i)
                    sum_squares(i)
                if type(b) is not int or b > 0:
                    hybrid_finish(b - 1)
                masked_max(0, (0, 1))
                masked_max(0, (2, 3))
                for i in range(8):
                    if i >= 1:
                        turn_probs(i - 1)
                        if i + 1 < 8:
                            sum_squares(i + 1)
                    if i + 2 < 8:
                        scale_query(i + 2)
                    if i == 3:
                        ln_stats(*nxt)
                    if i == 4:
                        ln_apply(*nxt)
                    if i + 1 < 8:
                        masked_max(i + 1, (0, 1))
                    if i + 2 < 8:
                        turn_query(i + 2)
                    normalise(i)
                    if i + 1 < 8:
                        masked_max(i + 1, (2, 3))
                turn_probs(7)
                if nxt[0] == HYBRID:
                    square_keys(nxt[1])
                    turn_keys(nxt[1])

            over_batches(dve, HYBRID, hybrid)
            hybrid_finish(B - 1)

            ln_stats(MOE, 1)
            dve.wait_ge(s_x, MOE * B)
            dve.wait_ge(s_cleared, 16)
            const(dve.tensor_scalar(before, causal[:, 0, 0:P], 0.0, None, ALU.is_lt))
            const(dve.tensor_copy(onesb, ones[:, :]))
            const(dve.tensor_scalar(lower[0:NE, :], causal[0:NE, 0, 0:NE], 0.0, None, ALU.is_lt))
            const(dve.tensor_tensor(upto[0:NE, :], lower[0:NE, :], ident[0:NE, 0:NE], ALU.add), "routing")

            def route(b):
                if type(b) is not int or b + 1 < B:
                    dve.wait_ge(f_row, b + 1)
                    ln_apply(MOE, b + 1)
                dve.wait_ge(f_e, b)
                dve.wait_ge(f_l, b + 1)
                dve.tensor_copy(fLG, PS[:, 7, 0:J * NE].rearrange("p (j e) -> p j e", j=J)).then_inc(f_lg, 1)
                if type(b) is not int or b + 2 < B:
                    ln_stats(MOE, b + 2)
                held(dve, f_lg, b + 1)
                for j in range(J):
                    last = dve.max(f_m8[:, j, :], fLG[:, j, :])
                last.then_inc(f_m, 1)
                dve.wait_ge(f_m, b + 1)
                dve.tensor_scalar(f_neg, f_m8[:, :, 0], -1.0, None, ALU.mult).then_inc(f_nm, 1)
                for j in range(J):
                    last = dve.max_index(f_i8[:, j, :], f_m8[:, j, :], fLG[:, j, :])
                last.then_inc(f_i, 1)
                dve.wait_ge(f_i, b + 1)
                dve.tensor_copy(f_if_, f_i8[:, :, 0]).then_inc(f_if, 1)
                dve.wait_ge(f_if, b + 1)
                for j in range(J):
                    last = dve.tensor_scalar(fOH[:, ds(J * b + j, 1), :].rearrange("p a e -> p (a e)"),
                                             iota[:, 0:NE], f_if_[:, j:j + 1], None, ALU.is_equal)
                last.then_inc(f_oh, 1)

            route(0)
            with dve.Fori(1, B - 3, 2) as b:
                route(b)
                route(b + 1)
            for b in range(B - 3, B):
                route(b)

            dve.wait_ge(f_count, 1)
            const(dve.tensor_scalar(f_tiles, PS[0:NE, 2, 0:1], 1.0 / HT, 0.5 - 0.5 / HT, ALU.mult, ALU.add))
            const(dve.tensor_scalar(f_tiles, f_tiles, MAGIC, None, ALU.add))
            const(dve.tensor_scalar(f_tiles, f_tiles, MAGIC, None, ALU.subtract))
            const(dve.tensor_scalar(tilesB[0:NE, :], ones[0:NE, :], f_tiles, None, ALU.mult), "tiles")
            dve.wait_ge(f_base, 1)
            const(dve.tensor_copy(f_incl, PS[0:NE, 4, 0:1]))
            const(dve.tensor_scalar(past[0:NE, :], iota[0:NE, :], f_incl, None, ALU.is_ge), "past")
            const(dve.tensor_scalar(fBASE, PS[:, 3, 0:NE], float(HT), None, ALU.mult))
            dve.wait_ge(f_rank, 1)
            const(dve.tensor_tensor(fSLOT, PS[:, 1, :].rearrange("p (i e) -> p i e", e=NE),
                                    bc(fBASE.unsqueeze(1), [P, TOK, NE]), ALU.add))
            const(dve.tensor_tensor(fSLOT, fSLOT, fOH, ALU.mult))
            const(dve.tensor_reduce(f_slot, fSLOT, AX.X, ALU.add))
            const(dve.tensor_copy(f_slotu, f_slot), "slots")
            dve.wait_ge(f_tex, 1)
            const(dve.tensor_scalar(f_ex, PS[0:1, 5, 0:TILES], float(NE - 1), None, ALU.min))
            const(dve.tensor_copy(f_exu, f_ex), "experts")
            dve.wait_ge(f_e, B)
            const(dve.reciprocal(f_w, f_sm))

            def remainder(k, u):
                dve.wait_ge(f_xh, u + 1)
                after(dve, f_xl, u - RING + 1)
                dve.tensor_tensor(sR[:, k, :], bank(k), sXH[:, k].rearrange("p t n -> p (t n)"), ALU.subtract) \
                    .then_inc(f_r1, 1)

            def scale(k, n, u):
                after(dve, s_stored[k], 16 * n)
                dve.wait_ge(f_y, u + 1)
                dve.tensor_tensor(sY[:, k], bank(4 + 2 * (k % 2), 2)[0:HT, :].rearrange("p (t d) -> p t d", t=QT),
                                  bc(esc[0:HT, :].unsqueeze(1), [HT, QT, D]), ALU.mult).then_inc(f_yo, 1)

            def experts(n):
                for k in range(RING):
                    u = RING * n + k
                    remainder(k, u)
                    if k >= 3:
                        scale(k - 3, n, u - 3)
                    elif type(n) is not int or n > 0:
                        scale(k + 1, n - 1, u - 3)

            over_rounds(dve, experts)
            for k in range(1, RING):
                scale(k, ROUNDS - 1, RING * (ROUNDS - 1) + k)
            for b in range(B):
                for j in range(J):
                    i = J * b + j
                    if i % (TOK // 4) == 0:
                        dve.wait_ge(s_back[i // (TOK // 4)], 4 * TOK)
                    last = dve.scalar_tensor_tensor(X[:, b, j, :], fBACK[:, i, :], f_w[:, i:i + 1], X[:, b, j, :],
                                                    ALU.mult, ALU.add)
                last.then_inc(s_x, 1)

        @block.sync
        def _(sp):
            sp.dma_start(X[:, :, :, :], I["x"].rearrange("b (j p) d -> p b j d", p=P)).then_inc(s_lx, 16)
            for dst, name in ((wbrT, "wbrT"), (wcrT, "wcrT"), (wcm, "wcm"), (ident, "ident")):
                sp.dma_start(dst[:, :], I[name]).then_inc(s_l0, 16)
            sp.dma_start(fly[:, 0, :], I["wbs"]).then_inc(s_l0, 16)
            sp.dma_start(factors[:, :], I["factors"].partition_broadcast(R)).then_inc(s_l0, 16)
            sp.dma_start(dvec[:, :], I["dvec"]).then_inc(s_l0, 16)
            sp.dma_start(ctxT[:, :, :, :], I["ctxT"].rearrange("(c p) b t -> p c b t", p=P)).then_inc(s_l1, 16)
            sp.dma_start(ctxN[:, :, :], I["ctx"].rearrange("b t d -> t b d")).then_inc(s_l1, 16)
            sp.dma_start(masku[:, :, :], I["mask"].partition_broadcast(P)).then_inc(s_l1, 16)
            for k, name in enumerate(("gateT", "valT", "outT")):
                sp.dma_start(wstage[:, C * HID * k:C * HID * (k + 1)].rearrange("p (c n) -> p c n", n=I[name].shape[1]),
                             I[name].rearrange("(c p) n -> p c n", p=P)).then_inc(s_lw, 16)
            sp.dma_start(gate_b, I["gate_b"].partition_broadcast(P)).then_inc(s_l2, 16)
            sp.dma_start(val_b, I["val_b"].partition_broadcast(P)).then_inc(s_l2, 16)
            sp.dma_start(ffo_b[:, :], I["ffo_b"].partition_broadcast(P)).then_inc(s_l2, 16)
            sp.dma_start(ew[:, :, :], I["ewT"].rearrange("(c p) n -> p c n", p=P)).then_inc(s_l5, 16)
            sp.dma_start(rwT[:, :, :], I["rwT"].rearrange("(c p) n -> p c n", p=P)).then_inc(s_l5, 16)
            sp.dma_start(iota[:, :], I["iota"].partition_broadcast(P)).then_inc(s_l5, 16)
            sp.dma_start(esc[:, :], I["esc"].partition_broadcast(P)).then_inc(s_l5, 16)
            sp.dma_start(w_in[:, :, :], I["w_in"].rearrange("(c p) n -> p c n", p=P)).then_inc(s_l3, 16)
            sp.dma_start(w_out[:, :, :], I["w_out"].rearrange("(c p) n -> p c n", p=P)).then_inc(s_l3, 16)
            sp.dma_start(bqk[:, :], I["bqk"]).then_inc(s_l3, 16)
            sp.dma_start(b_v[:, :], I["b_v"].partition_broadcast(P)).then_inc(s_l3, 16)
            sp.dma_start(b_o[:, :], I["b_o"].partition_broadcast(P)).then_inc(s_l3, 16)
            sp.dma_start(hmask[:, :], I["hmask"]).then_inc(s_l3, 16)
            sp.dma_start(causal[:, :, :], I["causal"]).then_inc(s_l3, 16)
            for dst, name in ((wq, "wq"), (wk, "wk"), (wv, "wv"), (wkc, "wkc"), (wvc, "wvc"), (wo, "wo"),
                              (cosT, "cos"), (sinT, "sin")):
                sp.dma_start(dst[:, :, :], I[name].rearrange("(c p) n -> p c n", p=P)).then_inc(s_l4, 16)
            for dst, name in ((qw, "qw"), (qws, "qws"), (kw, "kw"), (kws, "kws")):
                sp.dma_start(dst[:, :], I[name].partition_broadcast(P)).then_inc(s_l4, 16)
            sp.dma_start(kmask[:, :, :], I["kmask"]).then_inc(s_l4, 16)
            for e in range(4):
                sp.dma_start(mring[:, e, :], I["masksT"][e]).then_inc(s_mld[e], 16)
            with sp.Fori(1, NE // 4) as n:
                for e in range(4):
                    sp.wait_ge(s_mfree, 4 * n + (e - 3))
                    sp.dma_start(mring[:, e, :], I["masksT"][ds(4 * n + e, 1)].rearrange("a p n -> p (a n)"))\
                        .then_inc(s_mld[e], 16)
            sp.wait_ge(s_zero, 1)
            sp.dma_start(rows.rearrange("(t p) d -> p t d", p=P), bc(zeros.unsqueeze(1), [P, TILES * HT // P, D]))\
                .then_inc(s_cleared, 16)
            group_rows = rows.rearrange("(g t p) d -> g p t d", t=2, p=P)

            def groups(n):
                for k in range(RING):
                    g = RING * n + k
                    after(sp, f_tp, g - RING + 1)
                    sp.dma_start(sIN[:, k], group_rows[ds(g, 1)].rearrange("a p t d -> p (a t) d")) \
                        .then_inc(s_rows[k], 16)

            sp.wait_ge(s_sorted, 16 * TOK)
            over_rounds(sp, groups)
            with sp.Fori(0, B) as b:
                sp.wait_ge(s_x, MOE * B + b + 1)
                sp.dma_start(out[ds(b, 1)].rearrange("a (j p) d -> p (a j) d", p=P),
                             X[:, ds(b, 1), :, :].rearrange("p a j d -> p (a j) d")).then_inc(s_out, 16)
            sp.wait_ge(s_out, 16 * B)


        @block.gpsimd
        def _(pool):
            pool.memset(halves[:, :], -0.5).then_inc(s_pc, 1)
            pool.memset(ones[:, :], 1.0).then_inc(s_pc, 1)
            pool.memset(magic[:, :], MAGIC).then_inc(s_pc, 1)
            pool.memset(unmagic[:, :], -MAGIC).then_inc(s_pc, 1)
            pool.wait_ge(s_pc, 4)

            def rstds(phase, b):
                n = phase * B + b
                held(pool, s_mv, n + 1)
                pool.tensor_scalar(ve[:, :], mv[:, :, 1], LN_EPS, None, ALU.add).then_inc(s_ve, 1)
                pool.wait_ge(s_ve, n + 1)
                pool.tensor_tensor(rstd[:, :], ve[:, :], halves[:, 0:J], ALU.pow).then_inc(s_rs, 1)

            rstds(MIX, 0)
            for phase in (MIX, CROSS):
                over_batches(pool, phase, lambda b, nxt: rstds(*nxt))

            def ffn(b, nxt):
                rstds(*nxt)
                for j in range(J):
                    u = J * b + j
                    if j == 0:
                        pool.wait_ge(c_si, u + 1)
                        pool.wait_ge(c_vs, u + 1)
                        pool.wait_ge(c_hr, u)
                        pool.tensor_tensor(cH, cHS, cHV, ALU.mult).then_inc(c_h, 1)
                    for e in (2 * j, 2 * j + 1):
                        pool.wait_ge(s_mld[e], 16 * b + 16)
                        pool.tensor_tensor(EW[:, ds(4 * b + e, 1), :].rearrange("p a n -> p (a n)"),
                                           mring[:, e, :], ew[:, :, :].rearrange("p c n -> p (c n)"),
                                           ALU.mult).then_inc(s_mfree, 1)

            pool.wait_ge(s_c, mark["ew"])
            pool.wait_ge(s_tern, 3 * B)
            over_batches(pool, FFN, ffn)
            pool.wait_ge(s_mfree, NE)
            pool.memset(zeros, 0.0).then_inc(s_zero, 1)
            over_batches(pool, SELF, lambda b, nxt: rstds(*nxt))

            def turn_keys(b):
                for seg in range(3):
                    n = T if seg == 1 else P
                    pool.wait_ge(e_kr, 3 * b + seg + 1)
                    pool.tensor_tensor(eSQ[0:n, seg, :], eKR[0:n, seg, :], eKR[0:n, seg, :], ALU.mult)\
                        .then_inc(e_sq, 1)
                for seg in range(3):
                    n = T if seg == 1 else P
                    held(pool, e_ssq, 3 * b + seg + 1)
                    pool.tensor_scalar(e_kp[0:n, seg, :], e_ks[0:n, seg, :], RMS_EPS * XD, None, ALU.add)\
                        .then_inc(e_ve, 1)
                    pool.wait_ge(e_ve, 3 * b + seg + 1)
                    pool.tensor_tensor(e_rks[0:n, seg, :], e_kp[0:n, seg, :], halves[0:n, 0:XG], ALU.pow)\
                        .then_inc(e_rk, 1)
                for k, seg in enumerate((0, 2)):
                    pool.wait_ge(e_kn, 3 * b + seg + 1)
                    kn = eKR[:, seg, :].rearrange("p (g u v) -> p g u v", g=XG, u=2)
                    kb = eKB[:, k, :].rearrange("p (g u v) -> p g u v", g=XG, u=2)
                    for u in range(2):
                        last = pool.tensor_tensor(kb[:, :, u, :], kn[:, :, 1 - u, :],
                                                  bc(sink[:, k, 64 * u:64 * u + 64].unsqueeze(1), [P, XG, 64]),
                                                  ALU.mult)
                    last.then_inc(e_kb, 1)

            def hybrid(b, nxt):
                def query(i):
                    j, u = i // XG, 8 * b + i
                    pool.wait_ge(e_qr, u + 1)
                    pool.wait_ge(e_qf, u)
                    q = eQR.rearrange("p (g u v) -> p g u v", g=GH, u=2)
                    qb = eQB.rearrange("p (g u v) -> p g u v", g=GH, u=2)
                    for h in range(2):
                        last = pool.tensor_tensor(qb[:, :, h, :], q[:, :, 1 - h, :],
                                                  bc(sinq[:, j, 64 * h:64 * h + 64].unsqueeze(1), [P, GH, 64]),
                                                  ALU.mult)
                    last.then_inc(e_qb, 1)
                    pool.wait_ge(e_qq, u)
                    pool.tensor_tensor(eQS, eQR, eQR, ALU.mult).then_inc(e_qs, 1)
                    held(pool, e_qq, u + 1)
                    pool.tensor_scalar(e_q3, e_q2, RMS_EPS * XD, None, ALU.add).then_inc(e_qv, 1)
                    pool.wait_ge(e_qv, u + 1)
                    pool.wait_ge(e_e, u - 2 if i >= 3 else 8 * b)
                    pool.tensor_tensor(e_rqs[:, i % 3, :], e_q3, halves[:, 0:GH], ALU.pow).then_inc(e_rq, 1)

                for i in range(8):
                    query(i)
                    if i == 5:
                        rstds(*nxt)
                if nxt[0] == HYBRID:
                    turn_keys(nxt[1])

            turn_keys(0)
            over_batches(pool, HYBRID, hybrid)

            with pool.Fori(1, B) as b:
                rstds(MOE, b)
            pool.wait_ge(s_c, mark["slots"])
            pool.wait_ge(f_row, B)
            for i in range(TOK):
                pool.indirect_dma_start(rows[:, :], bass.IndirectOffsetOnAxis(ap=f_slotu[:, i:i + 1], axis=0),
                                        fROW[:, i, :], None).then_inc(s_sorted, 16)

            def low_parts(n):
                for k in range(RING):
                    u = RING * n + k
                    after(pool, f_y, u - RING + 1)
                    pool.wait_ge(f_xm, u + 1)
                    pool.tensor_tensor(sXL[:, k].rearrange("p t n -> p (t n)"), sR[:, k, :],
                                       sXM[:, k].rearrange("p t n -> p (t n)"), ALU.subtract).then_inc(f_xl, 1)

            over_rounds(pool, low_parts)
            for k in range(RING):
                pool.wait_ge(s_stored[k], 16 * ROUNDS)
            for i in range(TOK):
                pool.indirect_dma_start(fBACK[:, i, :], None, results[:, :],
                                        bass.IndirectOffsetOnAxis(ap=f_slotu[:, i:i + 1], axis=0))\
                    .then_inc(s_back[i // (TOK // 4)], 16)

        @block.scalar
        def _(act):
            def xt_copy(nxt, used=(), at=0):
                phase, b = nxt
                for s, value in used:
                    act.wait_ge(s, value)
                act.wait_ge(s_xtp, phase * B + b + 1)
                src, dst = (bank(at), XT[:, :, :].rearrange("p c s -> p (c s)")) if phase != FFN else \
                    (pXT[:, 0:D].bitcast(BF), cXT.rearrange("p c s -> p (c s)"))
                act.activation(dst, src, ACT.Copy).then_inc(s_xt, 1)

            act.wait_ge(s_pc, 4)
            xt_copy((MIX, 0))

            def mixer(b, nxt):
                xt_copy(nxt, [(a_mm, b + 1)])
                for k in range(3):
                    act.wait_ge(s_lw, 48)
                    act.wait_ge(s_abs, 3 * b + k)
                    act.activation(junk, wstage[:, ds(C * HID * k + C * HID // B * b, C * HID // B)], ACT.Abs,
                                   accum_out=wpart[:, k, ds(b, 1)]).then_inc(s_abs, 1)

            over_batches(act, MIX, mixer)

            def cross(b, nxt):
                def ready(k):
                    n = 3 * b + k
                    at = ds(C * HID * k + C * HID // B * b, C * HID // B)
                    act.wait_ge(s_clip, 2 * n + 2)
                    act.activation(ternaries[:, at], wstage[:, at], ACT.Identity, bias=unmagic[:, 0:1])\
                        .then_inc(s_tern, 1)

                act.wait_ge(b_m, b + 1)
                act.wait_ge(b_t, b)
                for j in range(J):
                    last = act.activation(bP[:, j, :], bSC[:, j, :], ACT.Exp, bias=b_nm[:, j:j + 1],
                                          accum_out=b_sum[:, j:j + 1])
                last.then_inc(b_e, 1)
                xt_copy(nxt, [(b_s, b + 1)])
                act.wait_ge(b_t, b + 1)
                act.wait_ge(b_o2, b)
                act.activation(bPT[0:T, :], PS[0:T, 2, 0:S], ACT.Copy).then_inc(b_tc, 1)
                for k in range(3):
                    ready(k)

            over_batches(act, CROSS, cross)

            def turned(b, j):
                u = J * b + j
                act.wait_ge(c_t, u + 1)
                act.wait_ge(c_o, u)
                act.activation(cHT.rearrange("p a b -> p (a b)"), bank(5).bitcast(BF), ACT.Copy).then_inc(c_ht, 1)

            def ffn(b, nxt):
                for j in range(J):
                    u = J * b + j
                    act.wait_ge(c_gs, u + 1)
                    act.activation(cHS, cHG, ACT.Silu).then_inc(c_si, 1)
                    if j == 1:
                        xt_copy(nxt, [(c_v, J * b + 2)])
                        turned(b, 0)
                    elif type(b) is not int or b > 0:
                        turned(b - 1, 1)
                    act.wait_ge(c_hq, u)
                    act.wait_ge(c_s[3], u + 1)
                    act.activation(cHR, cH, ACT.Identity, bias=magic[:, 0:1], scale=c_sh).then_inc(c_hr, 1)
                    act.wait_ge(c_hr, u + 1)
                    act.wait_ge(c_t, u)
                    act.activation(cHQ, cHR, ACT.Identity, bias=unmagic[:, 0:1]).then_inc(c_hq, 1)

            over_batches(act, FFN, ffn)
            turned(B - 1, 1)
            act.wait_ge(s_l3, 16 * 7)
            act.wait_ge(s_mfree, NE)

            def self_queries(b):
                act.wait_ge(d_pq, b + 1)
                for m in range(2):
                    last = act.activation(dQ[:, m, :], PS[:, 4, m * S:(m + 1) * S], ACT.Identity, bias=bqk[:, m:m + 1])
                last.then_inc(d_q, 1)
                for h in range(NH // 2):
                    last = act.activation(dK[:, NH // 2 + h, :], PS[:, 7, 0:S], ACT.Identity,
                                          bias=bk_head[:, h:h + 1], scale=hmask[:, h:h + 1])
                last.then_inc(d_k2, 1)

            def self_finish(b):
                act.wait_ge(d_ot, b + 1)
                act.activation(dOT.rearrange("p c s -> p (c s)"), bank(1), ACT.Copy).then_inc(d_oc, 1)

            def raw_keys(b, seg, at=1):
                n = T if seg == 1 else P
                act.wait_ge(e_k, 3 * b + seg + 1)
                act.wait_ge(e_kt, 3 * b)
                act.activation(eKR[0:n, seg, :], PS[0:n, at, :], ACT.Copy).then_inc(e_kr, 1)

            def context(b):
                act.wait_ge(e_v, 3 * b)
                act.activation(eCT[:, :, :], ctxT[:, :, ds(b, 1), :].rearrange("p c a t -> p c (a t)"), ACT.Copy)\
                    .then_inc(e_ct, 1)

            def self_attention(b, nxt):
                def exps(i):
                    j, u = i // 4, 8 * b + i
                    n = (j + 1) * P
                    act.wait_ge(d_nm, u + 1)
                    if i >= 2:
                        act.wait_ge(d_t, u - 1)
                    for hh in range(4):
                        h = j * NH + 4 * (i % 4) + hh
                        last = act.activation(dP[:, i % 2, hh, 0:n], dSS[:, i % 2, hh, 0:n], ACT.Exp,
                                              bias=d_neg[:, i % 2, hh:hh + 1], scale=0.25,
                                              accum_out=d_sum[:, h:h + 1])
                    last.then_inc(d_e, 1)

                if type(b) is not int or b > 0:
                    self_finish(b - 1)
                exps(0)
                for i in range(8):
                    if i + 1 < 8:
                        exps(i + 1)
                    if i % 2 == 0:
                        u = 8 * b + i
                        act.wait_ge(d_t, u + 1)
                        if i >= 2:
                            act.wait_ge(d_pv, u - 1)
                        n = 4 * (1 + i // 4) * P
                        act.activation(dPT[:, 0, :, :].rearrange("p a b -> p (a b)")[:, 0:n],
                                       bank(1, 2)[:, 0:n], ACT.Copy).then_inc(d_pt, 1)
                    if i == 4:
                        xt_copy(nxt, [(d_pq, b + 1)])
                if nxt[0] == SELF:
                    self_queries(nxt[1])
                else:
                    context(0)
                    for seg in range(3):
                        raw_keys(0, seg, 4 + seg)

            act.wait_ge(s_c, mark["bk_head"])
            self_queries(0)
            over_batches(act, SELF, self_attention)
            self_finish(B - 1)

            def hybrid(b, nxt):
                def raw_query(i):
                    u = 8 * b + i
                    act.wait_ge(e_q, u + 1)
                    act.wait_ge(e_qs, u)
                    act.wait_ge(e_qf, u)
                    act.activation(eQR, PS[:, 1, :], ACT.Copy).then_inc(e_qr, 1)

                def query(i):
                    u = 8 * b + i
                    act.wait_ge(e_qt, u + 1)
                    act.wait_ge(e_s, GH * u)
                    act.activation(eQT, PS[:, 2, :], ACT.Copy).then_inc(e_qc, 1)

                def exps(i):
                    j, u = i // XG, 8 * b + i
                    n = KEYS if j else P + T
                    act.wait_ge(e_nm, u + 1)
                    for hh in range(GH):
                        last = act.activation(eP[:, i % 2, hh, 0:n], eP[:, i % 2, hh, 0:n], ACT.Exp,
                                              bias=e_neg[:, i % 2, hh:hh + 1], scale=e_rqs[:, i % 3, hh:hh + 1],
                                              accum_out=e_sum[:, i % 2, hh:hh + 1])
                    last.then_inc(e_e, 1)

                def outputs(i):
                    u = 8 * b + i
                    j, g = i // XG, i % XG
                    act.wait_ge(e_pv, u + 1)
                    if i == 0:
                        act.wait_ge(e_y, J * b)
                    act.activation(eOT[:, GH * g:GH * g + GH, j * P:(j + 1) * P],
                                   PS[:, 0, :].rearrange("p (h s) -> p h s", h=GH), ACT.Copy).then_inc(e_oc, 1)

                raw_query(0)
                for seg in range(3):
                    n = T if seg == 1 else P
                    act.wait_ge(e_v, 3 * b + seg + 1)
                    act.activation(eV[0:n, seg, :], PS[0:n, 5 + seg, :], ACT.Copy).then_inc(e_vr, 1)
                for seg in range(3):
                    n = T if seg == 1 else P
                    at = (0, P, P + T)[seg]
                    act.wait_ge(e_kt, 3 * b + seg + 1)
                    act.activation(eKT[:, :, at:at + n],
                                   PS[:, 2 + seg, 0:XG * n].rearrange("p (g n) -> p g n", g=XG),
                                   ACT.Copy).then_inc(e_kc, 1)
                query(0)
                raw_query(1)

                def turn(i):
                    u = 8 * b + i
                    act.wait_ge(e_t, u + 1)
                    act.wait_ge(e_pv, u)
                    act.activation(ePT[:, 0, :], PS[:, 5, :], ACT.Copy).then_inc(e_pta, 1)

                for i in range(8):
                    if i >= 1:
                        turn(i - 1)
                    if i + 1 < 8:
                        query(i + 1)
                    if i + 2 < 8:
                        raw_query(i + 2)
                    exps(i)
                    if i == 5:
                        xt_copy(nxt, [(e_q, 8 * b + 8)], 1)
                        if nxt[0] == HYBRID:
                            context(nxt[1])
                    if i >= 1:
                        outputs(i - 1)
                    if nxt[0] == HYBRID and i >= 6:
                        raw_keys(nxt[1], i - 6)
                turn(7)
                if nxt[0] == HYBRID:
                    raw_keys(nxt[1], 2)
                outputs(7)

            over_batches(act, HYBRID, hybrid)

            def keep(b):
                act.wait_ge(s_xn, MOE * B + b + 1)
                act.activation(fROW[:, ds(J * b, J), :], XN[:, :, :], ACT.Copy).then_inc(f_row, 1)

            def route(b, nxt):
                if nxt[0] == MOE:
                    keep(nxt[1])
                    xt_copy(nxt, [(f_l, b + 1)])
                act.wait_ge(f_nm, b + 1)
                for j in range(J):
                    last = act.activation(fE[:, j, :], fLG[:, j, :], ACT.Exp, bias=f_neg[:, j:j + 1],
                                          accum_out=f_sm[:, ds(J * b + j, 1)])
                last.then_inc(f_e, 1)

            keep(0)
            over_batches(act, MOE, route)

            group_results = results.rearrange("(g t p) d -> g p t d", t=QT, p=HT)

            def store(k, u):
                act.wait_ge(f_yo, u + 1)
                act.dma_start(group_results[ds(u, 1)].rearrange("a p t d -> p (a t) d"), sY[:, k]) \
                    .then_inc(s_stored[k], 16)

            def parts(n):
                for k in range(RING):
                    u = RING * n + k
                    act.wait_ge(f_tp, u + 1)
                    after(act, f_y, u - RING + 1)
                    act.activation(sXH[:, k].rearrange("p t n -> p (t n)"), bank(k), ACT.Copy).then_inc(f_xh, 1)
                    act.wait_ge(f_r1, u + 1)
                    act.activation(sXM[:, k].rearrange("p t n -> p (t n)"), sR[:, k, :], ACT.Copy).then_inc(f_xm, 1)
                    if k >= 3:
                        store(k - 3, u - 3)
                    elif type(n) is not int or n > 0:
                        store(k + 1, u - 3)

            over_rounds(act, parts)
            for k in range(1, RING):
                store(k, RING * (ROUNDS - 1) + k)

        @block.tensor
        def _(pe):
            def product(dst, lhs, rhs, first=True, last=True):
                return pe.matmul(dst, lhs, rhs, start=first, stop=last)

            def xt_turn(phase, b, to=0):
                n = phase * B + b
                pe.wait_ge(s_xn, n + 1)
                pe.wait_ge(s_xt, n)
                for c in range(C):
                    for j in range(J):
                        at = c * S + j * P
                        if phase == FFN:
                            last = pe.transpose(pXT[:, 0:D].bitcast(BF)[:, at:at + P],
                                                cXB[:, j, c * P:(c + 1) * P], identb[:, :])
                        else:
                            last = pe.transpose(PS[:, to, at:at + P], XN[:, j, c * P:(c + 1) * P], ident[:, :])
                last.then_inc(s_xtp, 1)

            pe.wait_ge(s_c, mark["fly"])
            product(PS[0:NS, 1, 0:D], fly[:, LV % 2, :], wbrT[:, :])
            product(PS[0:NS, 2, 0:D], wcrT[:, :], wcm[:, :]).then_inc(s_pp, 1)
            pe.wait_ge(s_c, mark["folds"])
            for c in range(C):
                last = product(PS[:, 3 + c, 0:D], b_fold[:, c * P:(c + 1) * P], c_fold[:, :])
            last.then_inc(s_pp, 1)
            xt_turn(MIX, 0)
            pe.wait_ge(s_c, mark["mix"])

            def mixer(b, nxt):
                pe.wait_ge(s_xt, b + 1)
                pe.wait_ge(s_x, b)
                for j in range(J):
                    for c in range(C):
                        last = product(PS[:, 1, j * D:(j + 1) * D], XT[:, c, j * P:(j + 1) * P], mix[:, c, :],
                                       c == 0, c == C - 1)
                last.then_inc(a_mm, 1)
                xt_turn(*nxt)

            over_batches(pe, MIX, mixer)

            pe.wait_ge(s_c, mark["wsum"])
            product(PS[:, 7, 0:3], ones[:, :], wsum[:, :]).then_inc(s_ps, 1)

            def cross_scores(b):
                pe.wait_ge(s_xt, CROSS * B + b + 1)
                pe.wait_ge(b_c, b)
                for j in range(J):
                    for c in range(C):
                        last = product(PS[:, 1, j * T:(j + 1) * T], XT[:, c, j * P:(j + 1) * P],
                                       ctxT[:, c, ds(b, 1), :].rearrange("p a t -> p (a t)"), c == 0, c == C - 1)
                last.then_inc(b_s, 1)

            def cross(b, nxt):
                xt_turn(*nxt)
                if nxt[0] == CROSS:
                    cross_scores(nxt[1])
                held(pe, b_p, b + 1)
                for j in range(J):
                    last = pe.transpose(PS[0:T, 2, j * P:(j + 1) * P], bP[:, j, :], ident[:, :])
                last.then_inc(b_t, 1)
                pe.wait_ge(b_tc, b + 1)
                pe.wait_ge(s_x, CROSS * B + b)
                for j in range(J):
                    last = product(PS[:, 3, j * D:(j + 1) * D], bPT[0:T, j * P:(j + 1) * P],
                                   ctxN[:, ds(b, 1), :].rearrange("p a d -> p (a d)"))
                last.then_inc(b_o2, 1)

            pe.wait_ge(s_x, CROSS * B)
            cross_scores(0)
            over_batches(pe, CROSS, cross)

            def project(m, at, half):
                for c in range(C):
                    product(PS[:, at, half * S:(half + 1) * S], w_in[:, c, m * P:(m + 1) * P], XT[:, c, :],
                            c == 0, c == C - 1)

            def project_first(b):
                pe.wait_ge(s_xt, SELF * B + b + 1)
                after(pe, d_mx, 8 * b)
                project(0, 4, 0)
                project(1, 4, 1)
                project(3, 7, 0)

            def project_rest(b):
                project(2, 5, 0)
                for j in range(J):
                    for c in range(C):
                        last = product(PS[:, 6, j * D:(j + 1) * D], XT[:, c, j * P:(j + 1) * P],
                                       w_in[:, c, 2 * D:3 * D], c == 0, c == C - 1)
                last.then_inc(d_pq, 1)

            def gate(b, j):
                u = J * b + j
                pe.wait_ge(s_xt, FFN * B + b + 1)
                pe.wait_ge(c_gs, u)
                for n in range(2):
                    for c in range(C):
                        last = product(PS[:, 1 + n, :], cXT[:, c, j * P:(j + 1) * P],
                                       gateT[:, c, 512 * n:512 * n + 512], c == 0, c == C - 1)
                last.then_inc(c_g, 1)

            def value(b, j):
                u = J * b + j
                pe.wait_ge(c_vs, u)
                for n in range(2):
                    for c in range(C):
                        last = product(PS[:, 3 + n, :], cXT[:, c, j * P:(j + 1) * P],
                                       valT[:, c, 512 * n:512 * n + 512], c == 0, c == C - 1)
                last.then_inc(c_v, 1)

            def turn(b, j):
                u = J * b + j
                pe.wait_ge(c_ht, u)
                pe.wait_ge(c_hq, u + 1)
                for m in range(HC):
                    last = pe.transpose(bank(5).bitcast(BF)[:, m * P:(m + 1) * P], cHQ[:, m * P:(m + 1) * P], identb[:, :])
                last.then_inc(c_t, 1)

            def down(b, j):
                u = J * b + j
                pe.wait_ge(c_y, u)
                pe.wait_ge(c_ht, u + 1)
                for m in range(HC):
                    last = product(PS[:, 6, 0:D], cHT[:, m, :], outT[:, m, :], m == 0, m == HC - 1)
                last.then_inc(c_o, 1)

            def ffn(b, nxt):
                behind = type(b) is not int or b > 0
                if behind:
                    turn(b - 1, 1)
                gate(b, 1)
                if behind:
                    down(b - 1, 1)
                value(b, 1)
                xt_turn(*nxt)
                turn(b, 0)
                if nxt[0] == FFN:
                    gate(nxt[1], 0)
                down(b, 0)
                if nxt[0] == FFN:
                    value(nxt[1], 0)

            pe.wait_ge(s_tern, 3 * B)
            pe.wait_ge(s_x, FFN * B)
            gate(0, 0)
            value(0, 0)
            over_batches(pe, FFN, ffn)
            pe.wait_ge(s_l3, 16 * 7)
            pe.wait_ge(c_vs, J * B)
            project_first(0)
            turn(B - 1, 1)
            down(B - 1, 1)

            def self_turn(b):
                pe.wait_ge(d_pt, 8 * b + 8)
                pe.wait_ge(d_o, b + 1)
                for c in range(C):
                    for j in range(J):
                        last = pe.transpose(PS[:, 1, c * S + j * P:c * S + (j + 1) * P], dO[:, j, c * P:(c + 1) * P],
                                            ident[:, :])
                last.then_inc(d_ot, 1)

            def self_finish(b):
                pe.wait_ge(d_oc, b + 1)
                for j in range(J):
                    for c in range(C):
                        last = product(PS[:, 2, j * D:(j + 1) * D], dOT[:, c, j * P:(j + 1) * P], w_out[:, c, :],
                                       c == 0, c == C - 1)
                last.then_inc(d_y, 1)

            def raw_keys(b, seg, at=1):
                n = T if seg == 1 else P
                pe.wait_ge(s_xt, HYBRID * B + b + 1)
                pe.wait_ge(e_ct, b + 1)
                pe.wait_ge(e_kr, 3 * b + seg)
                for c in range(C):
                    last = product(PS[0:n, at, :], eCT[:, c, :] if seg == 1 else
                                   XT[:, c, (seg // 2) * P:(seg // 2 + 1) * P],
                                   (wkc if seg == 1 else wk)[:, c, :], c == 0, c == C - 1)
                last.then_inc(e_k, 1)

            def self_attention(b, nxt):
                def scores(i):
                    j, u = i // 4, 8 * b + i
                    n = (j + 1) * P
                    if i == 0:
                        pe.wait_ge(d_q, b + 1)
                        pe.wait_ge(d_k1, b + 1)
                    if i == 1:
                        pe.wait_ge(d_vv, b + 1)
                        pe.wait_ge(d_k2, b + 1)
                    if i >= 2:
                        pe.wait_ge(d_mx, u - 1)
                    for hh in range(4):
                        h = 4 * (i % 4) + hh
                        last = product(PS[:, 4 + 2 * (i % 2) + hh // 2, (hh % 2) * S:(hh % 2) * S + n],
                                       dQ[:, h // 8, j * P:(j + 1) * P], dK[:, h, 0:n])
                    last.then_inc(d_s, 1)

                def turn(i):
                    j, u = i // 4, 8 * b + i
                    pe.wait_ge(d_e, u + 1)
                    pe.wait_ge(d_pt, u)
                    if i == 0:
                        pe.wait_ge(d_yb, b)
                    for hh in range(4):
                        for k in range(j + 1):
                            at = (hh * (j + 1) + k) * P
                            last = pe.transpose(bank(1, 2)[:, at:at + P], dP[:, i % 2, hh, k * P:(k + 1) * P], ident[:, :])
                    last.then_inc(d_t, 1)

                def outputs(i):
                    j, u = i // 4, 8 * b + i
                    pe.wait_ge(d_pt, u + 1)
                    if i == 0:
                        pe.wait_ge(d_o, b)
                    for hh in range(4):
                        h = 4 * (i % 4) + hh
                        for k in range(j + 1):
                            last = product(PS[:, 3, j * D + h * DH:j * D + (h + 1) * DH],
                                           dPT[:, i % 2, hh * (j + 1) + k, :], dV[:, k, h * DH:(h + 1) * DH],
                                           k == 0, k == j)
                    last.then_inc(d_pv, 1)

                scores(0)
                if type(b) is not int or b > 0:
                    self_turn(b - 1)
                scores(1)
                if type(b) is not int or b > 0:
                    self_finish(b - 1)
                for i in range(8):
                    if i + 2 < 8:
                        scores(i + 2)
                    if i == 6 and nxt[0] == SELF:
                        project_first(nxt[1])
                        project_rest(nxt[1])
                    turn(i)
                    if i == 7 and nxt[0] == HYBRID:
                        pe.wait_ge(s_c, mark["tables"])
                        pe.wait_ge(d_mx, 8 * b + 8)
                        for seg in range(3):
                            raw_keys(0, seg, 4 + seg)
                    if i >= 1:
                        outputs(i - 1)
                    if i == 4:
                        xt_turn(*nxt)
                outputs(7)

            pe.wait_ge(s_x, SELF * B)
            project_rest(0)
            over_batches(pe, SELF, self_attention)
            self_turn(B - 1)
            self_finish(B - 1)


            def hybrid_finish(b, j):
                if j == 0:
                    pe.wait_ge(e_oc, 8 * b + 8)
                for h in range(XH):
                    last = product(PS[:, 0, j * D:(j + 1) * D], eOT[:, h, j * P:(j + 1) * P], wo[:, h, :],
                                   h == 0, h == XH - 1)
                last.then_inc(e_y, 1)

            def copied(b, i):
                return 12 * b + i + max(0, i - XG)

            def hybrid(b, nxt):
                def raw_query(i):
                    j, g, u = i // XG, i % XG, 8 * b + i
                    pe.wait_ge(e_qr, u)
                    for c in range(C):
                        last = product(PS[:, 1, :], XT[:, c, j * P:(j + 1) * P], wq[:, c, 512 * g:512 * g + 512],
                                       c == 0, c == C - 1)
                    last.then_inc(e_q, 1)

                def query(i):
                    u = 8 * b + i
                    pe.wait_ge(e_qf, u + 1)
                    pe.wait_ge(e_qc, u)
                    for hh in range(GH):
                        last = pe.transpose(PS[:, 2, hh * P:(hh + 1) * P], eQA[:, hh * XD:(hh + 1) * XD], ident[:, :])
                    last.then_inc(e_qt, 1)

                def scores(i, heads):
                    j, g, u = i // XG, i % XG, 8 * b + i
                    n = KEYS if j else P + T
                    pe.wait_ge(e_qc, u + 1)
                    for hh in heads:
                        if GH * i + hh >= 2:
                            pe.wait_ge(e_mx, GH * u + hh - 1)
                        product(PS[:, 3 + hh % 2, 0:n], eQT[:, hh * P:(hh + 1) * P], eKT[:, g, 0:n]).then_inc(e_s, 1)

                def turn(i):
                    j, u = i // XG, 8 * b + i
                    pe.wait_ge(e_p, u + 1)
                    pe.wait_ge(e_pta, u)
                    pe.wait_ge(e_ptd, copied(b, i))
                    for hh in range(GH):
                        for k, (at, n) in enumerate(((0, P), (P, T), (P + T, P))[0:2 + j]):
                            last = pe.transpose(PS[0:n, 5 + k, hh * P:(hh + 1) * P], eP[:, i % 2, hh, at:at + n], ident[:, :])
                    last.then_inc(e_t, 1)

                def outputs(i):
                    j, g, u = i // XG, i % XG, 8 * b + i
                    pe.wait_ge(e_pta, u + 1)
                    pe.wait_ge(e_oc, u)
                    if i == 0:
                        pe.wait_ge(s_x, HYBRID * B + b)
                    for k, n in enumerate((P, T, P)[0:2 + j]):
                        if k:
                            pe.wait_ge(e_ptd, copied(b, i) + k)
                        last = product(PS[:, 0, :], eV[0:n, k, g * XD:(g + 1) * XD], ePT[0:n, k, :], k == 0, k == 1 + j)
                    last.then_inc(e_pv, 1)

                pe.wait_ge(e_kr, 3 * b + 3)
                raw_query(0)
                pe.wait_ge(e_pta, 8 * b)
                pe.wait_ge(e_ptd, copied(b, 0))
                for seg in range(3):
                    n = T if seg == 1 else P
                    for c in range(C):
                        last = product(PS[0:n, 5 + seg, :], eCT[:, c, :] if seg == 1 else
                                       XT[:, c, (seg // 2) * P:(seg // 2 + 1) * P],
                                       (wvc if seg == 1 else wv)[:, c, :], c == 0, c == C - 1)
                    last.then_inc(e_v, 1)
                former = type(b) is not int or b > 0
                if former:
                    hybrid_finish(b - 1, 0)
                for seg in range(3):
                    n = T if seg == 1 else P
                    if seg == 1:
                        held(pe, e_ka, 3 * b + 2)
                    else:
                        pe.wait_ge(e_kf, 2 * b + 1 + seg // 2)
                    for g in range(XG):
                        last = pe.transpose(PS[:, 2 + seg, g * n:(g + 1) * n],
                                            eKF[0:n, seg, g * XD:(g + 1) * XD], ident[0:n, 0:n])
                    last.then_inc(e_kt, 1)
                pe.wait_ge(e_kc, 3 * b + 3)
                query(0)
                raw_query(1)
                if former:
                    hybrid_finish(b - 1, 1)
                scores(0, (0, 1))
                raw_query(2)
                scores(0, (2, 3))
                for i in range(8):
                    if i + 1 < 8:
                        query(i + 1)
                    if i == 0:
                        pe.wait_ge(e_vr, 3 * b + 3)
                    if i >= 1:
                        outputs(i - 1)
                    if i + 1 < 8:
                        scores(i + 1, (0, 1))
                    if i + 3 < 8:
                        raw_query(i + 3)
                    if i == 5:
                        pe.wait_ge(e_qr, 8 * b + 8)
                        xt_turn(*nxt, 1)
                    if nxt[0] == HYBRID and i >= 6:
                        raw_keys(nxt[1], i - 6)
                    if i + 1 < 8:
                        scores(i + 1, (2, 3))
                    turn(i)
                if nxt[0] == HYBRID:
                    raw_keys(nxt[1], 2)
                outputs(7)

            pe.wait_ge(s_x, HYBRID * B)
            over_batches(pe, HYBRID, hybrid)
            for j in range(J):
                hybrid_finish(B - 1, j)

            def route(b, nxt):
                pe.wait_ge(s_xt, MOE * B + b + 1)
                pe.wait_ge(f_lg, b)
                for j in range(J):
                    for c in range(C):
                        last = product(PS[:, 7, j * NE:(j + 1) * NE], XT[:, c, j * P:(j + 1) * P], rwT[:, c, :],
                                       c == 0, c == C - 1)
                last.then_inc(f_l, 1)
                if nxt[0] == MOE:
                    xt_turn(*nxt)

            over_batches(pe, MOE, route)
            pe.wait_ge(s_c, mark["routing"])
            pe.wait_ge(f_oh, B)
            for i in range(TOK):
                last = product(PS[0:NE, 2, 0:1], fOH[:, i, :], onesb[:, 0:1], i == 0, i == TOK - 1)
            last.then_inc(f_count, 1)
            product(PS[:, 1, :], before, fOH.rearrange("p i e -> p (i e)"), True, False)
            for i in range(TOK - 1):
                last = product(PS[:, 1, (i + 1) * NE:].rearrange("p (i e) -> p i e", e=NE), onesb,
                               bc(fOH[:, i:i + 1, :], [P, TOK - 1 - i, NE]), False, i == TOK - 2)
            last.then_inc(f_rank, 1)
            pe.wait_ge(s_c, mark["tiles"])
            product(PS[:, 3, 0:NE], tilesB[0:NE, :], lower[0:NE, :])
            product(PS[0:NE, 4, 0:1], upto[0:NE, :], f_tiles).then_inc(f_base, 1)
            pe.wait_ge(s_c, mark["past"])
            product(PS[:, 5, 0:TILES], ones[0:NE, :], past[0:NE, :]).then_inc(f_tex, 1)
            pe.wait_ge(s_c, mark["experts"])

            registers = [pe.alloc_register(f"expert{t}") for t in range(QT)]

            def apply(k, u):
                pe.load(registers, f_exu[0:1, ds(QT * u, QT)])
                expert = [bass.RuntimeValue.of_register_unchecked(r, min_val=0, max_val=NE - 1) for r in registers]
                after(pe, f_yo, u - 1)
                held(pe, f_xl, u + 1)
                for t in range(QT):
                    for m, part in enumerate((sXH, sXM, sXL)):
                        for c in range(C):
                            last = product(PS[0:HT, 4 + 2 * (k % 2) + t // 2, t % 2 * D:(t % 2 + 1) * D],
                                           part[:, k, t // 2, c * P + t % 2 * HT:c * P + t % 2 * HT + HT],
                                           EW[:, ds(expert[t], 1), c * D:(c + 1) * D].rearrange("p a d -> p (a d)"),
                                           m == 0 and c == 0, m == 2 and c == C - 1)
                last.then_inc(f_y, 1)

            def experts(n):
                for k in range(RING):
                    u = RING * n + k
                    pe.wait_ge(s_rows[k], 16 * n + 16)
                    after(pe, f_xl, u - RING + 1)
                    for t in range(2):
                        for c in range(C):
                            last = pe.transpose(PS[:, k, (t * C + c) * P:(t * C + c + 1) * P],
                                                sIN[:, k, t, c * P:(c + 1) * P], ident[:, :])
                    last.then_inc(f_tp, 1)
                    if k >= 2:
                        apply(k - 2, u - 2)
                    elif type(n) is not int or n > 0:
                        apply(k + 2, u - 2)

            over_rounds(pe, experts)
            for k in range(2, RING):
                apply(k, RING * (ROUNDS - 1) + k)


def kernel(**inputs):
    import concourse.bacc as bacc
    from concourse.bass_utils import run_bass_kernel_spmd

    f = {k: np.asarray(v) for k, v in inputs.items()}
    row = lambda a: np.ascontiguousarray(a.reshape(-1))
    swap = lambda a: np.concatenate([a[XD // 2:], a[:XD // 2]])
    w_in = f["L1_attn_W_in"]
    pos = np.arange(S, dtype=np.float32)
    inv = (1.0 / 10000.0 ** (np.arange(0, XD, 2, dtype=np.float32) / np.float32(XD))).astype(np.float32)
    ang = np.outer(pos, inv).astype(np.float32)
    cos, sin = np.cos(ang), np.sin(ang)
    tri = np.where(np.arange(S)[None, :] > np.arange(S)[:, None], NEG, 0.0).astype(np.float32)
    kmask = np.concatenate([tri[:, :P], np.zeros((S, T), np.float32), tri[:, P:]], axis=1)
    tiled = lambda a: np.ascontiguousarray(a.reshape(J, P, -1).transpose(1, 0, 2))
    masksT = f["L1_ffn_expert_masks"].transpose(0, 2, 1).reshape(NE, C, P, D).transpose(0, 2, 1, 3)
    arrays = {
        "x": f["x"],
        "ctx": f["ctx_2048"],
        "ctxT": f["ctx_2048"].transpose(2, 0, 1),
        "mask": f["mask_BxS2_bk0"],
        "wbrT": f["L0_attn_W_b_rank"].T, "wbs": f["L0_attn_W_b_state"],
        "wcrT": f["L0_attn_W_c_rank"].T, "wcm": f["L0_attn_W_c_model"],
        "factors": row(f["L0_attn_A_factors"]), "dvec": f["L0_attn_D_vec"].reshape(C, P).T,
        "gateT": f["L0_ffn_gate_w"].T, "valT": f["L0_ffn_val_w"].T, "outT": f["L0_ffn_out_w"].T,
        "gate_b": f["L0_ffn_gate_b"], "val_b": f["L0_ffn_val_b"], "ffo_b": f["L0_ffn_out_b"],
        "w_in": w_in, "w_out": f["L1_attn_W_out"],
        "bqk": f["L1_attn_b_in"][:2 * D].reshape(4, P).T, "b_v": f["L1_attn_b_in"][2 * D:], "b_o": f["L1_attn_b_out"],
        "wq": f["L1_xattn_wq"], "wk": f["L1_xattn_wk"], "wv": f["L1_xattn_wv"],
        "wkc": f["L1_xattn_wk_ctx"], "wvc": f["L1_xattn_wv_ctx"], "wo": f["L1_xattn_wo"],
        "qw": f["L1_xattn_q_norm_w"], "qws": swap(f["L1_xattn_q_norm_w"]),
        "kw": f["L1_xattn_k_norm_w"], "kws": swap(f["L1_xattn_k_norm_w"]),
        "ewT": f["L1_ffn_weight"].T, "rwT": f["L1_ffn_router_w"].T, "esc": f["L1_ffn_scale"],
        "masksT": masksT.reshape(NE, P, C * D),
        "ident": np.eye(P, dtype=np.float32),
        "hmask": np.repeat(np.eye(P // DH, dtype=np.float32), DH, axis=0),
        "causal": tiled(tri), "kmask": tiled(kmask),
        "cos": np.concatenate([cos, cos], 1), "sin": np.concatenate([-sin, sin], 1),
        "iota": np.arange(TILES, dtype=np.float32),
    }
    arrays = {f"in_{k}_dram": np.ascontiguousarray(v) for k, v in arrays.items()}
    nc = bacc.Bacc("TRN2", target_bir_lowering=False, num_devices=1)
    aps = {k[3:-5]: nc.dram_tensor(k, a.shape, mybir.dt.from_np(a.dtype), kind="ExternalInput").ap()
           for k, a in arrays.items()}
    out = nc.dram_tensor("out_dram", (B, S, D), mybir.dt.float32, kind="ExternalOutput").ap()
    rows = nc.dram_tensor("rows_dram", (TILES * HT, D), mybir.dt.float32, kind="Internal").ap()
    results = nc.dram_tensor("results_dram", (TILES * HT, D), mybir.dt.float32, kind="Internal").ap()
    decoder_kernel(nc, aps, out, rows, results)
    return run_bass_kernel_spmd(nc, [arrays], core_ids=[0]).results[0]["out_dram"]
```
